# Optimizing a Trainium2 kernel written in Bass

```python
import numpy as np
import jax
import jax.numpy as jnp

def _softmax(x, axis=-1):
    return jax.nn.softmax(x, axis=axis)

def _gelu(x):
    return jax.nn.gelu(x, approximate=True)

def _silu(x):
    return jax.nn.silu(x)

def _sigmoid(x):
    return jax.nn.sigmoid(x)

def _layernorm(x, axis=-1, eps=1e-05):
    m = jnp.mean(x, axis=axis, keepdims=True)
    v = jnp.var(x, axis=axis, keepdims=True)
    return (x - m) / jnp.sqrt(v + eps)

def _scatter_add(tgt, idx, src, axis=0):
    return tgt.at[idx].add(src)

def _segment_sum(src, seg, n):
    return jax.ops.segment_sum(src, seg, n)
kernel_name = 'mk_decoder_postln_d4_seqx_r8_060aa7'

def setup_inputs(seed: int=0):
    np.random.seed(seed)
    _w = jnp.asarray

    def _rec_inputs():
        import jax
        import jax.numpy as jnp
        _rk = jax.random.key(seed)
        x = 2.818e-05 + 1 * jax.random.normal(jax.random.fold_in(_rk, 1), (32, 128, 128), jnp.float32)
        _lenS = 128 - jax.random.randint(jax.random.fold_in(_rk, 7), (32,), 0, max(1, 128 // 4) + 1, jnp.int32)
        _lenS2 = 77 - jax.random.randint(jax.random.fold_in(_rk, 8), (32,), 0, max(1, 77 // 4) + 1, jnp.int32)
        _ctx_1024P = jax.random.normal(jax.random.fold_in(_rk, 11), (32, 16, 128), jnp.float32)
        _ctx_1024c = jax.random.dirichlet(jax.random.fold_in(_rk, 511), 0.3 * jnp.ones((16,), jnp.float32), (32, 77))
        _ctx_1024t = jnp.einsum('bsk,bkd->bsd', _ctx_1024c, _ctx_1024P)
        _ctx_1024t = _ctx_1024t * jax.lax.rsqrt(jnp.mean(jnp.square(_ctx_1024t)) + 1e-12) * 0.953939
        ctx_1024 = -0.000125008 + 0.999885 * (_ctx_1024t + 0.3 * jax.random.normal(jax.random.fold_in(_rk, 611), (32, 77, 128), jnp.float32))
        _validS = jnp.arange(128)[None, :] < _lenS[:, None]
        _validS2 = jnp.arange(77)[None, :] < _lenS2[:, None]
        _causal = jnp.tril(jnp.ones((128, 128), dtype=bool))
        mask_SxS2_fk1 = jnp.where(jnp.broadcast_to(_validS2[0:1, :], (128, 77)), 1.0, 0.0).astype(jnp.float32)
        mask_BxSxS2_ik0 = jnp.where(jnp.broadcast_to(_validS2[:, None, :], (32, 128, 77)), 0, 1).astype(jnp.int32)
        return (x, ctx_1024, mask_SxS2_fk1, mask_BxSxS2_ik0)
    x, ctx_1024, mask_SxS2_fk1, mask_BxSxS2_ik0 = _rec_inputs()

    def _L0_attn_setup():
        import jax, jax.numpy as jnp
        import numpy as np
        EPS = 1e-08

        def elu_feature_map(x):
            return jax.nn.elu(x) + 1.0
        key = jax.random.key(seed)
        ks = jax.random.split(key, 5)
        B, S, D = (2, 512, 128)
        scale = 1.0 / np.sqrt(D).astype(np.float32)
        x = jax.random.normal(ks[0], (B, S, D), dtype=jnp.float32)
        Wq = jax.random.normal(ks[1], (D, D), dtype=jnp.float32) * scale
        Wk = jax.random.normal(ks[2], (D, D), dtype=jnp.float32) * scale
        Wv = jax.random.normal(ks[3], (D, D), dtype=jnp.float32) * scale
        Wo = jax.random.normal(ks[4], (D, D), dtype=jnp.float32) * scale
        return {'x': x, 'Wq': Wq, 'Wk': Wk, 'Wv': Wv, 'Wo': Wo}
    _L0_attn_all = _L0_attn_setup()
    _L0_attn_in = {k: v for k, v in _L0_attn_all.items() if k in ('Wq', 'Wk', 'Wv', 'Wo')}
    del _L0_attn_all

    def _L0_xattn_setup():
        import jax, jax.numpy as jnp
        import numpy as np
        H = 8
        D = 128
        DQ = D // H
        BN = 64
        HID = 128
        B = 16
        S_T = 128
        S_M = 256
        SCALE = DQ ** 0.25
        EPS = 1e-05

        def _ln(x, g, b):
            m = jnp.mean(x, axis=-1, keepdims=True)
            v = jnp.mean(jnp.square(x - m), axis=-1, keepdims=True)
            return (x - m) * jax.lax.rsqrt(v + EPS) * g + b

        def _mhla(xq, xk, xv, Wq, Wk, Wv, Wo, masked):
            Q = jnp.einsum('bsq,hqd->bhsd', xq, Wq)
            K = jnp.einsum('bsq,hqd->bhsd', xk, Wk)
            V = jnp.einsum('bsq,hqd->bhsd', xv, Wv)
            if masked:
                s, d = (Q.shape[-2], Q.shape[-1])
                m = jnp.where(jnp.arange(d)[None, :] <= jnp.arange(s)[:, None], 0.0, -jnp.inf)
                Q = Q + m.astype(Q.dtype)
            A = jnp.einsum('bhsd,bhse->bhde', jax.nn.softmax(K / SCALE, axis=-1), V)
            Bm = jnp.einsum('bhsd,bhde->bhse', jax.nn.softmax(Q / SCALE, axis=-1), A)
            b, h, w, dd = Bm.shape
            Bm = Bm.reshape(b, w, h * dd)
            return Bm @ Wo.T
        key = jax.random.key(seed)
        ks = jax.random.split(key, 24)
        r = lambda k, sh, s=0.02: jax.random.normal(k, sh, jnp.float32) * s
        return {'mem': jax.random.normal(ks[0], (B, S_M, D), jnp.float32), 'y': jax.random.normal(ks[1], (B, S_T, D), jnp.float32), 'Wq1': r(ks[2], (H, D, DQ)), 'Wk1': r(ks[3], (H, D, DQ)), 'Wv1': r(ks[4], (H, D, DQ)), 'Wo1': r(ks[5], (D, D)), 'Wq2': r(ks[6], (H, D, DQ)), 'Wk2': r(ks[7], (H, D, DQ)), 'Wv2': r(ks[8], (H, D, DQ)), 'Wo2': r(ks[9], (D, D)), 'E1': r(ks[10], (BN, D)), 'D1': r(ks[11], (HID, BN)), 'E2': r(ks[12], (BN, HID)), 'D2': r(ks[13], (D, BN)), 'g1': jnp.ones((D,), jnp.float32), 'b1': jnp.zeros((D,), jnp.float32), 'g2': jnp.ones((D,), jnp.float32), 'b2': jnp.zeros((D,), jnp.float32), 'g3': jnp.ones((D,), jnp.float32), 'b3': jnp.zeros((D,), jnp.float32)}
    _L0_xattn_all = _L0_xattn_setup()
    _L0_xattn_in = {k: v for k, v in _L0_xattn_all.items() if k in ('Wq1', 'Wk1', 'Wv1', 'Wo1', 'Wq2', 'Wk2', 'Wv2', 'Wo2', 'E1', 'D1', 'E2', 'D2', 'g1', 'b1', 'g2', 'b2', 'g3', 'b3')}
    del _L0_xattn_all

    def _L0_ffn_setup():
        import jax, jax.numpy as jnp
        import numpy as np
        H, I, E, K = (128, 64, 32, 8)
        B, S = (4, 128)

        def silu(x):
            return x * jax.nn.sigmoid(x)
        key = jax.random.key(seed)
        ks = jax.random.split(key, 14)

        def w(k, shape, fan_in):
            return jax.random.normal(k, shape, jnp.float32) / np.float32(np.sqrt(fan_in))
        return {'hidden_states': jax.random.normal(ks[0], (B, S, H), jnp.float32), 'Wr': w(ks[1], (H, E), H), 'br': jnp.zeros((E,), jnp.float32), 'Wg_s': w(ks[2], (H, I), H), 'bg_s': jnp.zeros((I,), jnp.float32), 'Wu_s': w(ks[3], (H, I), H), 'bu_s': jnp.zeros((I,), jnp.float32), 'Wd_s': w(ks[4], (I, H), I), 'bd_s': jnp.zeros((H,), jnp.float32), 'Wg': w(ks[5], (E, H, I), H), 'bg': jnp.zeros((E, I), jnp.float32), 'Wu': w(ks[6], (E, H, I), H), 'bu': jnp.zeros((E, I), jnp.float32), 'Wd': w(ks[7], (E, I, H), I), 'bd': jnp.zeros((E, H), jnp.float32)}
    _L0_ffn_all = _L0_ffn_setup()
    _L0_ffn_in = {k: v for k, v in _L0_ffn_all.items() if k in ('Wr', 'br', 'Wg_s', 'bg_s', 'Wu_s', 'bu_s', 'Wd_s', 'bd_s', 'Wg', 'bg', 'Wu', 'bu', 'Wd', 'bd')}
    del _L0_ffn_all

    def _L1_attn_setup():
        import jax, jax.numpy as jnp
        import numpy as np
        D_K, D_MODEL, NUM_HEADS = (64, 128, 16)

        def _xavier(key, shape):
            fan_in, fan_out = (shape[-2], shape[-1])
            limit = float(np.sqrt(6.0 / (fan_in + fan_out)))
            return jax.random.uniform(key, shape, jnp.float32, -limit, limit)
        key = jax.random.key(seed)
        kx, kq, kk, kv, ko = jax.random.split(key, 5)
        x = jax.random.normal(kx, (2, 256, D_MODEL), dtype=jnp.float32)
        w_q = _xavier(kq, (NUM_HEADS, D_MODEL, D_K))
        w_k = _xavier(kk, (NUM_HEADS, D_MODEL, D_K))
        w_v = _xavier(kv, (NUM_HEADS, D_MODEL, D_K))
        w_o = _xavier(ko, (NUM_HEADS * D_K, D_MODEL))
        return {'x': x, 'w_q': w_q, 'w_k': w_k, 'w_v': w_v, 'w_o': w_o}
    _L1_attn_all = _L1_attn_setup()
    _L1_attn_in = {k: v for k, v in _L1_attn_all.items() if k in ('w_q', 'w_k', 'w_v', 'w_o')}
    del _L1_attn_all

    def _L1_xattn_setup():
        import jax, jax.numpy as jnp
        import numpy as np
        D_MODEL = 128
        N_HEADS = 16
        HEAD_DIM = D_MODEL // N_HEADS
        key = jax.random.key(seed)
        ks = jax.random.split(key, 10)
        B, Lq, Lkv = (4, 64, 256)
        s = 1.0 / np.sqrt(D_MODEL)
        return {'q': jax.random.normal(ks[0], (B, Lq, D_MODEL), jnp.float32), 'kv': jax.random.normal(ks[1], (B, Lkv, D_MODEL), jnp.float32), 'Wq': jax.random.normal(ks[2], (D_MODEL, D_MODEL), jnp.float32) * s, 'bq': jnp.zeros((D_MODEL,), jnp.float32), 'Wk': jax.random.normal(ks[3], (D_MODEL, D_MODEL), jnp.float32) * s, 'bk': jnp.zeros((D_MODEL,), jnp.float32), 'Wv': jax.random.normal(ks[4], (D_MODEL, D_MODEL), jnp.float32) * s, 'bv': jnp.zeros((D_MODEL,), jnp.float32), 'Wo': jax.random.normal(ks[5], (D_MODEL, D_MODEL), jnp.float32) * s, 'bo': jnp.zeros((D_MODEL,), jnp.float32)}
    _L1_xattn_all = _L1_xattn_setup()
    _L1_xattn_in = {k: v for k, v in _L1_xattn_all.items() if k in ('Wq', 'bq', 'Wk', 'bk', 'Wv', 'bv', 'Wo', 'bo')}
    del _L1_xattn_all

    def _L1_ffn_setup():
        import jax, jax.numpy as jnp
        import numpy as np
        D_IN, D_HID = (128, 512)

        def _ternary(key, shape):
            return jax.random.randint(key, shape, -1, 2).astype(jnp.float32)

        def _tlin(x, w, s):
            return jnp.einsum('bsi,oi->bso', x, w) * s
        key = jax.random.key(seed)
        ks = jax.random.split(key, 12)
        inv = lambda fan: 1.0 / np.sqrt(fan).astype(np.float32)
        return {'x': jax.random.normal(ks[0], (4, 256, D_IN), dtype=jnp.float32), 'w1_w': _ternary(ks[1], (D_HID, D_IN)), 'w1_s': jax.random.uniform(ks[2], (D_HID,), dtype=jnp.float32) * inv(D_IN), 'w2_w': _ternary(ks[3], (D_HID, D_IN)), 'w2_s': jax.random.uniform(ks[4], (D_HID,), dtype=jnp.float32) * inv(D_IN), 'h1_w': _ternary(ks[5], (D_HID, D_HID)), 'h1_s': jax.random.uniform(ks[6], (D_HID,), dtype=jnp.float32) * inv(D_HID), 'h2_w': _ternary(ks[7], (D_HID, D_HID)), 'h2_s': jax.random.uniform(ks[8], (D_HID,), dtype=jnp.float32) * inv(D_HID), 'w3_w': _ternary(ks[9], (D_IN, D_HID)), 'w3_s': jax.random.uniform(ks[10], (D_IN,), dtype=jnp.float32) * inv(D_HID)}
    _L1_ffn_all = _L1_ffn_setup()
    _L1_ffn_in = {k: v for k, v in _L1_ffn_all.items() if k in ('w1_w', 'w1_s', 'w2_w', 'w2_s', 'h1_w', 'h1_s', 'h2_w', 'h2_s', 'w3_w', 'w3_s')}
    del _L1_ffn_all

    def _L2_attn_setup():
        import jax, jax.numpy as jnp
        import numpy as np
        DIM = 128
        HEADS = 16
        HEAD_DIM = DIM // HEADS
        B, N = (4, 512)
        key = jax.random.key(seed)
        ks = jax.random.split(key, 9)
        s = 1.0 / np.sqrt(DIM)
        return {'x': jax.random.normal(ks[0], (B, N, DIM), dtype=jnp.float32), 'Wq': jax.random.uniform(ks[1], (DIM, DIM), jnp.float32, -s, s), 'bq': jax.random.uniform(ks[2], (DIM,), jnp.float32, -s, s), 'Wk': jax.random.uniform(ks[3], (DIM, DIM), jnp.float32, -s, s), 'bk': jax.random.uniform(ks[4], (DIM,), jnp.float32, -s, s), 'Wv': jax.random.uniform(ks[5], (DIM, DIM), jnp.float32, -s, s), 'bv': jax.random.uniform(ks[6], (DIM,), jnp.float32, -s, s), 'Wp': jax.random.uniform(ks[7], (DIM, DIM), jnp.float32, -s, s), 'bp': jax.random.uniform(ks[8], (DIM,), jnp.float32, -s, s)}
    _L2_attn_all = _L2_attn_setup()
    _L2_attn_in = {k: v for k, v in _L2_attn_all.items() if k in ('Wq', 'bq', 'Wk', 'bk', 'Wv', 'bv', 'Wp', 'bp')}
    del _L2_attn_all

    def _L2_xattn_setup():
        import jax, jax.numpy as jnp
        import numpy as np
        B, S, D, H = (2, 256, 128, 16)
        DEPTH = D // H

        def _split_heads(x):
            b, s, _ = x.shape
            return x.reshape(b, s, H, DEPTH).transpose(0, 2, 1, 3)
        key = jax.random.key(seed)
        ks = jax.random.split(key, 12)
        inp = {'xq': jax.random.normal(ks[0], (B, S, D), jnp.float32), 'xk': jax.random.normal(ks[1], (B, S, D), jnp.float32), 'xv': jax.random.normal(ks[2], (B, S, D), jnp.float32), 'mask': jnp.triu(jnp.ones((S, S), jnp.float32), k=1)}
        scale = 1.0 / np.sqrt(D)
        inp['Wq'] = jax.random.normal(ks[3], (D, D), jnp.float32) * scale
        inp['bq'] = jnp.zeros((D,), jnp.float32)
        inp['Wk'] = jax.random.normal(ks[4], (D, D), jnp.float32) * scale
        inp['bk'] = jnp.zeros((D,), jnp.float32)
        inp['Wv'] = jax.random.normal(ks[5], (D, D), jnp.float32) * scale
        inp['bv'] = jnp.zeros((D,), jnp.float32)
        inp['Wo'] = jax.random.normal(ks[6], (D, D), jnp.float32) * scale
        inp['bo'] = jnp.zeros((D,), jnp.float32)
        return inp
    _L2_xattn_all = _L2_xattn_setup()
    _L2_xattn_in = {k: v for k, v in _L2_xattn_all.items() if k in ('Wq', 'bq', 'Wk', 'bk', 'Wv', 'bv', 'Wo', 'bo')}
    del _L2_xattn_all

    def _L2_ffn_setup():
        import jax, jax.numpy as jnp
        import numpy as np
        B, S, D, F, E, NS, K = (2, 128, 128, 512, 8, 8, 2)
        FS = F // NS
        key = jax.random.key(seed)
        ks = jax.random.split(key, 8)
        scale = 0.02
        return {'hidden_states': jax.random.normal(ks[0], (B, S, D), jnp.float32), 'gate_W': jax.random.normal(ks[1], (E, D), jnp.float32) * scale, 'w1_e': jax.random.normal(ks[2], (E, D, F), jnp.float32) * scale, 'w3_e': jax.random.normal(ks[3], (E, D, F), jnp.float32) * scale, 'w2_e': jax.random.normal(ks[4], (E, F, D), jnp.float32) * scale, 'w1_s': jax.random.normal(ks[5], (NS, D, FS), jnp.float32) * scale, 'w3_s': jax.random.normal(ks[6], (NS, D, FS), jnp.float32) * scale, 'w2_s': jax.random.normal(ks[7], (NS, FS, D), jnp.float32) * scale}
    _L2_ffn_all = _L2_ffn_setup()
    _L2_ffn_in = {k: v for k, v in _L2_ffn_all.items() if k in ('gate_W', 'w1_e', 'w3_e', 'w2_e', 'w1_s', 'w3_s', 'w2_s')}
    del _L2_ffn_all

    def _L3_attn_setup():
        import jax, jax.numpy as jnp
        import numpy as np
        D_MODEL = 128
        N_HEADS = 16
        HEAD_DIM = D_MODEL // N_HEADS
        MAX_LEN = 256
        BATCH = 2
        SEQ = 256
        key = jax.random.key(seed)
        ks = jax.random.split(key, 10)
        s = 1.0 / np.sqrt(D_MODEL)
        inp = {'x': jax.random.normal(ks[0], (BATCH, SEQ, D_MODEL), dtype=jnp.float32), 'Wq': jax.random.uniform(ks[1], (D_MODEL, D_MODEL), jnp.float32, -s, s), 'bq': jax.random.uniform(ks[2], (D_MODEL,), jnp.float32, -s, s), 'Wk': jax.random.uniform(ks[3], (D_MODEL, D_MODEL), jnp.float32, -s, s), 'bk': jax.random.uniform(ks[4], (D_MODEL,), jnp.float32, -s, s), 'Wv': jax.random.uniform(ks[5], (D_MODEL, D_MODEL), jnp.float32, -s, s), 'bv': jax.random.uniform(ks[6], (D_MODEL,), jnp.float32, -s, s), 'Wo': jax.random.uniform(ks[7], (D_MODEL, D_MODEL), jnp.float32, -s, s), 'bo': jax.random.uniform(ks[8], (D_MODEL,), jnp.float32, -s, s), 'rel_emb': jax.random.normal(ks[9], (MAX_LEN * 2 - 1, HEAD_DIM), dtype=jnp.float32)}
        return inp
    _L3_attn_all = _L3_attn_setup()
    _L3_attn_in = {k: v for k, v in _L3_attn_all.items() if k in ('Wq', 'bq', 'Wk', 'bk', 'Wv', 'bv', 'Wo', 'bo', 'rel_emb')}
    del _L3_attn_all

    def _L3_xattn_setup():
        import jax, jax.numpy as jnp
        import numpy as np
        B, S, D, H = (2, 256, 128, 16)
        DK = D // H

        def _split_heads(x):
            b, s, _ = x.shape
            return x.reshape(b, s, H, DK).transpose(0, 2, 1, 3)
        key = jax.random.key(seed)
        ks = jax.random.split(key, 7)
        causal = jnp.tril(jnp.ones((S, S), dtype=jnp.int32))
        mask = jnp.broadcast_to(causal, (B, S, S))
        return {'query': jax.random.normal(ks[0], (B, S, D), dtype=jnp.float32), 'key': jax.random.normal(ks[1], (B, S, D), dtype=jnp.float32), 'value': jax.random.normal(ks[2], (B, S, D), dtype=jnp.float32), 'mask': mask, 'Wq': jax.random.normal(ks[3], (D, D), dtype=jnp.float32) * D ** (-0.5), 'Wk': jax.random.normal(ks[4], (D, D), dtype=jnp.float32) * D ** (-0.5), 'Wv': jax.random.normal(ks[5], (D, D), dtype=jnp.float32) * D ** (-0.5), 'Wo': jax.random.normal(ks[6], (D, D), dtype=jnp.float32) * D ** (-0.5)}
    _L3_xattn_all = _L3_xattn_setup()
    _L3_xattn_in = {k: v for k, v in _L3_xattn_all.items() if k in ('Wq', 'Wk', 'Wv', 'Wo')}
    del _L3_xattn_all

    def _L3_ffn_setup():
        import jax, jax.numpy as jnp
        import numpy as np
        B, N, D = (4, 512, 128)
        E, K, H, ITERS = (8, 2, 64, 2)
        DT = 0.1
        C = 2 * D

        def _gelu(x):
            return jax.nn.gelu(x, approximate=False)

        def _inl(ctrl, xs, vs, mu):
            a, b, g = jnp.split(ctrl, 3, axis=-1)
            v_next = jax.nn.sigmoid(a) * vs - jax.nn.softplus(b) * (xs - mu)
            x_next = xs + DT * jax.nn.sigmoid(g) * v_next
            return (x_next, v_next)

        def _experts(ctx, idx, w1, b1, w2, b2):
            out = jnp.zeros((ctx.shape[0], w2.shape[2]), ctx.dtype)
            for e in range(E):
                h = _gelu(ctx @ w1[e] + b1[e])
                o = h @ w2[e] + b2[e]
                out = out + jnp.where((idx == e)[:, None], o, jnp.float32(0))
            return out

        def _forward(x, integration_weight, mu, router_w1, router_b1, router_w2, router_b2, halt_w1, halt_b1, halt_w2, halt_b2, expert_w1, expert_b1, expert_w2, expert_b2, shared_w1, shared_b1, shared_w2, shared_b2, shared_weight, refine_w1, refine_b1, refine_w2, refine_b2):
            b, n, d = x.shape
            xf = x.reshape(b * n, d)
            logits = _gelu(xf @ router_w1 + router_b1) @ router_w2 + router_b2
            probs = jax.nn.softmax(logits, axis=-1)
            topk_p, topk_i = jax.lax.top_k(probs, K)
            topk_p = topk_p / jnp.sum(topk_p, axis=-1, keepdims=True)
            flat_idx = topk_i.reshape(-1)
            flat_w = topk_p.reshape(-1, 1)
            v = jnp.zeros_like(xf)
            integrated = xf
            for _ in range(ITERS):
                ctx = jnp.concatenate([integrated, v], axis=-1)
                shared_ctrl = _gelu(ctx @ shared_w1 + shared_b1) @ shared_w2 + shared_b2
                x_sh, v_sh = _inl(shared_ctrl, integrated, v, mu)
                sw = jax.nn.sigmoid(shared_weight)
                ctx_e = jnp.repeat(ctx, K, axis=0)
                x_e = jnp.repeat(integrated, K, axis=0)
                v_e = jnp.repeat(v, K, axis=0)
                ctrl = _experts(ctx_e, flat_idx, expert_w1, expert_b1, expert_w2, expert_b2)
                x_r, v_r = _inl(ctrl, x_e, v_e, mu)
                x_r = (x_r * flat_w).reshape(-1, K, d).sum(axis=1)
                v_r = (v_r * flat_w).reshape(-1, K, d).sum(axis=1)
                x_next = sw * x_sh + (1.0 - sw) * x_r
                v_next = sw * v_sh + (1.0 - sw) * v_r
                halt = jax.nn.sigmoid(_gelu(integrated @ halt_w1 + halt_b1) @ halt_w2 + halt_b2)
                integrated = integrated + halt * (x_next - integrated)
                v = v + halt * (v_next - v)
            refined = _gelu(integrated @ refine_w1 + refine_b1) @ refine_w2 + refine_b2
            out = xf + integration_weight * refined
            return out.reshape(b, n, d)
        key = jax.random.key(seed)
        ks = jax.random.split(key, 12)
        rn = lambda k, s, sc=0.02: jax.random.normal(k, s, dtype=jnp.float32) * sc
        z = lambda s: jnp.zeros(s, jnp.float32)
        return {'x': jax.random.normal(ks[0], (B, N, D), dtype=jnp.float32), 'integration_weight': jnp.full((D,), 0.5, jnp.float32), 'mu': z((D,)), 'router_w1': rn(ks[1], (D, D // 4)), 'router_b1': z((D // 4,)), 'router_w2': rn(ks[2], (D // 4, E)), 'router_b2': z((E,)), 'halt_w1': rn(ks[3], (D, D // 4)), 'halt_b1': z((D // 4,)), 'halt_w2': rn(ks[4], (D // 4, 1)), 'halt_b2': z((1,)), 'expert_w1': rn(ks[5], (E, C, H)), 'expert_b1': z((E, H)), 'expert_w2': rn(ks[6], (E, H, 3 * D)), 'expert_b2': z((E, 3 * D)), 'shared_w1': rn(ks[7], (C, H)), 'shared_b1': z((H,)), 'shared_w2': rn(ks[8], (H, 3 * D)), 'shared_b2': z((3 * D,)), 'shared_weight': jnp.float32(0.5), 'refine_w1': rn(ks[9], (D, 2 * D)), 'refine_b1': z((2 * D,)), 'refine_w2': rn(ks[10], (2 * D, D)), 'refine_b2': z((D,))}
    _L3_ffn_all = _L3_ffn_setup()
    _L3_ffn_in = {k: v for k, v in _L3_ffn_all.items() if k in ('integration_weight', 'mu', 'router_w1', 'router_b1', 'router_w2', 'router_b2', 'halt_w1', 'halt_b1', 'halt_w2', 'halt_b2', 'expert_w1', 'expert_b1', 'expert_w2', 'expert_b2', 'shared_w1', 'shared_b1', 'shared_w2', 'shared_b2', 'shared_weight', 'refine_w1', 'refine_b1', 'refine_w2', 'refine_b2')}
    del _L3_ffn_all
    return {'x': x, 'ctx_1024': ctx_1024, 'mask_SxS2_fk1': mask_SxS2_fk1, 'mask_BxSxS2_ik0': mask_BxSxS2_ik0, 'L0_attn_Wq': _L0_attn_in['Wq'], 'L0_attn_Wk': _L0_attn_in['Wk'], 'L0_attn_Wv': _L0_attn_in['Wv'], 'L0_attn_Wo': _L0_attn_in['Wo'], 'L0_xattn_Wq1': _L0_xattn_in['Wq1'], 'L0_xattn_Wk1': _L0_xattn_in['Wk1'], 'L0_xattn_Wv1': _L0_xattn_in['Wv1'], 'L0_xattn_Wo1': _L0_xattn_in['Wo1'], 'L0_xattn_Wq2': _L0_xattn_in['Wq2'], 'L0_xattn_Wk2': _L0_xattn_in['Wk2'], 'L0_xattn_Wv2': _L0_xattn_in['Wv2'], 'L0_xattn_Wo2': _L0_xattn_in['Wo2'], 'L0_xattn_E1': _L0_xattn_in['E1'], 'L0_xattn_D1': _L0_xattn_in['D1'], 'L0_xattn_E2': _L0_xattn_in['E2'], 'L0_xattn_D2': _L0_xattn_in['D2'], 'L0_xattn_g1': _L0_xattn_in['g1'], 'L0_xattn_b1': _L0_xattn_in['b1'], 'L0_xattn_g2': _L0_xattn_in['g2'], 'L0_xattn_b2': _L0_xattn_in['b2'], 'L0_xattn_g3': _L0_xattn_in['g3'], 'L0_xattn_b3': _L0_xattn_in['b3'], 'L0_ffn_Wr': _L0_ffn_in['Wr'], 'L0_ffn_br': _L0_ffn_in['br'], 'L0_ffn_Wg_s': _L0_ffn_in['Wg_s'], 'L0_ffn_bg_s': _L0_ffn_in['bg_s'], 'L0_ffn_Wu_s': _L0_ffn_in['Wu_s'], 'L0_ffn_bu_s': _L0_ffn_in['bu_s'], 'L0_ffn_Wd_s': _L0_ffn_in['Wd_s'], 'L0_ffn_bd_s': _L0_ffn_in['bd_s'], 'L0_ffn_Wg': _L0_ffn_in['Wg'], 'L0_ffn_bg': _L0_ffn_in['bg'], 'L0_ffn_Wu': _L0_ffn_in['Wu'], 'L0_ffn_bu': _L0_ffn_in['bu'], 'L0_ffn_Wd': _L0_ffn_in['Wd'], 'L0_ffn_bd': _L0_ffn_in['bd'], 'L1_attn_w_q': _L1_attn_in['w_q'], 'L1_attn_w_k': _L1_attn_in['w_k'], 'L1_attn_w_v': _L1_attn_in['w_v'], 'L1_attn_w_o': _L1_attn_in['w_o'], 'L1_xattn_Wq': _L1_xattn_in['Wq'], 'L1_xattn_bq': _L1_xattn_in['bq'], 'L1_xattn_Wk': _L1_xattn_in['Wk'], 'L1_xattn_bk': _L1_xattn_in['bk'], 'L1_xattn_Wv': _L1_xattn_in['Wv'], 'L1_xattn_bv': _L1_xattn_in['bv'], 'L1_xattn_Wo': _L1_xattn_in['Wo'], 'L1_xattn_bo': _L1_xattn_in['bo'], 'L1_ffn_w1_w': _L1_ffn_in['w1_w'], 'L1_ffn_w1_s': _L1_ffn_in['w1_s'], 'L1_ffn_w2_w': _L1_ffn_in['w2_w'], 'L1_ffn_w2_s': _L1_ffn_in['w2_s'], 'L1_ffn_h1_w': _L1_ffn_in['h1_w'], 'L1_ffn_h1_s': _L1_ffn_in['h1_s'], 'L1_ffn_h2_w': _L1_ffn_in['h2_w'], 'L1_ffn_h2_s': _L1_ffn_in['h2_s'], 'L1_ffn_w3_w': _L1_ffn_in['w3_w'], 'L1_ffn_w3_s': _L1_ffn_in['w3_s'], 'L2_attn_Wq': _L2_attn_in['Wq'], 'L2_attn_bq': _L2_attn_in['bq'], 'L2_attn_Wk': _L2_attn_in['Wk'], 'L2_attn_bk': _L2_attn_in['bk'], 'L2_attn_Wv': _L2_attn_in['Wv'], 'L2_attn_bv': _L2_attn_in['bv'], 'L2_attn_Wp': _L2_attn_in['Wp'], 'L2_attn_bp': _L2_attn_in['bp'], 'L2_xattn_Wq': _L2_xattn_in['Wq'], 'L2_xattn_bq': _L2_xattn_in['bq'], 'L2_xattn_Wk': _L2_xattn_in['Wk'], 'L2_xattn_bk': _L2_xattn_in['bk'], 'L2_xattn_Wv': _L2_xattn_in['Wv'], 'L2_xattn_bv': _L2_xattn_in['bv'], 'L2_xattn_Wo': _L2_xattn_in['Wo'], 'L2_xattn_bo': _L2_xattn_in['bo'], 'L2_ffn_gate_W': _L2_ffn_in['gate_W'], 'L2_ffn_w1_e': _L2_ffn_in['w1_e'], 'L2_ffn_w3_e': _L2_ffn_in['w3_e'], 'L2_ffn_w2_e': _L2_ffn_in['w2_e'], 'L2_ffn_w1_s': _L2_ffn_in['w1_s'], 'L2_ffn_w3_s': _L2_ffn_in['w3_s'], 'L2_ffn_w2_s': _L2_ffn_in['w2_s'], 'L3_attn_Wq': _L3_attn_in['Wq'], 'L3_attn_bq': _L3_attn_in['bq'], 'L3_attn_Wk': _L3_attn_in['Wk'], 'L3_attn_bk': _L3_attn_in['bk'], 'L3_attn_Wv': _L3_attn_in['Wv'], 'L3_attn_bv': _L3_attn_in['bv'], 'L3_attn_Wo': _L3_attn_in['Wo'], 'L3_attn_bo': _L3_attn_in['bo'], 'L3_attn_rel_emb': _L3_attn_in['rel_emb'], 'L3_xattn_Wq': _L3_xattn_in['Wq'], 'L3_xattn_Wk': _L3_xattn_in['Wk'], 'L3_xattn_Wv': _L3_xattn_in['Wv'], 'L3_xattn_Wo': _L3_xattn_in['Wo'], 'L3_ffn_integration_weight': _L3_ffn_in['integration_weight'], 'L3_ffn_mu': _L3_ffn_in['mu'], 'L3_ffn_router_w1': _L3_ffn_in['router_w1'], 'L3_ffn_router_b1': _L3_ffn_in['router_b1'], 'L3_ffn_router_w2': _L3_ffn_in['router_w2'], 'L3_ffn_router_b2': _L3_ffn_in['router_b2'], 'L3_ffn_halt_w1': _L3_ffn_in['halt_w1'], 'L3_ffn_halt_b1': _L3_ffn_in['halt_b1'], 'L3_ffn_halt_w2': _L3_ffn_in['halt_w2'], 'L3_ffn_halt_b2': _L3_ffn_in['halt_b2'], 'L3_ffn_expert_w1': _L3_ffn_in['expert_w1'], 'L3_ffn_expert_b1': _L3_ffn_in['expert_b1'], 'L3_ffn_expert_w2': _L3_ffn_in['expert_w2'], 'L3_ffn_expert_b2': _L3_ffn_in['expert_b2'], 'L3_ffn_shared_w1': _L3_ffn_in['shared_w1'], 'L3_ffn_shared_b1': _L3_ffn_in['shared_b1'], 'L3_ffn_shared_w2': _L3_ffn_in['shared_w2'], 'L3_ffn_shared_b2': _L3_ffn_in['shared_b2'], 'L3_ffn_shared_weight': _L3_ffn_in['shared_weight'], 'L3_ffn_refine_w1': _L3_ffn_in['refine_w1'], 'L3_ffn_refine_b1': _L3_ffn_in['refine_b1'], 'L3_ffn_refine_w2': _L3_ffn_in['refine_w2'], 'L3_ffn_refine_b2': _L3_ffn_in['refine_b2']}

def reference(x, ctx_1024, mask_SxS2_fk1, mask_BxSxS2_ik0, L0_attn_Wq, L0_attn_Wk, L0_attn_Wv, L0_attn_Wo, L0_xattn_Wq1, L0_xattn_Wk1, L0_xattn_Wv1, L0_xattn_Wo1, L0_xattn_Wq2, L0_xattn_Wk2, L0_xattn_Wv2, L0_xattn_Wo2, L0_xattn_E1, L0_xattn_D1, L0_xattn_E2, L0_xattn_D2, L0_xattn_g1, L0_xattn_b1, L0_xattn_g2, L0_xattn_b2, L0_xattn_g3, L0_xattn_b3, L0_ffn_Wr, L0_ffn_br, L0_ffn_Wg_s, L0_ffn_bg_s, L0_ffn_Wu_s, L0_ffn_bu_s, L0_ffn_Wd_s, L0_ffn_bd_s, L0_ffn_Wg, L0_ffn_bg, L0_ffn_Wu, L0_ffn_bu, L0_ffn_Wd, L0_ffn_bd, L1_attn_w_q, L1_attn_w_k, L1_attn_w_v, L1_attn_w_o, L1_xattn_Wq, L1_xattn_bq, L1_xattn_Wk, L1_xattn_bk, L1_xattn_Wv, L1_xattn_bv, L1_xattn_Wo, L1_xattn_bo, L1_ffn_w1_w, L1_ffn_w1_s, L1_ffn_w2_w, L1_ffn_w2_s, L1_ffn_h1_w, L1_ffn_h1_s, L1_ffn_h2_w, L1_ffn_h2_s, L1_ffn_w3_w, L1_ffn_w3_s, L2_attn_Wq, L2_attn_bq, L2_attn_Wk, L2_attn_bk, L2_attn_Wv, L2_attn_bv, L2_attn_Wp, L2_attn_bp, L2_xattn_Wq, L2_xattn_bq, L2_xattn_Wk, L2_xattn_bk, L2_xattn_Wv, L2_xattn_bv, L2_xattn_Wo, L2_xattn_bo, L2_ffn_gate_W, L2_ffn_w1_e, L2_ffn_w3_e, L2_ffn_w2_e, L2_ffn_w1_s, L2_ffn_w3_s, L2_ffn_w2_s, L3_attn_Wq, L3_attn_bq, L3_attn_Wk, L3_attn_bk, L3_attn_Wv, L3_attn_bv, L3_attn_Wo, L3_attn_bo, L3_attn_rel_emb, L3_xattn_Wq, L3_xattn_Wk, L3_xattn_Wv, L3_xattn_Wo, L3_ffn_integration_weight, L3_ffn_mu, L3_ffn_router_w1, L3_ffn_router_b1, L3_ffn_router_w2, L3_ffn_router_b2, L3_ffn_halt_w1, L3_ffn_halt_b1, L3_ffn_halt_w2, L3_ffn_halt_b2, L3_ffn_expert_w1, L3_ffn_expert_b1, L3_ffn_expert_w2, L3_ffn_expert_b2, L3_ffn_shared_w1, L3_ffn_shared_b1, L3_ffn_shared_w2, L3_ffn_shared_b2, L3_ffn_shared_weight, L3_ffn_refine_w1, L3_ffn_refine_b1, L3_ffn_refine_w2, L3_ffn_refine_b2):
    import jax
    import jax.numpy as jnp

    def _L0_attn_ref(x, Wq, Wk, Wv, Wo):
        import jax, jax.numpy as jnp
        import numpy as np
        EPS = 1e-08

        def elu_feature_map(x):
            return jax.nn.elu(x) + 1.0
        B, S, D = x.shape
        H = 16
        Dh = D // H

        def proj(W):
            return (x @ W.T).reshape(B, S, H, Dh)
        q = elu_feature_map(proj(Wq))
        k = elu_feature_map(proj(Wk))
        v = proj(Wv)
        q_t = jnp.moveaxis(q, 1, 0)
        k_t = jnp.moveaxis(k, 1, 0)
        v_t = jnp.moveaxis(v, 1, 0)

        def step(carry, qkv):
            kv_sum, k_sum = carry
            q_i, k_i, v_i = qkv
            kv_sum = kv_sum + jnp.einsum('bhd,bhe->bhde', k_i, v_i)
            k_sum = k_sum + k_i
            num = jnp.einsum('bhd,bhde->bhe', q_i, kv_sum)
            den = jnp.sum(q_i * k_sum, axis=-1, keepdims=True)
            out_i = num / (den + EPS)
            return ((kv_sum, k_sum), out_i)
        kv0 = jnp.zeros((B, H, Dh, Dh), dtype=x.dtype)
        ks0 = jnp.zeros((B, H, Dh), dtype=x.dtype)
        _, out = jax.lax.scan(step, (kv0, ks0), (q_t, k_t, v_t))
        out = jnp.moveaxis(out, 0, 1).reshape(B, S, D)
        return out @ Wo.T

    def _L0_xattn_ref(mem, y, Wq1, Wk1, Wv1, Wo1, Wq2, Wk2, Wv2, Wo2, E1, D1, E2, D2, g1, b1, g2, b2, g3, b3):
        import jax, jax.numpy as jnp
        import numpy as np
        H = 8
        D = 128
        DQ = D // H
        BN = 64
        HID = 128
        B = 16
        S_T = 128
        S_M = 256
        SCALE = DQ ** 0.25
        EPS = 1e-05

        def _ln(x, g, b):
            m = jnp.mean(x, axis=-1, keepdims=True)
            v = jnp.mean(jnp.square(x - m), axis=-1, keepdims=True)
            return (x - m) * jax.lax.rsqrt(v + EPS) * g + b

        def _mhla(xq, xk, xv, Wq, Wk, Wv, Wo, masked):
            Q = jnp.einsum('bsq,hqd->bhsd', xq, Wq)
            K = jnp.einsum('bsq,hqd->bhsd', xk, Wk)
            V = jnp.einsum('bsq,hqd->bhsd', xv, Wv)
            if masked:
                s, d = (Q.shape[-2], Q.shape[-1])
                m = jnp.where(jnp.arange(d)[None, :] <= jnp.arange(s)[:, None], 0.0, -jnp.inf)
                Q = Q + m.astype(Q.dtype)
            A = jnp.einsum('bhsd,bhse->bhde', jax.nn.softmax(K / SCALE, axis=-1), V)
            Bm = jnp.einsum('bhsd,bhde->bhse', jax.nn.softmax(Q / SCALE, axis=-1), A)
            b, h, w, dd = Bm.shape
            Bm = Bm.reshape(b, w, h * dd)
            return Bm @ Wo.T
        y = y + _mhla(y, y, y, Wq1, Wk1, Wv1, Wo1, masked=True)
        y = _ln(y, g1, b1)
        y = y + _mhla(y, mem, mem, Wq2, Wk2, Wv2, Wo2, masked=False)
        y = _ln(y, g2, b2)
        h = y @ E1.T @ D1.T
        h = h * jax.nn.sigmoid(h)
        ffn = h @ E2.T @ D2.T
        y = _ln(y + ffn, g3, b3)
        return y

    def _L0_ffn_ref(hidden_states, Wr, br, Wg_s, bg_s, Wu_s, bu_s, Wd_s, bd_s, Wg, bg, Wu, bu, Wd, bd):
        import jax, jax.numpy as jnp
        import numpy as np
        H, I, E, K = (128, 64, 32, 8)
        B, S = (4, 128)

        def silu(x):
            return x * jax.nn.sigmoid(x)
        b, s, h = hidden_states.shape
        T = b * s
        x = hidden_states.reshape(T, h)
        logits = jnp.dot(x.astype(jnp.float32), Wr) + br
        aff = jax.nn.sigmoid(logits)
        top_v, top_i = jax.lax.top_k(aff, K)
        top_w = top_v / (jnp.sum(top_v, axis=-1, keepdims=True) + 1e-09)
        top_w = top_w.astype(hidden_states.dtype)
        e_total = Wr.shape[1]
        w_full = jnp.zeros((T, e_total), hidden_states.dtype)
        w_full = w_full.at[jnp.arange(T)[:, None], top_i].set(top_w)
        shared = jnp.dot(silu(jnp.dot(x, Wg_s) + bg_s) * (jnp.dot(x, Wu_s) + bu_s), Wd_s) + bd_s
        gate = silu(jnp.einsum('th,ehi->eti', x, Wg) + bg[:, None, :])
        up = jnp.einsum('th,ehi->eti', x, Wu) + bu[:, None, :]
        down = jnp.einsum('eti,eih->eth', gate * up, Wd) + bd[:, None, :]
        routed = jnp.einsum('te,eth->th', w_full, down)
        return (shared + routed).reshape(b, s, h)

    def _L1_attn_ref(x, w_q, w_k, w_v, w_o):
        import jax, jax.numpy as jnp
        import numpy as np
        D_K, D_MODEL, NUM_HEADS = (64, 128, 16)

        def _xavier(key, shape):
            fan_in, fan_out = (shape[-2], shape[-1])
            limit = float(np.sqrt(6.0 / (fan_in + fan_out)))
            return jax.random.uniform(key, shape, jnp.float32, -limit, limit)
        scale = 1.0 / jnp.sqrt(jnp.asarray(D_K, dtype=jnp.float32))
        q = jnp.einsum('bsd,hdk->bhsk', x, w_q)
        k = jnp.einsum('bsd,hdk->bhsk', x, w_k)
        v = jnp.einsum('bsd,hdk->bhsk', x, w_v)
        scores = jnp.einsum('bhqk,bhmk->bhqm', q, k) * scale
        weights = jax.nn.softmax(scores, axis=-1)
        z = jnp.einsum('bhqm,bhmk->bhqk', weights, v)
        b, h, s, dk = z.shape
        z = jnp.transpose(z, (0, 2, 1, 3)).reshape(b, s, h * dk)
        z = jnp.einsum('bse,ed->bsd', z, w_o)
        return x + z

    def _L1_xattn_ref(q, kv, Wq, bq, Wk, bk, Wv, bv, Wo, bo):
        import jax, jax.numpy as jnp
        import numpy as np
        D_MODEL = 128
        N_HEADS = 16
        HEAD_DIM = D_MODEL // N_HEADS
        B, Lq, _ = q.shape
        Lkv = kv.shape[1]
        qh = (q @ Wq.T + bq).reshape(B, Lq, N_HEADS, HEAD_DIM)
        kh = (kv @ Wk.T + bk).reshape(B, Lkv, N_HEADS, HEAD_DIM)
        vh = (kv @ Wv.T + bv).reshape(B, Lkv, N_HEADS, HEAD_DIM)
        scale = 1.0 / np.sqrt(HEAD_DIM).astype(np.float32)
        scores = jnp.einsum('bqhd,bkhd->bhqk', qh, kh) * scale
        attn = jax.nn.softmax(scores, axis=-1)
        ctx = jnp.einsum('bhqk,bkhd->bqhd', attn, vh).reshape(B, Lq, D_MODEL)
        out = ctx @ Wo.T + bo
        return out

    def _L1_ffn_ref(x, w1_w, w1_s, w2_w, w2_s, h1_w, h1_s, h2_w, h2_s, w3_w, w3_s):
        import jax, jax.numpy as jnp
        import numpy as np
        D_IN, D_HID = (128, 512)

        def _ternary(key, shape):
            return jax.random.randint(key, shape, -1, 2).astype(jnp.float32)

        def _tlin(x, w, s):
            return jnp.einsum('bsi,oi->bso', x, w) * s
        h = jax.nn.silu(_tlin(x, w1_w, w1_s)) * _tlin(x, w2_w, w2_s)
        h = jax.nn.gelu(_tlin(h, h1_w, h1_s), approximate=False)
        h = jax.nn.gelu(_tlin(h, h2_w, h2_s), approximate=False)
        return _tlin(h, w3_w, w3_s)

    def _L2_attn_ref(x, Wq, bq, Wk, bk, Wv, bv, Wp, bp):
        import jax, jax.numpy as jnp
        import numpy as np
        DIM = 128
        HEADS = 16
        HEAD_DIM = DIM // HEADS
        B, N = (4, 512)
        b, n, d = x.shape
        q = x @ Wq + bq
        k = x @ Wk + bk
        v = x @ Wv + bv
        split = lambda t: t.reshape(b, n, HEADS, HEAD_DIM).transpose(0, 2, 1, 3)
        q, k, v = (split(q), split(k), split(v))
        q = jax.nn.elu(q) + 1.0
        k = jax.nn.elu(k) + 1.0
        kv = jnp.einsum('bhnd,bhnf->bhdf', k, v)
        out = jnp.einsum('bhnd,bhdf->bhnf', q, kv)
        out = out.transpose(0, 2, 1, 3).reshape(b, n, d)
        return out @ Wp + bp

    def _L2_xattn_ref(xq, xk, xv, mask, Wq, bq, Wk, bk, Wv, bv, Wo, bo):
        import jax, jax.numpy as jnp
        import numpy as np
        B, S, D, H = (2, 256, 128, 16)
        DEPTH = D // H

        def _split_heads(x):
            b, s, _ = x.shape
            return x.reshape(b, s, H, DEPTH).transpose(0, 2, 1, 3)
        q = _split_heads(xq @ Wq + bq)
        k = _split_heads(xk @ Wk + bk)
        v = _split_heads(xv @ Wv + bv)
        logits = jnp.einsum('bhqd,bhkd->bhqk', q, k) / jnp.sqrt(jnp.float32(DEPTH))
        logits = logits + mask[None, None, :, :] * -1000000000.0
        weights = jax.nn.softmax(logits, axis=-1)
        attn = jnp.einsum('bhqk,bhkd->bhqd', weights, v)
        concat = attn.transpose(0, 2, 1, 3).reshape(xq.shape[0], -1, D)
        return concat @ Wo + bo

    def _L2_ffn_ref(hidden_states, gate_W, w1_e, w3_e, w2_e, w1_s, w3_s, w2_s):
        import jax, jax.numpy as jnp
        import numpy as np
        B, S, D, F, E, NS, K = (2, 128, 128, 512, 8, 8, 2)
        FS = F // NS
        b, s, d = hidden_states.shape
        e = gate_W.shape[0]
        flat = hidden_states.reshape(-1, d)
        T = flat.shape[0]
        logits = (flat @ gate_W.T).astype(jnp.float32)
        probs = jax.nn.softmax(logits, axis=-1)
        top_v, top_i = jax.lax.top_k(probs, K)
        gates = jnp.zeros((T, e), probs.dtype).at[jnp.arange(T)[:, None], top_i].set(top_v)
        g = jax.nn.silu(jnp.einsum('td,edf->etf', flat, w1_e))
        u = jnp.einsum('td,edf->etf', flat, w3_e)
        out_e = jnp.einsum('etf,efd->etd', g * u, w2_e)
        routed = jnp.einsum('te,etd->td', gates, out_e).reshape(b, s, d)
        gs = jax.nn.silu(jnp.einsum('bsd,ndf->nbsf', hidden_states, w1_s))
        us = jnp.einsum('bsd,ndf->nbsf', hidden_states, w3_s)
        shared = jnp.einsum('nbsf,nfd->bsd', gs * us, w2_s) / w1_s.shape[0]
        alpha = 0.5
        return alpha * shared + (1.0 - alpha) * routed

    def _L3_attn_ref(x, Wq, bq, Wk, bk, Wv, bv, Wo, bo, rel_emb):
        import jax, jax.numpy as jnp
        import numpy as np
        D_MODEL = 128
        N_HEADS = 16
        HEAD_DIM = D_MODEL // N_HEADS
        MAX_LEN = 256
        BATCH = 2
        SEQ = 256
        B, L, _ = x.shape

        def lin(x, W, b):
            return jnp.einsum('bld,ed->ble', x, W) + b

        def split_heads(t):
            return t.reshape(B, L, N_HEADS, HEAD_DIM).transpose(0, 2, 1, 3)
        q = split_heads(lin(x, Wq, bq))
        k = split_heads(lin(x, Wk, bk))
        v = split_heads(lin(x, Wv, bv))
        r = jnp.arange(L)
        idx = r[None, :] - r[:, None] + (MAX_LEN - 1)
        rel = rel_emb[idx]
        qk = jnp.einsum('bhld,bhrd->bhlr', q, k) / np.sqrt(HEAD_DIM)
        qk = qk + jnp.einsum('bhld,lrd->bhlr', q, rel)
        att = jax.nn.softmax(qk, axis=-1)
        out = jnp.einsum('bhlr,bhrd->bhld', att, v)
        out = out.transpose(0, 2, 1, 3).reshape(B, L, D_MODEL)
        return lin(out, Wo, bo)

    def _L3_xattn_ref(query, key, value, mask, Wq, Wk, Wv, Wo):
        import jax, jax.numpy as jnp
        import numpy as np
        B, S, D, H = (2, 256, 128, 16)
        DK = D // H

        def _split_heads(x):
            b, s, _ = x.shape
            return x.reshape(b, s, H, DK).transpose(0, 2, 1, 3)
        q = _split_heads(query @ Wq.T)
        k = _split_heads(key @ Wk.T)
        v = _split_heads(value @ Wv.T)
        inv_scale = jnp.asarray(DK ** 0.5, dtype=q.dtype)
        scores = jnp.einsum('bhqd,bhkd->bhqk', q, k) * inv_scale
        min_val = jnp.finfo(scores.dtype).min
        scores = jnp.where(mask[:, None, :, :] == 0, min_val, scores)
        attn = jax.nn.softmax(scores.astype(jnp.float32), axis=-1).astype(scores.dtype)
        ctx = jnp.einsum('bhqk,bhkd->bhqd', attn, v)
        ctx = ctx.transpose(0, 2, 1, 3).reshape(query.shape[0], -1, D)
        return ctx @ Wo.T

    def _L3_ffn_ref(x, integration_weight, mu, router_w1, router_b1, router_w2, router_b2, halt_w1, halt_b1, halt_w2, halt_b2, expert_w1, expert_b1, expert_w2, expert_b2, shared_w1, shared_b1, shared_w2, shared_b2, shared_weight, refine_w1, refine_b1, refine_w2, refine_b2):
        import jax, jax.numpy as jnp
        import numpy as np
        B, N, D = (4, 512, 128)
        E, K, H, ITERS = (8, 2, 64, 2)
        DT = 0.1
        C = 2 * D

        def _gelu(x):
            return jax.nn.gelu(x, approximate=False)

        def _inl(ctrl, xs, vs, mu):
            a, b, g = jnp.split(ctrl, 3, axis=-1)
            v_next = jax.nn.sigmoid(a) * vs - jax.nn.softplus(b) * (xs - mu)
            x_next = xs + DT * jax.nn.sigmoid(g) * v_next
            return (x_next, v_next)

        def _experts(ctx, idx, w1, b1, w2, b2):
            out = jnp.zeros((ctx.shape[0], w2.shape[2]), ctx.dtype)
            for e in range(E):
                h = _gelu(ctx @ w1[e] + b1[e])
                o = h @ w2[e] + b2[e]
                out = out + jnp.where((idx == e)[:, None], o, jnp.float32(0))
            return out

        def _forward(x, integration_weight, mu, router_w1, router_b1, router_w2, router_b2, halt_w1, halt_b1, halt_w2, halt_b2, expert_w1, expert_b1, expert_w2, expert_b2, shared_w1, shared_b1, shared_w2, shared_b2, shared_weight, refine_w1, refine_b1, refine_w2, refine_b2):
            b, n, d = x.shape
            xf = x.reshape(b * n, d)
            logits = _gelu(xf @ router_w1 + router_b1) @ router_w2 + router_b2
            probs = jax.nn.softmax(logits, axis=-1)
            topk_p, topk_i = jax.lax.top_k(probs, K)
            topk_p = topk_p / jnp.sum(topk_p, axis=-1, keepdims=True)
            flat_idx = topk_i.reshape(-1)
            flat_w = topk_p.reshape(-1, 1)
            v = jnp.zeros_like(xf)
            integrated = xf
            for _ in range(ITERS):
                ctx = jnp.concatenate([integrated, v], axis=-1)
                shared_ctrl = _gelu(ctx @ shared_w1 + shared_b1) @ shared_w2 + shared_b2
                x_sh, v_sh = _inl(shared_ctrl, integrated, v, mu)
                sw = jax.nn.sigmoid(shared_weight)
                ctx_e = jnp.repeat(ctx, K, axis=0)
                x_e = jnp.repeat(integrated, K, axis=0)
                v_e = jnp.repeat(v, K, axis=0)
                ctrl = _experts(ctx_e, flat_idx, expert_w1, expert_b1, expert_w2, expert_b2)
                x_r, v_r = _inl(ctrl, x_e, v_e, mu)
                x_r = (x_r * flat_w).reshape(-1, K, d).sum(axis=1)
                v_r = (v_r * flat_w).reshape(-1, K, d).sum(axis=1)
                x_next = sw * x_sh + (1.0 - sw) * x_r
                v_next = sw * v_sh + (1.0 - sw) * v_r
                halt = jax.nn.sigmoid(_gelu(integrated @ halt_w1 + halt_b1) @ halt_w2 + halt_b2)
                integrated = integrated + halt * (x_next - integrated)
                v = v + halt * (v_next - v)
            refined = _gelu(integrated @ refine_w1 + refine_b1) @ refine_w2 + refine_b2
            out = xf + integration_weight * refined
            return out.reshape(b, n, d)
        return _forward(x, integration_weight, mu, router_w1, router_b1, router_w2, router_b2, halt_w1, halt_b1, halt_w2, halt_b2, expert_w1, expert_b1, expert_w2, expert_b2, shared_w1, shared_b1, shared_w2, shared_b2, shared_weight, refine_w1, refine_b1, refine_w2, refine_b2)
    x = _layernorm(x + _L0_attn_ref(x, L0_attn_Wq, L0_attn_Wk, L0_attn_Wv, L0_attn_Wo), axis=-1)
    x = _layernorm(x + _L0_xattn_ref(ctx_1024, x, L0_xattn_Wq1, L0_xattn_Wk1, L0_xattn_Wv1, L0_xattn_Wo1, L0_xattn_Wq2, L0_xattn_Wk2, L0_xattn_Wv2, L0_xattn_Wo2, L0_xattn_E1, L0_xattn_D1, L0_xattn_E2, L0_xattn_D2, L0_xattn_g1, L0_xattn_b1, L0_xattn_g2, L0_xattn_b2, L0_xattn_g3, L0_xattn_b3), axis=-1)
    x = _layernorm(x + _L0_ffn_ref(x, L0_ffn_Wr, L0_ffn_br, L0_ffn_Wg_s, L0_ffn_bg_s, L0_ffn_Wu_s, L0_ffn_bu_s, L0_ffn_Wd_s, L0_ffn_bd_s, L0_ffn_Wg, L0_ffn_bg, L0_ffn_Wu, L0_ffn_bu, L0_ffn_Wd, L0_ffn_bd), axis=-1)
    x = _layernorm(x + _L1_attn_ref(x, L1_attn_w_q, L1_attn_w_k, L1_attn_w_v, L1_attn_w_o), axis=-1)
    x = _layernorm(x + _L1_xattn_ref(x, ctx_1024, L1_xattn_Wq, L1_xattn_bq, L1_xattn_Wk, L1_xattn_bk, L1_xattn_Wv, L1_xattn_bv, L1_xattn_Wo, L1_xattn_bo), axis=-1)
    x = _layernorm(x + _L1_ffn_ref(x, L1_ffn_w1_w, L1_ffn_w1_s, L1_ffn_w2_w, L1_ffn_w2_s, L1_ffn_h1_w, L1_ffn_h1_s, L1_ffn_h2_w, L1_ffn_h2_s, L1_ffn_w3_w, L1_ffn_w3_s), axis=-1)
    x = _layernorm(x + _L2_attn_ref(x, L2_attn_Wq, L2_attn_bq, L2_attn_Wk, L2_attn_bk, L2_attn_Wv, L2_attn_bv, L2_attn_Wp, L2_attn_bp), axis=-1)
    x = _layernorm(x + _L2_xattn_ref(x, ctx_1024, ctx_1024, mask_SxS2_fk1, L2_xattn_Wq, L2_xattn_bq, L2_xattn_Wk, L2_xattn_bk, L2_xattn_Wv, L2_xattn_bv, L2_xattn_Wo, L2_xattn_bo), axis=-1)
    x = _layernorm(x + _L2_ffn_ref(x, L2_ffn_gate_W, L2_ffn_w1_e, L2_ffn_w3_e, L2_ffn_w2_e, L2_ffn_w1_s, L2_ffn_w3_s, L2_ffn_w2_s), axis=-1)
    x = _layernorm(x + _L3_attn_ref(x, L3_attn_Wq, L3_attn_bq, L3_attn_Wk, L3_attn_bk, L3_attn_Wv, L3_attn_bv, L3_attn_Wo, L3_attn_bo, L3_attn_rel_emb), axis=-1)
    x = _layernorm(x + _L3_xattn_ref(x, ctx_1024, ctx_1024, mask_BxSxS2_ik0, L3_xattn_Wq, L3_xattn_Wk, L3_xattn_Wv, L3_xattn_Wo), axis=-1)
    x = _layernorm(x + _L3_ffn_ref(x, L3_ffn_integration_weight, L3_ffn_mu, L3_ffn_router_w1, L3_ffn_router_b1, L3_ffn_router_w2, L3_ffn_router_b2, L3_ffn_halt_w1, L3_ffn_halt_b1, L3_ffn_halt_w2, L3_ffn_halt_b2, L3_ffn_expert_w1, L3_ffn_expert_b1, L3_ffn_expert_w2, L3_ffn_expert_b2, L3_ffn_shared_w1, L3_ffn_shared_b1, L3_ffn_shared_w2, L3_ffn_shared_b2, L3_ffn_shared_weight, L3_ffn_refine_w1, L3_ffn_refine_b1, L3_ffn_refine_w2, L3_ffn_refine_b2), axis=-1)
    return x

_drawn_inputs = setup_inputs


def setup_inputs(seed=0):
    import zlib

    import numpy as np

    out = dict(_drawn_inputs(seed))
    spreads = {'L0_xattn_g1': (1.0, 0.2),
     'L0_xattn_b1': (0.0, 0.1),
     'L0_xattn_g2': (1.0, 0.2),
     'L0_xattn_b2': (0.0, 0.1),
     'L0_xattn_g3': (1.0, 0.2),
     'L0_xattn_b3': (0.0, 0.1),
     'L0_ffn_br': (0.0, 0.598),
     'L0_ffn_bg_s': (0.0, 0.488),
     'L0_ffn_bu_s': (0.0, 0.1),
     'L0_ffn_bd_s': (0.0, 0.1),
     'L0_ffn_bg': (0.0, 0.8),
     'L0_ffn_bu': (0.0, 0.8),
     'L0_ffn_bd': (0.0, 0.331),
     'L1_xattn_bq': (0.0, 0.1),
     'L1_xattn_bk': (0.0, 2.0),
     'L1_xattn_bv': (0.0, 0.1),
     'L1_xattn_bo': (0.0, 0.1),
     'L2_xattn_bq': (0.0, 0.1),
     'L2_xattn_bk': (0.0, 2.0),
     'L2_xattn_bv': (0.0, 0.1),
     'L2_xattn_bo': (0.0, 0.1),
     'L3_ffn_integration_weight': (0.5, 0.6),
     'L3_ffn_mu': (0.0, 2.0),
     'L3_ffn_router_b1': (0.0, 2.0),
     'L3_ffn_router_b2': (0.0, 2.0),
     'L3_ffn_halt_b1': (0.0, 2.0),
     'L3_ffn_expert_b1': (0.0, 2.0),
     'L3_ffn_expert_b2': (0.0, 2.0),
     'L3_ffn_shared_b1': (0.0, 2.0),
     'L3_ffn_shared_b2': (0.0, 2.0),
     'L3_ffn_refine_b1': (0.0, 0.8),
     'L3_ffn_refine_b2': (0.0, 0.296)}
    factors = {'L0_attn_Wq': 6.116,
     'L0_xattn_Wq1': 8.0,
     'L0_xattn_Wk1': 8.0,
     'L0_xattn_Wv1': 2.72,
     'L0_xattn_Wo1': 3.396,
     'L0_xattn_Wq2': 8.0,
     'L0_xattn_Wk2': 8.0,
     'L0_xattn_E1': 8.0,
     'L0_xattn_D1': 8.0,
     'L0_xattn_E2': 8.0,
     'L0_xattn_D2': 8.0,
     'L1_ffn_w1_w': 8.0,
     'L1_ffn_w1_s': 8.0,
     'L1_ffn_w2_w': 8.0,
     'L1_ffn_w2_s': 8.0,
     'L1_ffn_h1_w': 8.0,
     'L1_ffn_h1_s': 8.0,
     'L1_ffn_h2_w': 8.0,
     'L1_ffn_h2_s': 8.0,
     'L1_ffn_w3_w': 8.0,
     'L1_ffn_w3_s': 8.0,
     'L2_attn_bq': 4.141,
     'L2_attn_bk': 3.739,
     'L2_attn_bp': 22.04,
     'L2_ffn_gate_W': 8.0,
     'L2_ffn_w1_e': 8.0,
     'L2_ffn_w3_e': 8.0,
     'L2_ffn_w2_e': 8.0,
     'L2_ffn_w1_s': 8.0,
     'L2_ffn_w3_s': 8.0,
     'L2_ffn_w2_s': 8.0,
     'L3_attn_Wq': 5.13,
     'L3_attn_bq': 8.0,
     'L3_attn_Wk': 8.0,
     'L3_attn_bk': 64.0,
     'L3_attn_rel_emb': 5.156,
     'L3_ffn_router_w1': 41.277,
     'L3_ffn_router_w2': 32.742,
     'L3_ffn_halt_w1': 27.299,
     'L3_ffn_halt_w2': 8.0,
     'L3_ffn_expert_w1': 35.127,
     'L3_ffn_expert_w2': 33.165,
     'L3_ffn_shared_w1': 8.0,
     'L3_ffn_shared_w2': 8.0,
     'L3_ffn_refine_w1': 5.851,
     'L3_ffn_refine_w2': 5.351}
    for name, (base, spread) in spreads.items():
        noise = np.random.default_rng([zlib.crc32(name.encode()), seed]).standard_normal(out[name].shape)
        drawn = base * np.exp(spread * noise) if base else spread * noise
        out[name] = jnp.asarray(drawn.astype(out[name].dtype))
    for name, factor in factors.items():
        out[name] = (out[name] * factor).astype(out[name].dtype)
    return out
```

```python
from contextlib import ExitStack

import numpy as np
import concourse.bass as bass
from concourse import mybir

F32 = mybir.dt.float32
BF16 = mybir.dt.bfloat16
I32 = mybir.dt.int32
U32 = mybir.dt.uint32
ALU = mybir.AluOpType
ACT = mybir.ActivationFunctionType
AX = mybir.AxisListType
ENG = mybir.EngineType

P = 128
NB = 4
NG = 2
G = range(NG)
T = NB * P
KC = 77
EPS = 1e-5

L0A, L0X, L0F, L1A, L1X, L1F, L2A, L2X, L2F, L3A, L3X, L3F = range(12)
LN_KEYS = [L0A, "x1", "x2", "x3", L0X, L0F, L1A, L1X, L1F, L2A, L2X, L2F, L3A, L3X, L3F]
NORMS = ([(L0A, 0), (L0A, 1), ("x1", 0), ("x1", 1), ("x2", 0), ("x3", 0), ("x2", 1), (L0X, 0), ("x3", 1), (L0X, 1)]
         + [(k, g) for k in LN_KEYS[5:] for g in G])
SUBS = [n for n in NORMS if n[0] != L0X]
TURNS = ([(k, g) for k in ("in", L0A, "x1") for g in range(NG)] + [("x2", 0), ("x2", 1), (L0X, 0), (L0X, 1)]
         + [(k, g) for k in LN_KEYS[5:] if k != L3F for g in range(NG)])


class Signal:

    def __init__(self, sem, events):
        self.sem = sem
        self.value = {e: n + 1 for n, e in enumerate(events)}

    def __getitem__(self, event):
        return self.value[event]


def build(nc, dram, cols, out, steps):
    ctx = ExitStack()
    with ctx:
        def sb(name, shape, dt=F32):
            return ctx.enter_context(nc.sbuf_tensor(name, shape, dt))

        ps = ctx.enter_context(nc.psum_tensor("ps", [P, 8, T], F32))
        sems = []

        def signal(name, events):
            s = ctx.enter_context(nc.semaphore(name))
            sems.append(s)
            return Signal(s, events)

        def dma_sem(name):
            return ctx.enter_context(nc.semaphore(name))

        def pairs(keys, n=G):
            return [(k, i) for k in keys for i in n]

        x_tok = [sb(f"x_tok{g}", [P, NB, P]) for g in G]
        xT = [sb(f"xT{g}", [P, T]) for g in G]
        y_tok = [sb(f"y_tok{g}", [P, NB, P]) for g in G]
        stats = [sb(f"stats{g}", [P, NB, 6]) for g in G]
        mean_var = [sb(f"mean_var{g}", [P, NB, 2]) for g in G]
        rstd = [sb(f"rstd{g}", [P, NB]) for g in G]
        rstd_e = [sb(f"rstd_e{g}", [P, NB]) for g in G]
        minus_half = sb("minus_half", [P, NB])
        ctxT = sb("ctxT", [P, NG * NB * KC])
        mask_i = sb("mask_i", [P, NG * NB, KC], I32)
        const = sb("const", [P, cols["const"]["_width"]])
        expand = sb("expand", [96, 32 * 64], BF16)
        expand8 = sb("expand8", [24, 8 * P], BF16)
        ident_bf = sb("ident_bf", [P, P], BF16)
        w_first = [sb(f"w_{L}", [P, cols[L]["_width"]]) for L in (L0A, L0X)]
        w_even = sb("w_even", [P, max(cols[L]["_width"] for L in range(2, 12, 2))])
        w_odd = sb("w_odd", [P, max(cols[L]["_width"] for L in range(3, 12, 2))])
        x_in = [sb(f"x_in{g}", [P, NB, P]) for g in G]
        ARENA = [9216, 11600]
        arena = [sb(f"arena{k}", [P, ARENA[k]]) for k in range(2)]

        def W(L, name, rows=P):
            o, r, c = cols[L][name]
            t = w_first[L] if L in (L0A, L0X) else (w_even if L % 2 == 0 else w_odd)
            return t[0:r, o:o + c]

        def C(name):
            o, r, c = cols["const"][name]
            return const[0:r, o:o + c]

        ident = C("ident")

        class Carve:
            def __init__(self, k, base=None, start=0):
                self.t, self.o = (arena[k] if base is None else base), start

            def take(self, n, rows=P):
                a = self.t[0:rows, self.o:self.o + n]
                self.o += n
                assert self.o <= self.t.shape[1], self.o
                return a

        w_first_loaded = dma_sem("first_weights_loaded")
        const_loaded = dma_sem("const_loaded")
        first_x_loaded = dma_sem("first_x_loaded")
        w_loaded = {L: signal(f"weights_loaded_{L}", []) for L in range(2, 12)}
        x_loaded = signal("x_loaded", [])
        ctx_loaded = signal("ctx_loaded", [])
        stored = signal("result_stored", [])
        x_ready = signal("x_ready", NORMS)
        y_ready = signal("moments_ready", NORMS)
        sub_read = signal("sublayer_result_read", SUBS)
        rstd_ready = signal("rstd_ready", NORMS)
        res_ready = signal("residual_ready", [("x1", 0), ("x3", 0), ("x1", 1), ("x3", 1), ("x2", 0), ("x2", 1)]
                           + pairs([L1X, L2A, L2X, L3A]))
        sub_ready = signal("sublayer_result", SUBS)
        xT_psum = signal("transposed_state", TURNS)
        xT_ready = signal("xT_ready", TURNS)
        layer_done = signal("sublayer_products_done", list(range(12)))

        def bank(k):
            return ps[:, k, :]

        def bcast(a, n):
            return a.rearrange("p (m o) -> p m o", o=1).to_broadcast([a.shape[0], a.shape[1], n])

        def each_sequence(row):
            return row.rearrange("p (o d) -> p o d", o=1).to_broadcast([P, NB, P])

        def pe_turn_state(pe, key, g):
            if key != "in":
                pe.wait_ge(x_ready.sem, x_ready[key, g])
            for b in range(NB):
                mm = nc.tensor.transpose(ps[:, 6 + g, b * P:(b + 1) * P], src_of(key)[g][:, b, :], ident)
            mm.then_inc(xT_psum.sem, 1)

        def src_of(key):
            return x_in if key == "in" else y_tok if key in ("x1", "x2") else x_tok

        def act_copy_state(act, key, g, out, **kw):
            act.wait_ge(xT_psum.sem, xT_psum[key, g])
            nc.scalar.activation(out, bank(6 + g), ACT.Identity, **kw).then_inc(xT_ready.sem, 1)

        def dve_moments(dve, key, g):
            nc.vector.drain()
            for b in range(NB):
                nc.vector.bn_stats(stats[g][:, b, :], y_tok[g][:, b, :])
            nc.vector.drain()
            for b in range(NB):
                i = nc.vector.bn_aggr(mean_var[g][:, b, :], stats[g][:, b, :])
            i.then_inc(y_ready.sem, 1)

        def dve_normalise(dve, key, g, out):
            dve.wait_ge(rstd_ready.sem, rstd_ready[key, g])
            for b in range(NB):
                i = nc.vector.tensor_scalar(out[:, b, :], y_tok[g][:, b, :], mean_var[g][:, b, 0:1],
                                            rstd[g][:, b:b + 1], ALU.subtract, ALU.mult)
            i.then_inc(x_ready.sem, 1)

        def dve_sum(dve, key, g, residual=None, twice=False):
            dve.wait_ge(sub_ready.sem, sub_ready[key, g])
            res = x_tok[g] if residual is None else residual
            if key in ("x2", "x3", L1X, L2A, L2X, L3A):
                rk = {"x2": "x1", "x3": "x2"}.get(key, key)
                dve.wait_ge(res_ready.sem, res_ready[rk, g])
            yf = y_tok[g][:, :, :].rearrange("p b d -> p (b d)")
            rf = res[:, :, :].rearrange("p b d -> p (b d)")
            if twice:
                i = nc.vector.scalar_tensor_tensor(out=yf, in0=rf, scalar=2.0, in1=bank(6 + g),
                                                   op0=ALU.mult, op1=ALU.add)
            else:
                i = nc.vector.tensor_tensor(yf, bank(6 + g), rf, ALU.add)
            i.then_inc(sub_read.sem, 1)
            dve_moments(dve, key, g)

        def dve_norm(dve, key, g, residual=None, twice=False):
            dve_sum(dve, key, g, residual, twice)
            dve_normalise(dve, key, g, y_tok[g] if key in ("x1", "x2", "x3") else x_tok[g])

        def pool_rstd(pool, key, g):
            pool.wait_ge(y_ready.sem, y_ready[key, g])
            nc.gpsimd.tensor_scalar(rstd_e[g][:, :], mean_var[g][:, :, 1], EPS, None, ALU.add)
            nc.gpsimd.drain()
            nc.gpsimd.tensor_tensor(rstd[g][:, :], rstd_e[g][:, :], minus_half[:, :], ALU.pow)\
                .then_inc(rstd_ready.sem, 1)

        def pool_add_bias(pool, key, before, g, row):
            pool.wait_ge(xT_psum.sem, xT_psum[before, g])
            nc.gpsimd.tensor_tensor(x_tok[g][:, :, :], x_tok[g][:, :, :], each_sequence(row), ALU.add)\
                .then_inc(res_ready.sem, 1)

        c = Carve(0)
        a_ex = [c.take(2 * P) for _ in range(2)]
        a_re = [c.take(2 * P) for _ in range(2)]
        a_v = [c.take(P) for _ in range(2)]
        a_f = [c.take(2 * P) for _ in range(3)]
        a_kv = [c.take(8 * P) for _ in range(2)]
        a_pr = [c.take(8 * P) for _ in range(2)]
        a_kq = [c.take(P) for _ in range(2)]
        a_num = [c.take(P) for _ in range(2)]
        a_den = [c.take(16) for _ in range(2)]
        a_o = [c.take(T).rearrange("p (b d) -> p b d", b=NB) for g in G]
        a_oT = [c.take(T) for g in G]

        SEQ = range(NG * NB)
        a_proj = signal("a_projected", SEQ)
        a_elu = signal("a_elu_parts", SEQ)
        a_feat = signal("a_features", SEQ)
        a_outer = signal("a_keys_values", SEQ)
        a_cum = signal("a_summed_over_tokens", SEQ)
        a_mul = signal("a_times_query", SEQ)
        a_on = signal("a_heads", SEQ)
        a_turn = signal("a_heads_turned", list(G))
        a_oc = signal("a_heads_copied", list(G))

        def pe_l0a(pe):
            def project(j):
                g, b = divmod(j, NB)
                if j:
                    pe.wait_ge(a_elu.sem, a_elu[j - 1])
                nc.tensor.matmul(ps[:, 7, 0:3 * P], xT[g][:, b * P:(b + 1) * P], W(L0A, "Wqkv"),
                                 start=True, stop=True).then_inc(a_proj.sem, 1)

            def cumulate(j):
                pe.wait_ge(a_outer.sem, a_outer[j])
                if j >= 2:
                    pe.wait_ge(a_mul.sem, a_mul[j - 2])
                nc.tensor.matmul(ps[:, j % 2, 0:P], C("causal"), a_f[j % 3][:, P:2 * P], start=True, stop=True)
                for k in range(2):
                    mm = nc.tensor.matmul(bank(2 + 2 * (j % 2) + k), C("causal"), a_kv[j % 2][:, k * T:(k + 1) * T],
                                          start=True, stop=True)
                mm.then_inc(a_cum.sem, 1)

            def project_heads(g):
                pe.wait_ge(a_on.sem, a_on[NB * g + NB - 1])
                for b in range(NB):
                    mm = nc.tensor.transpose(ps[:, 6 + g, b * P:(b + 1) * P], a_o[g][:, b, :], ident)
                mm.then_inc(a_turn.sem, 1)
                if g:
                    pe_turn_state(pe, L0A, 0)
                pe.wait_ge(a_oc.sem, a_oc[g])
                for b in range(NB):
                    mm = nc.tensor.matmul(ps[:, 6 + g, b * P:(b + 1) * P], a_oT[g][:, b * P:(b + 1) * P],
                                          W(L0A, "Wo"), start=True, stop=True)
                mm.then_inc(sub_ready.sem, 1)

            for g in G:
                pe_turn_state(pe, "in", g)
            pe.wait_ge(xT_ready.sem, xT_ready["in", 1])
            for j in range(3):
                project(j)
            for j in SEQ:
                cumulate(j)
                if j + 3 in SEQ:
                    project(j + 3)
                if j == 5:
                    project_heads(0)
            project_heads(1)
            nc.tensor.drain().then_inc(layer_done.sem, 1)

        def act_values(g, keys, dst, src):
            v = src.rearrange("p (b q r e) -> p b q r e", b=NB, q=4, r=4)
            for r in range(4):
                d = dst[g][0:keys, :, r, :].rearrange("p b (q r e) -> p b q r e", q=4, r=4)
                i = nc.scalar.activation(d[:, :, :, r, :], v[:, :, :, r, :], ACT.Copy)
            return i

        def act_l0a(act):
            def elu_parts(j):
                act.wait_ge(a_proj.sem, a_proj[j])
                if j >= 2:
                    act.wait_ge(a_outer.sem, a_outer[j - 2])
                nc.scalar.activation(a_ex[j % 2], ps[:, 7, 0:2 * P], ACT.Relu, scale=-1.0)
                nc.scalar.activation(a_re[j % 2], ps[:, 7, 0:2 * P], ACT.Relu)
                nc.scalar.activation(a_v[j % 2], ps[:, 7, 2 * P:3 * P], ACT.Copy)
                nc.scalar.drain()
                nc.scalar.activation(a_ex[j % 2], a_ex[j % 2], ACT.Exp, scale=-1.0).then_inc(a_elu.sem, 1)

            for g in G:
                act_copy_state(act, "in", g, xT[g][:, :])
            for j in SEQ:
                elu_parts(j)
                if j == 7:
                    act.wait_ge(a_turn.sem, a_turn[0])
                    nc.scalar.activation(a_oT[0], bank(6), ACT.Copy).then_inc(a_oc.sem, 1)
            act.wait_ge(a_turn.sem, a_turn[1])
            nc.scalar.activation(a_oT[1], bank(7), ACT.Copy).then_inc(a_oc.sem, 1)
            act_copy_state(act, L0A, 0, xT[0][:, :])

        def dve_l0a(dve):
            def features(j):
                dve.wait_ge(a_elu.sem, a_elu[j])
                if j >= 3:
                    dve.wait_ge(a_cum.sem, a_cum[j - 3])
                nc.vector.tensor_tensor(a_f[j % 3], a_ex[j % 2], a_re[j % 2], ALU.add).then_inc(a_feat.sem, 1)

            def heads(j):
                g, b = divmod(j, NB)
                u = j % 2
                q = a_f[j % 3][:, 0:P]
                dve.wait_ge(a_cum.sem, a_cum[j])
                kv = ps[:, 2 + 2 * u:4 + 2 * u, :].rearrange("p k (h e d) -> p (k h) e d", e=8, d=8)
                qb = q.rearrange("p (h o d) -> p h o d", o=1, d=8).to_broadcast([P, 16, 8, 8])
                nc.vector.tensor_tensor(a_kq[u], ps[:, u, 0:P], q, ALU.mult)
                nc.vector.tensor_tensor(a_pr[u].rearrange("p (h e d) -> p h e d", e=8, d=8), kv, qb, ALU.mult)\
                    .then_inc(a_mul.sem, 1)
                nc.vector.drain()
                nc.vector.tensor_reduce(a_den[u], a_kq[u].rearrange("p (h d) -> p h d", d=8), AX.X, ALU.add)
                nc.vector.tensor_reduce(a_num[u], a_pr[u].rearrange("p (n d) -> p n d", d=8), AX.X, ALU.add)
                nc.vector.drain()
                nc.vector.tensor_scalar(a_den[u], a_den[u], 1e-8, None, ALU.add)
                nc.vector.drain()
                nc.vector.reciprocal(a_den[u], a_den[u])
                nc.vector.drain()
                nc.vector.tensor_tensor(a_o[g][:, b, :].rearrange("p (h e) -> p h e", e=8),
                                        a_num[u].rearrange("p (h e) -> p h e", e=8), bcast(a_den[u], 8), ALU.mult)\
                    .then_inc(a_on.sem, 1)

            features(0)
            features(1)
            for j in SEQ:
                if j + 2 in SEQ:
                    features(j + 2)
                heads(j)
                if j == 6:
                    dve_sum(dve, L0A, 0, x_in[0])
            dve_normalise(dve, L0A, 0, x_tok[0])
            dve_sum(dve, L0A, 1, x_in[1])

        def pool_l0a(pool):
            for j in SEQ:
                pool.wait_ge(a_feat.sem, a_feat[j])
                if j >= 2:
                    pool.wait_ge(a_cum.sem, a_cum[j - 2])
                k = a_f[j % 3][:, P:2 * P].rearrange("p (h o d) -> p h o d", o=1, d=8).to_broadcast([P, 16, 8, 8])
                v = a_v[j % 2].rearrange("p (h e o) -> p h e o", e=8, o=1).to_broadcast([P, 16, 8, 8])
                nc.gpsimd.tensor_tensor(a_kv[j % 2].rearrange("p (h e d) -> p h e d", e=8, d=8), k, v, ALU.mult)\
                    .then_inc(a_outer.sem, 1)
                if j == 7:
                    pool_rstd(pool, L0A, 0)
            pool_rstd(pool, L0A, 1)

        c = Carve(1)
        x_D = [c.take(2 * P) for _ in range(2)]
        x_V = [c.take(P) for _ in range(2)]
        x_max = [c.take(16) for _ in range(2)]
        x_A = c.take(P)
        x_QT = c.take(P)
        x_BT = [c.take(8 * P).rearrange("p (s m) -> p s m", s=8) for _ in range(2)]
        x_M = [c.take(P) for _ in range(2)]
        x_h = [c.take(T) for g in G]
        x_res = [c.take(T).rearrange("p (b d) -> p b d", b=NB) for g in G]
        x_yT = [c.take(T) for g in G]
        x_th = [c.take(T) for g in G]

        X2 = [(n, j) for n in range(2) for j in range(8)]
        x_fold = signal("x_bottlenecks_folded", [0])
        x_M_ready = signal("x_folded_copied", [0])
        x_qkv = signal("x_qkv", X2)
        x_shift = signal("x_shifted", X2)
        x_vs = signal("x_values", X2)
        x_exp = signal("x_exp", X2)
        x_sm = signal("x_softmaxed", X2)
        x_ab = signal("x_kv_and_q", X2)
        x_Am = signal("x_kv_blocks", X2)
        x_qc = signal("x_q_copied", X2)
        x_bt = signal("x_heads", X2)
        x_bm = signal("x_heads_spread", X2)
        x_pr = signal("x_projected", X2)
        x_hp = signal("x_hidden", list(G))
        x_tn = signal("x_tanh", list(G))
        x_hs = signal("x_silu", list(G))

        def pe_l0x(pe):
            nc.tensor.matmul(ps[:, 4, 0:P], W(L0X, "E1", 64), W(L0X, "D1", 64), start=True, stop=True)
            nc.tensor.matmul(ps[:, 4, P:2 * P], W(L0X, "E2", 64), W(L0X, "D2", 64), start=True, stop=True)\
                .then_inc(x_fold.sem, 1)

            def project(n, j):
                g, b = divmod(j, NB)
                if b == 0:
                    if n == 0 and g:
                        pe_turn_state(pe, L0A, g)
                    key = L0A if n == 0 else "x1"
                    if n == 1:
                        pe_turn_state(pe, "x1", g)
                    pe.wait_ge(xT_ready.sem, xT_ready[key, g])
                if (n, j) >= (0, 2):
                    m = 8 * n + j - 2
                    pe.wait_ge(x_shift.sem, m + 1)
                    pe.wait_ge(x_vs.sem, m + 1)
                cs = slice(b * P, (b + 1) * P)
                if n == 0:
                    mm = nc.tensor.matmul(ps[:, j % 2, 0:3 * P], xT[g][:, cs], W(L0X, "qkv0"), start=True, stop=True)
                else:
                    nc.tensor.matmul(ps[:, j % 2, 0:P], x_yT[g][:, cs], W(L0X, "qkv1")[:, 0:P], start=True, stop=True)
                    if j == 0:
                        pe.wait_ge(ctx_loaded.sem, 32)
                    mm = nc.tensor.matmul(ps[0:KC, j % 2, P:3 * P], ctxT[:, j * KC:(j + 1) * KC],
                                          W(L0X, "qkv1")[:, P:3 * P], start=True, stop=True)
                mm.then_inc(x_qkv.sem, 1)

            def kv(n, j):
                pe.wait_ge(x_sm.sem, x_sm[n, j])
                pe.wait_ge(x_vs.sem, x_vs[n, j])
                if (n, j) > (0, 0):
                    pe.wait_ge(x_Am.sem, x_Am[n, j] - 1)
                    pe.wait_ge(x_qc.sem, x_qc[n, j] - 1)
                rows = P if n == 0 else KC
                nc.tensor.matmul(ps[:, 2, 0:P], x_D[j % 2][0:rows, P:2 * P], x_V[j % 2][0:rows, :],
                                 start=True, stop=True)
                nc.tensor.transpose(ps[:, 5, 0:P], x_D[j % 2][:, 0:P], ident).then_inc(x_ab.sem, 1)

            def heads(n, j):
                pe.wait_ge(x_Am.sem, x_Am[n, j])
                pe.wait_ge(x_qc.sem, x_qc[n, j])
                if (n, j) > (0, 0):
                    pe.wait_ge(x_bm.sem, x_bm[n, j] - 1)
                nc.tensor.matmul(ps[:, 3, 0:P], x_A, x_QT, start=True, stop=True).then_inc(x_bt.sem, 1)

            def out(n, j):
                g, b = divmod(j, NB)
                pe.wait_ge(x_bm.sem, x_bm[n, j])
                for s in range(8):
                    mm = nc.tensor.matmul(ps[:, 6 + g, b * P:(b + 1) * P], x_BT[j % 2][:, s, :],
                                          W(L0X, f"Wo{n}")[:, s * P:(s + 1) * P], start=(s == 0), stop=(s == 7))
                mm.then_inc(x_pr.sem, 1)
                if b == NB - 1:
                    nc.tensor.drain().then_inc(sub_ready.sem, 1)

            def hidden(g):
                pe.wait_ge(xT_ready.sem, xT_ready["x2", g])
                if g == 0:
                    pe.wait_ge(x_M_ready.sem, 1)
                nc.tensor.matmul(bank(4 + g), x_M[0], x_yT[g], start=True, stop=True).then_inc(x_hp.sem, 1)

            def down(g):
                pe.wait_ge(x_hs.sem, x_hs[g])
                for b in range(NB):
                    mm = nc.tensor.matmul(ps[:, 6 + g, b * P:(b + 1) * P], x_h[g][:, b * P:(b + 1) * P], x_M[1],
                                          start=True, stop=True)
                mm.then_inc(sub_ready.sem, 1)

            project(*X2[0])
            for i in range(len(X2) + 2):
                if 0 <= i - 1 < len(X2):
                    heads(*X2[i - 1])
                if i + 1 < len(X2):
                    project(*X2[i + 1])
                if i < len(X2):
                    kv(*X2[i])
                if i >= 2:
                    out(*X2[i - 2])
                if i == 14:
                    pe_turn_state(pe, "x2", 0)
                if i == 15:
                    hidden(0)
                if i == 16:
                    down(0)
            pe_turn_state(pe, "x2", 1)
            hidden(1)
            pe_l0f_route(pe, 0)
            down(1)
            nc.tensor.drain().then_inc(layer_done.sem, 1)

        def act_l0x(act):
            act.wait_ge(x_fold.sem, 1)
            nc.scalar.activation(x_M[0], ps[:, 4, 0:P], ACT.Copy)
            nc.scalar.activation(x_M[1], ps[:, 4, P:2 * P], ACT.Copy, scale=0.5).then_inc(x_M_ready.sem, 1)
            def spread(n, j):
                act.wait_ge(x_bt.sem, x_bt[n, j])
                if (n, j) >= (0, 2):
                    act.wait_ge(x_pr.sem, x_pr[n, j] - 2)
                src = ps[:, 3, 0:P].rearrange("p (m s) -> p m s", s=8)
                for h in range(8):
                    dst = x_BT[j % 2][:, :, 16 * h:16 * h + 16].rearrange("p s m -> p m s")
                    i = nc.scalar.activation(dst, src, ACT.Copy, scale=C("head16")[:, h:h + 1])
                i.then_inc(x_bm.sem, 1)

            def ffn_state(g):
                act_copy_state(act, "x2", g, x_yT[g], scale=W(L0X, "g2c"), bias=W(L0X, "b2c"))

            def ffn_gate(g):
                act.wait_ge(x_hp.sem, x_hp[g])
                nc.scalar.activation(x_th[g], bank(4 + g), ACT.Tanh, scale=0.5).then_inc(x_tn.sem, 1)

            def copy_state(n, g):
                if n == 0:
                    act_copy_state(act, L0A, g, xT[g][:, :])
                else:
                    act_copy_state(act, "x1", g, x_yT[g], scale=W(L0X, "g1c"), bias=W(L0X, "b1c"))

            for i, (n, j) in enumerate(X2):
                if i + 1 < len(X2) and X2[i + 1][1] % NB == 0:
                    copy_state(X2[i + 1][0], X2[i + 1][1] // NB)
                act.wait_ge(x_shift.sem, x_shift[n, j])
                nc.scalar.activation(x_D[j % 2], x_D[j % 2], ACT.Exp, scale=0.5).then_inc(x_exp.sem, 1)
                if i >= 2:
                    act.wait_ge(x_ab.sem, i - 1)
                nc.scalar.activation(x_V[j % 2], ps[:, j % 2, 2 * P:3 * P], ACT.Copy).then_inc(x_vs.sem, 1)
                if i:
                    spread(*X2[i - 1])
                act.wait_ge(x_ab.sem, x_ab[n, j])
                if i:
                    act.wait_ge(x_bt.sem, i)
                nc.scalar.activation(x_QT, ps[:, 5, 0:P], ACT.Copy).then_inc(x_qc.sem, 1)
                if i == 14:
                    ffn_state(0)
            spread(*X2[-1])
            ffn_gate(0)
            ffn_state(1)
            ffn_gate(1)
            act_l0f_affinity(act)

        def dve_l0x_last_sum(dve, g):
            nc.vector.drain()
            nc.vector.tensor_tensor(y_tok[g][:, :, :], y_tok[g][:, :, :], each_sequence(W(L0X, "g3")), ALU.mult)
            nc.vector.drain()
            dve.wait_ge(res_ready.sem, res_ready["x3", g])
            nc.vector.tensor_tensor(y_tok[g][:, :, :], y_tok[g][:, :, :], x_tok[g][:, :, :], ALU.add)
            dve_moments(dve, L0X, g)

        def dve_l0x(dve):
            def shift(n, j):
                dve.wait_ge(x_qkv.sem, x_qkv[n, j])
                if (n, j) >= (0, 2):
                    dve.wait_ge(x_ab.sem, x_ab[n, j] - 2)
                d = x_D[j % 2].rearrange("p (h e) -> p h e", e=16)
                s = ps[:, j % 2, 0:2 * P].rearrange("p (h e) -> p h e", e=16)
                m = x_max[j % 2]
                if n == 0:
                    early = C("early").rearrange("p (o e) -> p o e", o=1).to_broadcast([P, 8, 16])
                    nc.vector.tensor_tensor(d[:, 0:8, :], s[:, 0:8, :], early, ALU.add)
                    nc.vector.drain()
                    nc.vector.tensor_reduce(m[:, 0:8], d[:, 0:8, :], AX.X, ALU.max)
                    nc.vector.tensor_reduce(m[:, 8:16], s[:, 8:16, :], AX.X, ALU.max)
                    nc.vector.drain()
                    nc.vector.tensor_tensor(d[:, 0:8, :], d[:, 0:8, :], bcast(m[:, 0:8], 16), ALU.subtract)
                    i = nc.vector.tensor_tensor(d[:, 8:16, :], s[:, 8:16, :], bcast(m[:, 8:16], 16), ALU.subtract)
                else:
                    nc.vector.tensor_reduce(m, s, AX.X, ALU.max)
                    nc.vector.drain()
                    i = nc.vector.tensor_tensor(d, s, bcast(m, 16), ALU.subtract)
                i.then_inc(x_shift.sem, 1)

            def soft(n, j):
                dve.wait_ge(x_exp.sem, x_exp[n, j])
                d = x_D[j % 2].rearrange("p (h e) -> p h e", e=16)
                m = x_max[j % 2]
                nc.vector.tensor_reduce(m, d, AX.X, ALU.add)
                nc.vector.drain()
                nc.vector.reciprocal(m, m)
                nc.vector.drain()
                nc.vector.tensor_tensor(d, d, bcast(m, 16), ALU.mult).then_inc(x_sm.sem, 1)

            def blocks(n, j):
                dve.wait_ge(x_ab.sem, x_ab[n, j])
                if (n, j) > (0, 0):
                    dve.wait_ge(x_bt.sem, x_bt[n, j] - 1)
                nc.vector.tensor_tensor(x_A, ps[:, 2, 0:P], C("block16"), ALU.mult).then_inc(x_Am.sem, 1)

            def silu(g):
                dve.wait_ge(x_tn.sem, x_tn[g])
                nc.vector.scalar_tensor_tensor(out=x_h[g], in0=x_th[g], scalar=1.0, in1=bank(4 + g),
                                               op0=ALU.add, op1=ALU.mult).then_inc(x_hs.sem, 1)

            norms = {6: ("x1", 0), 10: ("x1", 1), 14: ("x2", 0)}
            for i in range(len(X2) + 1):
                if i < len(X2):
                    shift(*X2[i])
                if i == 0:
                    dve_normalise(dve, L0A, 1, x_tok[1])
                if i in norms:
                    key, g = norms[i]
                    dve_sum(dve, key, g, None if key == "x1" else x_res[g])
                if i:
                    blocks(*X2[i - 1])
                if i < len(X2):
                    soft(*X2[i])
                if i in norms:
                    dve_normalise(dve, *norms[i], y_tok[norms[i][1]])
            silu(0)
            dve_sum(dve, "x3", 0, x_res[0])
            dve_sum(dve, "x2", 1, x_res[1])
            dve_normalise(dve, "x3", 0, y_tok[0])
            dve_normalise(dve, "x2", 1, y_tok[1])
            dve_l0x_last_sum(dve, 0)
            dve_normalise(dve, L0X, 0, x_tok[0])
            silu(1)
            dve_l0f_biased(dve, 0)
            dve_l0f_weights(dve, 0)
            dve_sum(dve, "x3", 1, x_res[1])

        def pool_l0x(pool):
            def affine(key, g, k):
                pool.wait_ge(xT_psum.sem, xT_psum[key, g])
                nc.gpsimd.tensor_tensor(x_res[g], y_tok[g][:, :, :], each_sequence(W(L0X, f"g{k}")), ALU.mult)
                nc.gpsimd.drain()
                nc.gpsimd.tensor_tensor(x_res[g], x_res[g], each_sequence(W(L0X, f"b{k}")), ALU.add)\
                    .then_inc(res_ready.sem, 1)

            for g in G:
                pool_rstd(pool, "x1", g)
                affine("x1", g, 1)
                nc.gpsimd.tensor_tensor(x_tok[g][:, :, :], x_tok[g][:, :, :], each_sequence(W(L0X, "b3")), ALU.add)\
                    .then_inc(res_ready.sem, 1)
            pool_rstd(pool, "x2", 0)
            affine("x2", 0, 2)
            pool_rstd(pool, "x3", 0)
            pool_rstd(pool, "x2", 1)
            pool_rstd(pool, L0X, 0)
            affine("x2", 1, 2)
            pool_rstd(pool, "x3", 1)
            pool_rstd(pool, L0X, 1)

        def split3(src, dst):
            nc.vector.tensor_copy(dst[:, :, 0, :], src)
            nc.vector.drain()
            nc.vector.tensor_tensor(src, src, dst[:, :, 0, :], ALU.subtract)
            nc.vector.drain()
            nc.vector.tensor_copy(dst[:, :, 1, :], src)
            nc.vector.drain()
            nc.vector.tensor_tensor(src, src, dst[:, :, 1, :], ALU.subtract)
            nc.vector.drain()
            return nc.vector.tensor_copy(dst[:, :, 2, :], src)

        def pe_turn_result(pe, key, g, copied, subT):
            pe.wait_ge(copied.sem, copied[g])
            for b in range(NB):
                mm = nc.tensor.transpose(ps[:, 6 + g, b * P:(b + 1) * P], subT[g][:, b * P:(b + 1) * P], ident)
            mm.then_inc(sub_ready.sem, 1)

        c = Carve(0)
        f_lg = [c.take(NB * 32).rearrange("p (b e) -> p b e", b=NB) for g in G]
        f_rep = [c.take(NB * 32).rearrange("p (b e) -> p b e", b=NB) for g in G]
        f_top = [c.take(NB * 8).rearrange("p (b e) -> p b e", b=NB) for g in G]
        f_sum = [c.take(NB) for g in G]
        f_w3 = [c.take(NB * 48).bitcast(BF16).rearrange("p (b s e) -> p b s e", b=NB, s=3) for g in G]
        f_wT3 = [c.take(T // 2, 96).bitcast(BF16) for g in G]
        f_sg = [c.take(T) for _ in range(2)]
        f_h = [c.take(T) for _ in range(2)]
        f_hw = [c.take(T) for _ in range(2)]
        f_sT = [c.take(T) for g in G]
        f_bdf = c.take(P, 96)
        f_bd3 = c.take(3 * P // 2, 96).bitcast(BF16).rearrange("p (s d) -> p s d", s=3)

        NP = 17
        FP = [(g, p) for g in G for p in range(NP)]
        f_route = signal("f_logits", list(G))
        f_bias = signal("f_logits_biased", list(G))
        f_tanh = signal("f_tanh", list(G))
        f_split = signal("f_weights_split", list(G))
        f_turn = signal("f_weights_turned", list(G))
        f_wc = signal("f_weights_copied", list(G))
        f_gu = signal("f_gate_up", FP)
        f_silu = signal("f_silu", FP)
        f_hid = signal("f_up_done", FP)
        f_wtd = signal("f_hidden_weighted", FP)
        f_down = signal("f_down", FP)
        f_copied = signal("f_result_copied", list(G))

        def pe_l0f_route(pe, g):
            if g == 0:
                pe.wait_ge(w_loaded[L0F].sem, 16)
            pe_turn_state(pe, L0X, g)
            pe.wait_ge(xT_ready.sem, xT_ready[L0X, g])
            for b in range(NB):
                mm = nc.tensor.matmul(ps[:, 4 + g, 32 * b:32 * b + 32], xT[g][:, b * P:(b + 1) * P],
                                      W(L0F, "Wr"), start=True, stop=True)
            mm.then_inc(f_route.sem, 1)

        def pe_l0f(pe):
            def turn_weights(g):
                pe.wait_ge(f_split.sem, f_split[g])
                for b in range(NB):
                    mm = nc.tensor.transpose(bank(4 + g)[0:96, 0:T // 2].bitcast(BF16)[:, b * P:(b + 1) * P],
                                             f_w3[g][:, b, :, :].rearrange("p s e -> p (s e)"), ident_bf[:, :])
                mm.then_inc(f_turn.sem, 1)

            def gate_up(g, p):
                i = FP.index((g, p))
                rows = P if p < 16 else 64
                if i >= 2:
                    pe.wait_ge(f_hid.sem, i - 1)
                for k, w in ((0, "Wg"), (2, "Wu")):
                    lhsT = W(L0F, w)[:, p * P:(p + 1) * P] if p < 16 else W(L0F, w + "s")
                    mm = nc.tensor.matmul(ps[0:rows, k + i % 2, :], lhsT, xT[g][:, :], start=True, stop=True)
                mm.then_inc(f_gu.sem, 1)
                if p == 0:
                    turn_weights(g)

            def down(g, p):
                i = FP.index((g, p))
                rows = P if p < 16 else 64
                pe.wait_ge(f_wtd.sem, f_wtd[g, p])
                lhsT = W(L0F, "Wd")[:, p * P:(p + 1) * P] if p < 16 else W(L0F, "Wds", 64)
                nc.tensor.matmul(bank(6 + g), lhsT, f_hw[i % 2][0:rows, :], start=(p == 0), stop=False)\
                    .then_inc(f_down.sem, 1)
                if p == 16:
                    pe.wait_ge(f_bd.sem, 1)
                    for k in range(3):
                        mm = nc.tensor.matmul(bank(6 + g), f_bd3[:, k, :], f_wT3[g], start=False, stop=(k == 2))
                    mm.then_inc(f_acc.sem, 1)

            def spread(g, p):
                if p == 0:
                    pe.wait_ge(f_wc.sem, f_wc[g])
                i = FP.index((g, p))
                if p >= 1:
                    pe.wait_ge(f_wtd.sem, f_wtd[g, p - 1])
                nc.tensor.matmul(bank(4 + g), expand[:, p * P:(p + 1) * P], f_wT3[g], start=True, stop=True)\
                    .then_inc(f_sp.sem, 1)

            for i, (g, p) in enumerate(FP):
                gate_up(g, p)
                if i >= 1:
                    down(*FP[i - 1])
                if p < 16:
                    spread(g, p)
                if i == 4:
                    pe_l0f_route(pe, 1)
                if i == NP + 2:
                    pe_turn_result(pe, L0F, 0, f_copied, f_sT)
            down(*FP[-1])
            pe_turn_result(pe, L0F, 1, f_copied, f_sT)
            nc.tensor.drain().then_inc(layer_done.sem, 1)

        f_sp = signal("f_weights_spread", [(g, p) for g in G for p in range(16)])
        f_bd = signal("f_bias_split", [0])
        f_acc = signal("f_result", list(G))

        def act_affinity(act, g):
            act.wait_ge(f_bias.sem, f_bias[g])
            nc.scalar.activation(f_rep[g], f_lg[g], ACT.Tanh, scale=0.5).then_inc(f_tanh.sem, 1)

        def act_l0f_affinity(act):
            act_copy_state(act, L0X, 0, xT[0][:, :])
            act_affinity(act, 0)

        def act_l0f(act):
            def weights(g):
                act.wait_ge(f_turn.sem, f_turn[g])
                nc.scalar.activation(f_wT3[g], bank(4 + g)[0:96, 0:T // 2].bitcast(BF16), ACT.Copy)\
                    .then_inc(f_wc.sem, 1)

            for i, (g, p) in enumerate(FP):
                rows = P if p < 16 else 64
                if i == 5:
                    act_copy_state(act, L0X, 1, xT[1][:, :])
                if i == 7:
                    act_affinity(act, 1)
                act.wait_ge(f_gu.sem, f_gu[g, p])
                if i >= 2:
                    act.wait_ge(f_hid.sem, i - 1)
                bg = W(L0F, "bg")[:, p:p + 1] if p < 16 else W(L0F, "bgs", 64)
                nc.scalar.activation(f_sg[i % 2][0:rows, :], ps[0:rows, i % 2, :], ACT.Silu, bias=bg)\
                    .then_inc(f_silu.sem, 1)
                if p == 0:
                    weights(g)
                if i == NP + 1:
                    copy_result(act, 0)
            copy_result(act, 1)

        def copy_result(act, g):
            act.wait_ge(f_acc.sem, f_acc[g])
            nc.scalar.activation(f_sT[g], bank(6 + g), ACT.Identity, bias=W(L0F, "bds")).then_inc(f_copied.sem, 1)

        def dve_l0f_biased(dve, g):
            dve.wait_ge(f_route.sem, f_route[g])
            nc.vector.tensor_tensor(f_lg[g], ps[:, 4 + g, 0:P].rearrange("p (b e) -> p b e", b=NB),
                                    W(L0F, "br").rearrange("p (o e) -> p o e", o=1).to_broadcast([P, NB, 32]),
                                    ALU.add).then_inc(f_bias.sem, 1)

        def dve_l0f_weights(dve, g):
            dve.wait_ge(f_tanh.sem, f_tanh[g])
            nc.vector.tensor_scalar(f_lg[g], f_rep[g], 0.5, 0.5, ALU.mult, ALU.add)
            nc.vector.drain()
            for b in range(NB):
                nc.vector.max(f_top[g][:, b, :], f_lg[g][:, b, :])
            nc.vector.drain()
            for b in range(NB):
                nc.vector.match_replace(f_rep[g][:, b, :], f_top[g][:, b, :], f_lg[g][:, b, :], -1.0)
            nc.vector.tensor_reduce(f_sum[g], f_top[g], AX.X, ALU.add)
            nc.vector.drain()
            nc.vector.tensor_tensor(f_rep[g], f_rep[g], f_lg[g], ALU.not_equal)
            nc.vector.tensor_scalar(f_sum[g], f_sum[g], 1e-9, None, ALU.add)
            nc.vector.drain()
            nc.vector.reciprocal(f_sum[g], f_sum[g])
            nc.vector.tensor_tensor(f_lg[g], f_lg[g], f_rep[g], ALU.mult)
            nc.vector.drain()
            nc.vector.tensor_tensor(f_lg[g], f_lg[g], bcast(f_sum[g], 32), ALU.mult)
            nc.vector.drain()
            split3(f_lg[g], f_w3[g]).then_inc(f_split.sem, 1)

        def dve_l0f(dve):
            def split_biases():
                dve.wait_ge(w_loaded[L0F].sem, 16)
                nc.vector.tensor_copy(f_bdf, W(L0F, "bd", 96))
                nc.vector.drain()
                split3(f_bdf.rearrange("p (o d) -> p o d", o=1), f_bd3.rearrange("p (o s) d -> p o s d", o=1))\
                    .then_inc(f_bd.sem, 1)

            for i, (g, p) in enumerate(FP):
                rows = P if p < 16 else 64
                if i == 6:
                    dve_l0f_biased(dve, 1)
                if i == 8:
                    dve_l0f_weights(dve, 1)
                dve.wait_ge(f_silu.sem, f_silu[g, p])
                if i >= 2:
                    dve.wait_ge(f_down.sem, i - 1)
                bu = W(L0F, "bu")[:, p:p + 1] if p < 16 else W(L0F, "bus", 64)
                dst = f_h[i % 2] if p < 16 else f_hw[i % 2]
                i1 = nc.vector.scalar_tensor_tensor(out=dst[0:rows, :], in0=ps[0:rows, 2 + i % 2, :], scalar=bu,
                                                    in1=f_sg[i % 2][0:rows, :], op0=ALU.add, op1=ALU.mult)
                i1.then_inc(f_hid.sem, 1)
                nc.vector.drain()
                if p < 16:
                    dve.wait_ge(f_sp.sem, f_sp[g, p])
                    nc.vector.tensor_tensor(f_hw[i % 2], f_h[i % 2], bank(4 + g), ALU.mult).then_inc(f_wtd.sem, 1)
                else:
                    nc.vector.drain().then_inc(f_wtd.sem, 1)
                if i == 0:
                    dve_normalise(dve, "x3", 1, y_tok[1])
                    dve_l0x_last_sum(dve, 1)
                if i == 1:
                    dve_normalise(dve, L0X, 1, x_tok[1])
                if i == 3:
                    split_biases()
                if i == NP + 3:
                    dve_sum(dve, L0F, 0)
                if i == NP + 4:
                    dve_normalise(dve, L0F, 0, x_tok[0])
            dve_sum(dve, L0F, 1)

        def pool_l0f(pool):
            for g in G:
                pool_rstd(pool, L0F, g)

        c = Carve(1)
        b_V = c.take(NB * 1024).rearrange("p (b n) -> p b n", b=NB)
        b_q = [c.take(T) for _ in range(2)]
        b_k = [c.take(T) for _ in range(2)]
        b_P = [c.take(8 * P).rearrange("p (m k) -> p m k", m=8) for _ in range(3)]
        b_PT = c.take(8 * P).rearrange("p (m q) -> p m q", m=8)
        b_z = [c.take(T) for _ in range(2)]
        b_max = [c.take(8) for _ in range(2)]
        b_sum = [c.take(8) for _ in range(3)]

        b_sub_T = [arena[0][:, g * T:(g + 1) * T] for g in G]

        BU = [(g, c) for g in G for c in range(8)]
        NU = len(BU)
        b_vp = signal("b_values", [(g, b) for g in G for b in range(NB)])
        b_va = signal("b_values_low", [(g, b) for g in G for b in range(NB)])
        b_vd = signal("b_values_high", [(g, b) for g in G for b in range(NB)])
        b_qk = signal("b_queries_keys", [(i, w) for i in range(NU) for w in "qk"])
        b_qkc = signal("b_queries_keys_copied", [(i, w) for i in range(NU) for w in "qk"])
        b_sc = signal("b_scores", range(NU))
        b_sub = signal("b_less_max", range(NU))
        b_exp = signal("b_exp", range(NU))
        b_rs = signal("b_sums", range(NU))
        b_nm = signal("b_probs", range(NU))
        b_pt = signal("b_probs_turned", range(NU))
        b_ea = signal("b_turned_low", range(NU))
        b_ed = signal("b_turned_high", range(NU))
        b_zp = signal("b_heads", range(NU))
        b_zc = signal("b_heads_copied", range(NU))
        b_acc = signal("b_projected", range(NU))
        b_copied = signal("b_result_copied", list(G))

        def pe_l1a(pe):
            pe.wait_ge(w_loaded[L1A].sem, 16)

            def values(g):
                for b in range(NB):
                    if g and b == 0:
                        pe.wait_ge(b_zc.sem, b_zc[7])
                        pe.wait_ge(b_qkc.sem, b_qkc[10, "k"])
                    if b:
                        pe.wait_ge(b_va.sem, b_va[g, b - 1])
                        pe.wait_ge(b_vd.sem, b_vd[g, b - 1])
                    for k in range(2):
                        mm = nc.tensor.matmul(bank(4 + k), xT[g][:, b * P:(b + 1) * P],
                                              W(L1A, "Wv")[:, T * k:T * k + T], start=True, stop=True)
                    mm.then_inc(b_vp.sem, 1)

            def project(i):
                g, c = BU[i]
                if i == 0 or i == 11:
                    pe.wait_ge(b_va.sem, b_va[g if i else 0, NB - 1])
                    pe.wait_ge(b_vd.sem, b_vd[g if i else 0, NB - 1])
                if i >= 4:
                    pe.wait_ge(b_zc.sem, b_zc[i - 4])
                nc.tensor.matmul(bank(4), W(L1A, "Wq")[:, c * P:(c + 1) * P], xT[g][:, :], start=True, stop=True)\
                    .then_inc(b_qk.sem, 1)
                if i >= 1:
                    pe.wait_ge(b_qkc.sem, b_qkc[i - 1, "k"])
                nc.tensor.matmul(bank(5), W(L1A, "Wk")[:, c * P:(c + 1) * P], xT[g][:, :], start=True, stop=True)\
                    .then_inc(b_qk.sem, 1)

            def scores(i):
                pe.wait_ge(b_qkc.sem, b_qkc[i, "k"])
                if i:
                    pe.wait_ge(b_sub.sem, b_sub[i - 1])
                for b in range(NB):
                    for h in range(2):
                        cs = slice(b * P, (b + 1) * P)
                        mm = nc.tensor.matmul(ps[:, h, cs],
                                             
                                              b_q[i % 2][64 * h:64 * h + 64, cs], b_k[i % 2][64 * h:64 * h + 64, cs],
                                              start=True, stop=True, tile_position=(64 * h, 0))
                mm.then_inc(b_sc.sem, 1)

            def turn(i):
                pe.wait_ge(b_nm.sem, b_nm[i])
                if i:
                    pe.wait_ge(b_ea.sem, b_ea[i - 1])
                    pe.wait_ge(b_ed.sem, b_ed[i - 1])
                for m in range(8):
                    mm = nc.tensor.transpose(ps[:, 2 + m // 4, (m % 4) * P:(m % 4 + 1) * P], b_P[i % 3][:, m, :], ident)
                mm.then_inc(b_pt.sem, 1)

            def heads(i):
                g, c = BU[i]
                pe.wait_ge(b_ea.sem, b_ea[i])
                pe.wait_ge(b_ed.sem, b_ed[i])
                if i + 3 < NU:
                    pe.wait_ge(b_qkc.sem, b_qkc[i + 3, "q"])
                elif i:
                    pe.wait_ge(b_zc.sem, b_zc[i - 1])
                for b in range(NB):
                    for h in range(2):
                        mm = nc.tensor.matmul(ps[64 * h:64 * h + 64, 4, b * P:(b + 1) * P],
                                              b_V[:, b, c * P + 64 * h:c * P + 64 * h + 64], b_PT[:, 4 * h + b, :],
                                              start=True, stop=True, tile_position=(0, 64 * h))
                mm.then_inc(b_zp.sem, 1)

            def out(i):
                g, c = BU[i]
                pe.wait_ge(b_zc.sem, b_zc[i])
                nc.tensor.matmul(bank(6 + g), W(L1A, "Wo")[:, c * P:(c + 1) * P], b_z[i % 2],
                                 start=(c == 0), stop=(c == 7)).then_inc(b_acc.sem, 1)

            pe_turn_state(pe, L0F, 0)
            pe.wait_ge(xT_ready.sem, xT_ready[L0F, 0])
            values(0)
            project(0)
            for i in range(NU + 4):
                if i < NU:
                    scores(i)
                if 0 <= i - 3 < NU:
                    heads(i - 3)
                if 0 <= i - 4 < NU:
                    out(i - 4)
                if i == 5:
                    pe_turn_state(pe, L0F, 1)
                    pe.wait_ge(xT_ready.sem, xT_ready[L0F, 1])
                if i == 10:
                    values(1)
                if i + 1 < NU:
                    project(i + 1)
                if 0 <= i - 2 < NU:
                    turn(i - 2)
                if i == 13:
                    pe_turn_result(pe, L1A, 0, b_copied, b_sub_T)
                if i == NU + 1:
                    pe.wait_ge(b_sub.sem, b_sub[NU - 1])
                    pe_context_part(pe, L1X, "k")
                if i == NU + 2:
                    pe_context_queries(pe, L1X, 0)
                if i == NU + 3:
                    pe_context_part(pe, L1X, "v")
            pe_turn_result(pe, L1A, 1, b_copied, b_sub_T)
            nc.tensor.drain().then_inc(layer_done.sem, 1)

        def act_l1a(act):
            def project(i):
                act.wait_ge(b_qk.sem, b_qk[i, "q"])
                if i >= 2:
                    act.wait_ge(b_sc.sem, b_sc[i - 2])
                nc.scalar.activation(b_q[i % 2], bank(4), ACT.Copy).then_inc(b_qkc.sem, 1)
                act.wait_ge(b_qk.sem, b_qk[i, "k"])
                nc.scalar.activation(b_k[i % 2], bank(5), ACT.Copy).then_inc(b_qkc.sem, 1)

            def values(g):
                for b in range(NB):
                    act.wait_ge(b_vp.sem, b_vp[g, b])
                    nc.scalar.activation(b_V[:, b, 0:T], bank(4), ACT.Copy).then_inc(b_va.sem, 1)

            def result(g):
                act.wait_ge(b_acc.sem, b_acc[8 * g + 7])
                nc.scalar.activation(b_sub_T[g], bank(6 + g), ACT.Copy).then_inc(b_copied.sem, 1)

            act_copy_state(act, L0F, 0, xT[0][:, :])
            values(0)
            project(0)
            for i in range(NU + 5):
                if 0 <= i - 3 < NU:
                    act.wait_ge(b_zp.sem, b_zp[i - 3])
                    if i - 3 >= 2:
                        act.wait_ge(b_acc.sem, b_acc[i - 5])
                    nc.scalar.activation(b_z[(i - 3) % 2], bank(4), ACT.Copy).then_inc(b_zc.sem, 1)
                if i < NU:
                    act.wait_ge(b_sub.sem, b_sub[i])
                    nc.scalar.activation(b_P[i % 3], b_P[i % 3], ACT.Exp, scale=0.125).then_inc(b_exp.sem, 1)
                if i == 5:
                    act_copy_state(act, L0F, 1, xT[1][:, :])
                if i == 10:
                    values(1)
                if i + 1 < NU:
                    project(i + 1)
                if 0 <= i - 2 < NU:
                    act.wait_ge(b_pt.sem, b_pt[i - 2])
                    nc.scalar.activation(b_PT[:, 0:4, :], bank(2).rearrange("p (m q) -> p m q", m=4), ACT.Copy)\
                        .then_inc(b_ea.sem, 1)
                if i == 12:
                    result(0)
                if i == NU + 2:
                    act_context_part(act, L1X, "k")
                    act_copy_state(act, L1A, 0, xT[0][:, :])
            result(1)
            act_context_part(act, L1X, "v")

        def dve_l1a(dve):
            def less_max(i):
                dve.wait_ge(b_sc.sem, b_sc[i])
                if i >= 3:
                    dve.wait_ge(b_pt.sem, b_pt[i - 3])
                s = ps[:, 0:2, :].rearrange("p o (m k) -> p (o m) k", k=P)
                nc.vector.tensor_reduce(b_max[i % 2], s, AX.X, ALU.max)
                nc.vector.drain()
                nc.vector.tensor_tensor(b_P[i % 3], s, bcast(b_max[i % 2], P), ALU.subtract).then_inc(b_sub.sem, 1)

            def sums(i):
                dve.wait_ge(b_exp.sem, b_exp[i])
                nc.vector.tensor_reduce(b_sum[i % 3], b_P[i % 3], AX.X, ALU.add)
                nc.vector.drain()
                nc.vector.reciprocal(b_sum[i % 3], b_sum[i % 3]).then_inc(b_rs.sem, 1)

            def values(g):
                for b in range(NB):
                    dve.wait_ge(b_vp.sem, b_vp[g, b])
                    nc.vector.tensor_copy(b_V[:, b, T:2 * T], bank(5)).then_inc(b_vd.sem, 1)

            values(0)
            dve_normalise(dve, L0F, 1, x_tok[1])
            for i in range(NU + 5):
                if i < NU:
                    less_max(i)
                if i == 15:
                    dve_normalise(dve, L1A, 0, x_tok[0])
                if i == 10:
                    values(1)
                if 0 <= i - 1 < NU:
                    sums(i - 1)
                if 0 <= i - 2 < NU:
                    dve.wait_ge(b_pt.sem, b_pt[i - 2])
                    nc.vector.tensor_copy(b_PT[:, 4:8, :], bank(3).rearrange("p (m q) -> p m q", m=4))\
                        .then_inc(b_ed.sem, 1)
                if i == 14:
                    dve_context_columns(dve, L1X)
                    dve_sum(dve, L1A, 0, twice=True)
            dve_context_queries(dve, L1X, 0)
            dve_sum(dve, L1A, 1, twice=True)

        def pool_l1a(pool):
            pool_context_zero(pool, L1X)
            for i in range(NU):
                pool.wait_ge(b_rs.sem, b_rs[i])
                nc.gpsimd.tensor_tensor(b_P[i % 3], b_P[i % 3], bcast(b_sum[i % 3], P), ALU.mult).then_inc(b_nm.sem, 1)
                if i == 13:
                    pool_rstd(pool, L1A, 0)
            pool_rstd(pool, L1A, 1)

        SMALL = [L1X, L2X, L3A, L3X]
        U = range(16)
        us = [(L, u) for L in SMALL for u in U]
        lg = [(L, g) for L in SMALL for g in G]
        cl = [(L, w, g) for L in (L1X, L2X, L3X) for w in "kv" for g in G]
        c_kvp = signal("c_context_kv", cl)
        c_kc = signal("c_keys_copied", lg)
        c_vc = signal("c_values_copied", lg)
        c_zero = signal("c_zeroed", lg)
        c_mask = signal("c_mask_columns", SMALL)
        c_qp = signal("c_queries", lg)
        c_qc = signal("c_queries_copied", lg)
        c_sc = signal("c_scores", us)
        c_sub = signal("c_less_max", us)
        c_exp = signal("c_exp", us)
        c_rs = signal("c_sums", us)
        c_nm = signal("c_probs", us)
        c_pt = signal("c_probs_turned", us)
        c_ea = signal("c_turned_low", us)
        c_ed = signal("c_turned_high", us)
        c_pv = signal("c_heads", us)
        c_oc = signal("c_heads_copied", lg)

        def slot(L):
            return w_even if L % 2 == 0 else w_odd

        def buffers(L):
            m = {}
            a = Carve(L % 2)
            w = Carve(0, slot(L), cols[L]["_width"])
            nk = P if L == L3A else KC
            if L == L3A:
                e = Carve(0, w_even, cols[L3X]["_width"])
                o = Carve(0)
                m["S"] = [e.take(NB * 16 * P).rearrange("p (m t) -> p m t", t=P),
                          a.take(NB * 16 * P).rearrange("p (m t) -> p m t", t=P)]
                m["v"] = [t.take(NB * 4 * P).rearrange("p (b r d) -> p b r d", b=NB, r=4) for t in (e, a)]
                m["k"] = [t.take(NB * 4 * P).rearrange("p (b r k) -> p b r k", b=NB, r=4) for t in (e, w)]
                m["q2"] = e.take(NG * T)
                m["q"] = m["oT"] = [m["q2"][:, g * T:(g + 1) * T] for g in G]
                m["Q"] = [o.take(16 * P).rearrange("p (t b h) -> p t b h", b=NG * NB, h=16) for _ in range(2)]
                m["bk"] = a.take(4)
                m["rs"] = a.take(4)
                o = Carve(0, start=4352)
                m["P"] = [o.take(8 * nk).rearrange("p (m k) -> p m k", m=8) for _ in range(3)]
            else:
                m["q"] = [a.take(T) for g in G]
                m["oT"] = m["q"]
                m["v"] = [w.take(NB * 4 * P).rearrange("p (b r d) -> p b r d", b=NB, r=4) for g in G]
                m["k"] = [a.take(NB * 4 * KC).rearrange("p (b r k) -> p b r k", b=NB, r=4) for g in G]
                m["neg"] = a.take(NG * NB * KC).rearrange("p (b k) -> p b k", k=KC)
                m["bk"] = a.take(4)
                m["P"] = [a.take(8 * nk).rearrange("p (m k) -> p m k", m=8) for _ in range(3)]
            m["PT"] = a.take(8 * P).rearrange("p (m q) -> p m q", m=8)
            m["max"] = [a.take(8) for _ in range(2)]
            m["sum"] = [a.take(8) for _ in range(3)]
            m["nk"] = nk
            return m

        CB = {L: buffers(L) for L in SMALL}
        PREV = {L1X: L1A, L2X: L2A, L3A: L2F, L3X: L3A}

        def scores_view(L, u):
            nk = CB[L]["nk"]
            return ps[:, 2 * (u % 2):2 * (u % 2) + 2, 0:4 * nk].rearrange("p o (r k) -> p o r k", k=nk)

        def pe_probs_turn(pe, L, u):
            m = CB[L]
            nk = m["nk"]
            pe.wait_ge(c_nm.sem, c_nm[L, u])
            if u:
                pe.wait_ge(c_ea.sem, c_ea[L, u - 1])
                pe.wait_ge(c_ed.sem, c_ed[L, u - 1])
            for h in range(8):
                mm = nc.tensor.transpose(ps[0:nk, 4 + h // 4, (h % 4) * P:(h % 4 + 1) * P], m["P"][u % 3][:, h, :],
                                         ident)
            mm.then_inc(c_pt.sem, 1)

        def pe_heads(pe, L, u):
            m = CB[L]
            nk = m["nk"]
            j, half = divmod(u, 2)
            g, b = divmod(j, NB)
            pe.wait_ge(c_ea.sem, c_ea[L, u])
            pe.wait_ge(c_ed.sem, c_ed[L, u])
            if u % 8 == 0:
                pe.wait_ge(c_vc.sem, c_vc[L, g])
                pe.wait_ge(c_qc.sem, c_qc[L, g])
            for i in range(2):
                c0 = 32 * (2 * half + i)
                for r in range(4):
                    mm = nc.tensor.matmul(ps[c0:c0 + 32, 6 + g, b * P:(b + 1) * P],
                                          m["v"][g][0:nk, b, r, c0:c0 + 32], m["PT"][0:nk, 4 * i + r, :],
                                          start=(r == 0), stop=(r == 3), tile_position=(0, c0))
            mm.then_inc(c_pv.sem, 1)

        def pe_project_heads(pe, L, g):
            pe.wait_ge(c_oc.sem, c_oc[L, g])
            for b in range(NB):
                mm = nc.tensor.matmul(ps[:, 6 + g, b * P:(b + 1) * P], CB[L]["oT"][g][:, b * P:(b + 1) * P],
                                      W(L, "Wo"), start=True, stop=True)
            mm.then_inc(sub_ready.sem, 1)

        def act_exp(act, L, u, scale):
            act.wait_ge(c_sub.sem, c_sub[L, u])
            p = CB[L]["P"][u % 3]
            nc.scalar.activation(p, p, ACT.Exp, scale=scale).then_inc(c_exp.sem, 1)

        def act_turned(act, L, u):
            act.wait_ge(c_pt.sem, c_pt[L, u])
            if u:
                act.wait_ge(c_pv.sem, c_pv[L, u - 1])
            nk = CB[L]["nk"]
            nc.scalar.activation(CB[L]["PT"][0:nk, 0:4, :], ps[0:nk, 4, :].rearrange("p (m q) -> p m q", m=4),
                                 ACT.Copy).then_inc(c_ea.sem, 1)

        def act_heads(act, L, g):
            act.wait_ge(c_pv.sem, c_pv[L, 8 * g + 7])
            kw = {} if L == L3X else {"bias": W(L, "bv")}
            nc.scalar.activation(CB[L]["oT"][g], bank(6 + g), ACT.Identity, **kw).then_inc(c_oc.sem, 1)

        def dve_less_max(dve, L, u):
            m = CB[L]
            dve.wait_ge(c_sc.sem, c_sc[L, u])
            if u >= 3:
                dve.wait_ge(c_pt.sem, c_pt[L, u - 3])
            p = m["P"][u % 3]
            s = scores_view(L, u)
            mx = m["max"][u % 2]
            p4 = p.rearrange("p (o r) k -> p o r k", o=2)
            if L in (L2X, L3X):
                j = u // 2
                neg = m["neg"][:, j if L == L3X else 0, :].rearrange("p (r k) -> p r k", r=1).to_broadcast([P, 4, KC])
                scale = float(np.float32(8.0) ** np.float32(0.5 if L == L3X else -0.5))
                for o in range(2):
                    nc.vector.scalar_tensor_tensor(out=p4[:, o, :, :], in0=s[:, o, :, :], scalar=scale, in1=neg,
                                                   op0=ALU.mult, op1=ALU.add)
                nc.vector.drain()
                nc.vector.tensor_reduce(mx, p, AX.X, ALU.max)
                nc.vector.drain()
                i = nc.vector.tensor_tensor(p, p, bcast(mx, m["nk"]), ALU.subtract)
            else:
                nc.vector.tensor_reduce(mx.rearrange("p (o r) -> p o r", o=2), s, AX.X, ALU.max)
                nc.vector.drain()
                i = nc.vector.tensor_tensor(p4, s, mx.rearrange("p (o r q) -> p o r q", o=2, q=1)
                                            .to_broadcast([P, 2, 4, m["nk"]]), ALU.subtract)
            i.then_inc(c_sub.sem, 1)

        def dve_sums(dve, L, u):
            m = CB[L]
            dve.wait_ge(c_exp.sem, c_exp[L, u])
            nc.vector.tensor_reduce(m["sum"][u % 3], m["P"][u % 3], AX.X, ALU.add)
            nc.vector.drain()
            nc.vector.reciprocal(m["sum"][u % 3], m["sum"][u % 3]).then_inc(c_rs.sem, 1)

        def dve_turned(dve, L, u):
            nk = CB[L]["nk"]
            dve.wait_ge(c_pt.sem, c_pt[L, u])
            if u:
                dve.wait_ge(c_pv.sem, c_pv[L, u - 1])
            nc.vector.tensor_copy(CB[L]["PT"][0:nk, 4:8, :], ps[0:nk, 5, :].rearrange("p (m q) -> p m q", m=4))\
                .then_inc(c_ed.sem, 1)

        def pool_probs(pool, L, u):
            m = CB[L]
            pool.wait_ge(c_rs.sem, c_rs[L, u])
            nc.gpsimd.tensor_tensor(m["P"][u % 3], m["P"][u % 3], bcast(m["sum"][u % 3], m["nk"]), ALU.mult)\
                .then_inc(c_nm.sem, 1)

        def pe_context_part(pe, L, w):
            for g in G:
                if w == "k":
                    if g == 0:
                        pe.wait_ge(w_loaded[L].sem, 16)
                    cs = slice(g * NB * KC, (g + 1) * NB * KC)
                    mm = nc.tensor.matmul(ps[:, g, 0:NB * KC], W(L, "Wk"), ctxT[:, cs], start=True, stop=True)
                else:
                    pe.wait_ge(c_kc.sem, c_kc[L, g])
                    for b in range(NB):
                        k0 = (g * NB + b) * KC
                        mm = nc.tensor.matmul(ps[0:KC, g, b * P:(b + 1) * P], ctxT[:, k0:k0 + KC], W(L, "Wv"),
                                              start=True, stop=True)
                mm.then_inc(c_kvp.sem, 1)

        def act_context_part(act, L, w):
            m = CB[L]
            if w == "k":
                act.wait_ge(c_mask.sem, c_mask[L])
            for g in G:
                act.wait_ge(c_kvp.sem, c_kvp[L, w, g])
                if w == "k":
                    for r in range(4):
                        kw = {} if L == L3X else {"bias": m["bk"][:, r:r + 1]}
                        i = nc.scalar.activation(m["k"][g][:, :, r, :],
                                                 ps[:, g, 0:NB * KC].rearrange("p (b k) -> p b k", b=NB),
                                                 ACT.Identity, scale=C("res4")[:, r:r + 1], **kw)
                    i.then_inc(c_kc.sem, 1)
                else:
                    act.wait_ge(c_zero.sem, c_zero[L, g])
                    act_values(g, KC, m["v"], ps[0:KC, g, :]).then_inc(c_vc.sem, 1)

        def dve_context_columns(dve, L):
            m = CB[L]
            dve.wait_ge(w_loaded[L].sem, 16)
            if L != L3X:
                nc.vector.tensor_scalar(m["bk"], C("res4"), W(L, "bk"), None, ALU.mult)
            if L == L2X:
                nc.vector.tensor_scalar(m["neg"][:, 0, :], W(L, "mask"), -1000000000.0, None, ALU.mult)
            if L == L3X:
                nc.vector.tensor_scalar(m["neg"], mask_i[:, :, :], 0.0, float(np.finfo(np.float32).min),
                                        ALU.is_equal, ALU.mult)
            nc.vector.drain().then_inc(c_mask.sem, 1)

        def pool_context_zero(pool, L):
            if L == L3X:
                pool.wait_ge(c_sc.sem, c_sc[L3A, 8])
            else:
                pool.wait_ge(layer_done.sem, layer_done[L - 2])
            for g in G:
                nc.gpsimd.memset(CB[L]["v"][g][0:KC, :, :, :], 0.0).then_inc(c_zero.sem, 1)

        def pe_context_queries(pe, L, g):
            pe_turn_state(pe, PREV[L], g)
            pe.wait_ge(xT_ready.sem, xT_ready[PREV[L], g])
            nc.tensor.matmul(bank(6 + g), W(L, "Wq"), xT[g][:, :], start=True, stop=True).then_inc(c_qp.sem, 1)

        def dve_context_queries(dve, L, g):
            dve.wait_ge(c_qp.sem, c_qp[L, g])
            if L == L3X:
                i = nc.vector.tensor_copy(CB[L]["q"][g], bank(6 + g))
            else:
                i = nc.vector.tensor_scalar(CB[L]["q"][g], bank(6 + g), W(L, "bq"), None, ALU.add)
            i.then_inc(c_qc.sem, 1)

        def pe_context(L):
            m = CB[L]

            def run(pe):
                def scores(u):
                    j, half = divmod(u, 2)
                    g, b = divmod(j, NB)
                    if u == 0:
                        pe.wait_ge(c_vc.sem, c_vc[L, 1])
                    if u % 8 == 0:
                        pe.wait_ge(c_qc.sem, c_qc[L, g])
                    if u >= 2:
                        pe.wait_ge(c_sub.sem, c_sub[L, u - 2])
                    for i in range(2):
                        r = 32 * (2 * half + i)
                        mm = nc.tensor.matmul(ps[:, 2 * (u % 2) + i, 0:4 * KC], m["q"][g][r:r + 32, b * P:(b + 1) * P],
                                              m["k"][g][r:r + 32, b, :, :], start=True, stop=True,
                                              tile_position=(r, 0))
                    mm.then_inc(c_sc.sem, 1)

                if L == L2X:
                    pe_context_queries(pe, L, 0)
                for i in range(16 + 3):
                    if i == 5:
                        pe_context_queries(pe, L, 1)
                    if i < 16:
                        scores(i)
                    if 0 <= i - 3:
                        pe_heads(pe, L, i - 3)
                    if 0 <= i - 2 < 16:
                        pe_probs_turn(pe, L, i - 2)
                    if i == 12:
                        pe_project_heads(pe, L, 0)
                    if i == 17 and L == L2X:
                        pe_l2f_route(pe, 0)
                    if i == 16 and L == L1X:
                        pe_turn_state(pe, L1X, 0)
                    if i == 17 and L == L1X:
                        pe_l1f_gate_up(pe, 0)
                if L == L1X:
                    pe_l1f_gate_up(pe, 1)
                pe_project_heads(pe, L, 1)
                nc.tensor.drain().then_inc(layer_done.sem, 1)
            return run

        def act_context(L):
            m = CB[L]
            scale = float(1.0 / np.sqrt(np.float32(8.0))) if L == L1X else 1.0

            def run(act):
                if L == L2X:
                    act_copy_state(act, L2A, 0, xT[0][:, :])
                for i in range(16 + 2):
                    if i == 5:
                        act_copy_state(act, PREV[L], 1, xT[1][:, :])
                    if i < 16:
                        act_exp(act, L, i, scale)
                    if 0 <= i - 2:
                        act_turned(act, L, i - 2)
                    if i == 11:
                        act_heads(act, L, 0)
                    if i == 17 and L == L1X:
                        act_copy_state(act, L1X, 0, xT[0][:, :])
                    if i == 17 and L == L2X:
                        act_copy_state(act, L2X, 0, xT[0][:, :])
                act_heads(act, L, 1)
                if L == L1X:
                    for n in range(2):
                        act_l1f_tanh(act, n)
                if L == L2X:
                    act_l2f_exps(act, 0)
            return run

        def dve_context(L):
            m = CB[L]

            def run(dve):
                if L == L2X:
                    dve_context_queries(dve, L, 0)
                for i in range(16 + 2):
                    if i == 6:
                        dve_context_queries(dve, L, 1)
                    if i < 16:
                        dve_less_max(dve, L, i)
                    if i == 0:
                        dve_normalise(dve, PREV[L], 1, x_tok[1])
                    if i == 14:
                        dve_normalise(dve, L, 0, x_tok[0])
                    if 0 <= i - 1 < 16:
                        dve_sums(dve, L, i - 1)
                    if 0 <= i - 2:
                        dve_turned(dve, L, i - 2)
                    if i == 13:
                        dve_sum(dve, L, 0)
                    if i == 15 and L == L1X:
                        dve_l1f_scales(dve)
                if L == L2X:
                    dve_l2f_less_max(dve, 0)
                    dve_l2f_weights(dve, 0)
                dve_sum(dve, L, 1)
                if L == L3X:
                    dve_normalise(dve, L, 1, x_tok[1])
            return run

        def pool_context(L):
            m = CB[L]

            def run(pool):
                if L != L3X:
                    pool_add_bias(pool, L, PREV[L], 0, W(L, "bo"))
                for u in U:
                    if u == 7 and L != L3X:
                        pool_add_bias(pool, L, PREV[L], 1, W(L, "bo"))
                    pool_probs(pool, L, u)
                    if u == 12:
                        pool_rstd(pool, L, 0)
                pool_rstd(pool, L, 1)
            return run

        c = Carve(1)
        g_h = [c.take(4 * T).rearrange("p (c t) -> p c t", c=4) for g in G]
        g_y = [c.take(4 * T).rearrange("p (c t) -> p c t", c=4) for g in G]
        g_th = [c.take(T) for _ in range(2)]
        g_t = c.take(T)
        g_sT = [c.take(T) for g in G]
        g_s1h = c.take(4)
        g_s12 = c.take(4)

        GC = [(g, c) for g in G for c in range(4)]
        g_const = signal("g_scales", [0])
        g_gu = signal("g_gate_up", GC)
        g_tanh = signal("g_tanh", GC)
        g_in = signal("g_gated", GC)
        g_mm = signal("g_hidden_products", [(s, g, c) for s in range(2) for (g, c) in GC])
        g_gelu = signal("g_gelu", [(s, g, c) for s in range(2) for (g, c) in GC])
        g_acc = signal("g_result", list(G))
        g_copied = signal("g_result_copied", list(G))

        def pe_l1f_gate_up(pe, i):
            g, c = GC[i]
            if i == 0:
                pe.wait_ge(w_loaded[L1F].sem, 16)
                pe.wait_ge(c_sub.sem, c_sub[L1X, 15])
            if c == 0:
                pe.wait_ge(xT_ready.sem, xT_ready[L1X, g])
            if i >= 2:
                pe.wait_ge(g_in.sem, i - 1)
            for k, w in ((0, "w1"), (2, "w2")):
                mm = nc.tensor.matmul(bank(k + i % 2), W(L1F, w)[:, c * P:(c + 1) * P], xT[g][:, :],
                                      start=True, stop=True)
            mm.then_inc(g_gu.sem, 1)

        def pe_l1f(pe):
            for i, (g, c) in enumerate(GC):
                if i >= 2:
                    if c == 0:
                        pe_turn_state(pe, L1X, g)
                    pe_l1f_gate_up(pe, i)
            for s, (w, src) in enumerate((("h1", g_h), ("h2", g_y))):
                for i, (g, c) in enumerate(GC):
                    n = 8 * s + i
                    if c == 0 and s == 0:
                        pe.wait_ge(g_in.sem, g_in[g, 3])
                    elif c == 0:
                        pe.wait_ge(g_gelu.sem, g_gelu[s - 1, g, 3])
                    if n >= 2:
                        pe.wait_ge(g_gelu.sem, n - 1)
                    for k in range(4):
                        mm = nc.tensor.matmul(bank(4 + n % 2), W(L1F, w)[:, k * T + c * P:k * T + (c + 1) * P],
                                              src[g][:, k, :], start=(k == 0), stop=(k == 3))
                    mm.then_inc(g_mm.sem, 1)
            for g in G:
                pe.wait_ge(g_gelu.sem, g_gelu[1, g, 3])
                for k in range(4):
                    mm = nc.tensor.matmul(bank(6 + g), W(L1F, "w3")[:, k * P:(k + 1) * P], g_h[g][:, k, :],
                                          start=(k == 0), stop=(k == 3))
                mm.then_inc(g_acc.sem, 1)
            for g in G:
                pe_turn_result(pe, L1F, g, g_copied, g_sT)
            nc.tensor.drain().then_inc(layer_done.sem, 1)

        def act_l1f_tanh(act, i):
            g, c = GC[i]
            if i == 0:
                act.wait_ge(g_const.sem, 1)
            act.wait_ge(g_gu.sem, g_gu[g, c])
            if i >= 2:
                act.wait_ge(g_in.sem, i - 1)
            nc.scalar.activation(g_th[i % 2], bank(i % 2), ACT.Tanh, scale=g_s1h[:, c:c + 1]).then_inc(g_tanh.sem, 1)

        def act_l1f(act):
            for i, (g, c) in enumerate(GC):
                if i >= 2:
                    if c == 0:
                        act_copy_state(act, L1X, g, xT[g][:, :])
                    act_l1f_tanh(act, i)
            for s, (w, dst) in enumerate((("h1", g_y), ("h2", g_h))):
                for g, c in GC:
                    act.wait_ge(g_mm.sem, g_mm[s, g, c])
                    nc.scalar.activation(dst[g][:, c, :], bank(4 + c % 2), ACT.Gelu, scale=W(L1F, w + "s")[:, c:c + 1])\
                        .then_inc(g_gelu.sem, 1)
            for g in G:
                act.wait_ge(g_acc.sem, g_acc[g])
                nc.scalar.activation(g_sT[g], bank(6 + g), ACT.Identity, scale=W(L1F, "w3s")).then_inc(g_copied.sem, 1)

        def dve_l1f_scales(dve):
            dve.wait_ge(w_loaded[L1F].sem, 16)
            nc.vector.tensor_scalar(g_s1h, W(L1F, "w1s"), 0.5, None, ALU.mult)
            nc.vector.drain()
            nc.vector.tensor_tensor(g_s12, g_s1h, W(L1F, "w2s"), ALU.mult)
            nc.vector.drain().then_inc(g_const.sem, 1)

        def dve_l1f(dve):
            for i, (g, c) in enumerate(GC):
                dve.wait_ge(g_tanh.sem, g_tanh[g, c])
                nc.vector.scalar_tensor_tensor(out=g_t, in0=g_th[i % 2], scalar=1.0, in1=bank(i % 2),
                                               op0=ALU.add, op1=ALU.mult)
                nc.vector.drain()
                nc.vector.scalar_tensor_tensor(out=g_h[g][:, c, :], in0=g_t, scalar=g_s12[:, c:c + 1],
                                               in1=bank(2 + i % 2), op0=ALU.mult, op1=ALU.mult).then_inc(g_in.sem, 1)
                nc.vector.drain()
                if i == 1:
                    dve_normalise(dve, L1X, 1, x_tok[1])
            for g in G:
                dve_norm(dve, L1F, g)

        def pool_l1f(pool):
            for g in G:
                pool_rstd(pool, L1F, g)

        c = Carve(0)
        d_q = [c.take(T) for g in G]
        d_kv = [c.take(NB * 2 * P).rearrange("p (b w d) -> p b w d", b=NB, w=2) for g in G]
        d_e = [c.take(T) for g in G]
        d_f = [c.take(T) for g in G]
        d_KV = [c.take(T) for g in G]
        d_oT = [c.take(T) for g in G]

        d_pr = signal("d_projected", [(w, g) for g in G for w in ("q", "kv")])
        d_min = signal("d_min", [(w, g) for g in G for w in "qk"])
        d_exp = signal("d_exp", [(w, g) for g in G for w in "qk"])
        d_feat = signal("d_features", list(G))
        d_kvp = signal("d_kv_products", list(G))
        d_blk = signal("d_kv_blocks", list(G))
        d_op = signal("d_heads", list(G))
        d_oc = signal("d_heads_copied", list(G))

        def pe_l2a(pe):
            pe.wait_ge(w_loaded[L2A].sem, 16)
            for g in G:
                pe_turn_state(pe, L1F, g)
                pe.wait_ge(xT_ready.sem, xT_ready[L1F, g])
                nc.tensor.matmul(bank(3 * g), W(L2A, "Wq"), xT[g][:, :], start=True, stop=True).then_inc(d_pr.sem, 1)
                for b in range(NB):
                    mm = nc.tensor.matmul(ps[:, 3 * g + 1 + b // 2, (b % 2) * 256:(b % 2) * 256 + 256],
                                          xT[g][:, b * P:(b + 1) * P], W(L2A, "Wkv"), start=True, stop=True)
                mm.then_inc(d_pr.sem, 1)
            for g in G:
                pe.wait_ge(d_feat.sem, d_feat[g])
                for b in range(NB):
                    mm = nc.tensor.matmul(ps[:, 3 * g, b * P:(b + 1) * P], d_kv[g][:, b, 0, :], d_kv[g][:, b, 1, :],
                                          start=True, stop=True)
                mm.then_inc(d_kvp.sem, 1)
            for g in G:
                pe.wait_ge(d_blk.sem, d_blk[g])
                for b in range(NB):
                    mm = nc.tensor.matmul(ps[:, 3 * g + 1, b * P:(b + 1) * P], d_KV[g][:, b * P:(b + 1) * P],
                                          d_q[g][:, b * P:(b + 1) * P], start=True, stop=True)
                mm.then_inc(d_op.sem, 1)
            pe.wait_ge(d_oc.sem, d_oc[0])
            pe_context_part(pe, L2X, "k")
            for g in G:
                pe.wait_ge(d_oc.sem, d_oc[g])
                for b in range(NB):
                    mm = nc.tensor.matmul(ps[:, 6 + g, b * P:(b + 1) * P], d_oT[g][:, b * P:(b + 1) * P],
                                          W(L2A, "Wo"), start=True, stop=True)
                mm.then_inc(sub_ready.sem, 1)
            pe_context_part(pe, L2X, "v")
            nc.tensor.drain().then_inc(layer_done.sem, 1)

        def act_l2a(act):
            for g in G:
                act_copy_state(act, L1F, g, xT[g][:, :])
            for g in G:
                for w, buf in (("q", d_e[g]), ("k", d_f[g])):
                    act.wait_ge(d_min.sem, d_min[w, g])
                    nc.scalar.activation(buf, buf, ACT.Exp).then_inc(d_exp.sem, 1)
            for g in G:
                act.wait_ge(d_op.sem, d_op[g])
                nc.scalar.activation(d_oT[g], bank(3 * g + 1), ACT.Copy).then_inc(d_oc.sem, 1)
            for w in "kv":
                act_context_part(act, L2X, w)

        def dve_l2a(dve):
            dve.wait_ge(w_loaded[L2A].sem, 16)
            for g in G:
                dve.wait_ge(d_pr.sem, d_pr["q", g])
                nc.vector.tensor_scalar(d_q[g], bank(3 * g), W(L2A, "bq"), None, ALU.add)
                nc.vector.drain()
                nc.vector.tensor_scalar(d_e[g], d_q[g], 0.0, None, ALU.min).then_inc(d_min.sem, 1)
                dve.wait_ge(d_pr.sem, d_pr["kv", g])
                kv = ps[:, 3 * g + 1:3 * g + 3, :].rearrange("p o (b n) -> p (o b) n", b=2)
                bkv = W(L2A, "bkv").rearrange("p (o n) -> p o n", o=1).to_broadcast([P, NB, 2 * P])
                nc.vector.tensor_tensor(d_kv[g].rearrange("p b w d -> p b (w d)"), kv, bkv, ALU.add)
                nc.vector.drain()
                nc.vector.tensor_scalar(d_f[g].rearrange("p (b d) -> p b d", b=NB), d_kv[g][:, :, 0, :], 0.0, None,
                                        ALU.min).then_inc(d_min.sem, 1)
            for g in G:
                dve.wait_ge(d_exp.sem, d_exp["k", g])
                nc.vector.scalar_tensor_tensor(out=d_q[g], in0=d_q[g], scalar=0.0, in1=d_e[g], op0=ALU.max, op1=ALU.add)
                nc.vector.scalar_tensor_tensor(out=d_kv[g][:, :, 0, :], in0=d_kv[g][:, :, 0, :], scalar=0.0,
                                               in1=d_f[g].rearrange("p (b d) -> p b d", b=NB),
                                               op0=ALU.max, op1=ALU.add).then_inc(d_feat.sem, 1)
            for g in G:
                dve.wait_ge(d_kvp.sem, d_kvp[g])
                blk = C("block8").rearrange("p (o d) -> p o d", o=1).to_broadcast([P, NB, P])
                nc.vector.tensor_tensor(d_KV[g].rearrange("p (b d) -> p b d", b=NB),
                                        bank(3 * g).rearrange("p (b d) -> p b d", b=NB), blk, ALU.mult)\
                    .then_inc(d_blk.sem, 1)
            dve_context_columns(dve, L2X)
            dve_norm(dve, L2A, 0)
            dve_sum(dve, L2A, 1)

        def pool_l2a(pool):
            pool_context_zero(pool, L2X)
            for g in G:
                pool_add_bias(pool, L2A, L1F, g, W(L2A, "bo"))
            for g in G:
                pool_rstd(pool, L2A, g)

        c = Carve(0)
        e_lg = [c.take(NB * 8).rearrange("p (b e) -> p b e", b=NB) for g in G]
        e_top = [c.take(NB * 8).rearrange("p (b e) -> p b e", b=NB) for g in G]
        e_idx = [c.take(NB * 8).bitcast(U32).rearrange("p (b e) -> p b e", b=NB) for g in G]
        e_idf = [c.take(NB * 8).rearrange("p (b e) -> p b e", b=NB) for g in G]
        e_sel = [c.take(NB * 16).rearrange("p (s b e) -> p s b e", s=2, b=NB) for g in G]
        e_m = [c.take(NB) for g in G]
        e_w3 = [c.take(NB * 12).bitcast(BF16).rearrange("p (b s e) -> p b s e", b=NB, s=3) for g in G]
        e_wT3 = [c.take(T // 2, 24).bitcast(BF16) for g in G]
        e_xw = [c.take(T) for _ in range(2)]
        e_sg = [c.take(T) for _ in range(2)]
        e_h = [c.take(T) for _ in range(2)]
        e_sT = [c.take(T) for g in G]

        EC = [(g, n) for g in G for n in range(36)]
        EX = [(g, e) for g in G for e in range(8)]
        e_route = signal("e_logits", list(G))
        e_sub = signal("e_logits_less_max", list(G))
        e_exp = signal("e_exp", list(G))
        e_split = signal("e_weights_split", list(G))
        e_turn = signal("e_weights_turned", list(G))
        e_wc = signal("e_weights_copied", list(G))
        e_sp = signal("e_weights_spread", EX)
        e_xs = signal("e_state_weighted", EX)
        e_gu = signal("e_gate_up", EC)
        e_silu = signal("e_silu", EC)
        e_hid = signal("e_hidden", EC)
        e_down = signal("e_down", EC)
        e_copied = signal("e_result_copied", list(G))

        def top_two(lg, top, idx, idf, sel):
            for b in range(NB):
                nc.vector.max(top[:, b, :], lg[:, b, :])
            nc.vector.drain()
            for b in range(NB):
                nc.vector.max_index(idx[:, b, :], top[:, b, :], lg[:, b, :])
            nc.vector.drain()
            nc.vector.tensor_copy(idf, idx)
            nc.vector.drain()
            iota = C("iota8").rearrange("p (o e) -> p o e", o=1).to_broadcast([P, NB, 8])
            for k in range(2):
                i = nc.vector.tensor_tensor(sel[:, k, :, :], idf[:, :, k:k + 1].to_broadcast([P, NB, 8]), iota,
                                            ALU.is_equal)
            nc.vector.drain()
            return i

        def pe_l2f_route(pe, g):
            if g == 0:
                pe.wait_ge(w_loaded[L2F].sem, 16)
            pe_turn_state(pe, L2X, g)
            pe.wait_ge(xT_ready.sem, xT_ready[L2X, g])
            if g:
                pe.wait_ge(e_xs.sem, e_xs[0, 0])
            for b in range(NB):
                mm = nc.tensor.matmul(ps[:, 6 - g, 8 * b:8 * b + 8], xT[g][:, b * P:(b + 1) * P], W(L2F, "gate"),
                                      start=True, stop=True)
            mm.then_inc(e_route.sem, 1)

        def pe_l2f(pe):
            def turn_weights(g):
                pe.wait_ge(e_split.sem, e_split[g])
                for b in range(NB):
                    mm = nc.tensor.transpose(bank(5)[0:24, 0:T // 2].bitcast(BF16)[:, b * P:(b + 1) * P],
                                             e_w3[g][:, b, :, :].rearrange("p s e -> p (s e)"), ident_bf[:, :])
                mm.then_inc(e_turn.sem, 1)

            def spread(g, e):
                if e == 0:
                    pe.wait_ge(e_wc.sem, e_wc[g])
                if (g, e) > (0, 0):
                    pe.wait_ge(e_xs.sem, e_xs[g, e] - 1)
                nc.tensor.matmul(bank(4), expand8[:, e * P:(e + 1) * P], e_wT3[g], start=True, stop=True)\
                    .then_inc(e_sp.sem, 1)

            def gate_up(i):
                g, n = EC[i]
                if i >= 2:
                    pe.wait_ge(e_hid.sem, i - 1)
                if n < 32:
                    w1, w3 = W(L2F, "w1")[:, n * P:(n + 1) * P], W(L2F, "w3")[:, n * P:(n + 1) * P]
                    x3 = e_xw[(n // 4) % 2]
                    if n % 4 == 0:
                        pe.wait_ge(e_xs.sem, e_xs[g, n // 4])
                else:
                    m = n - 32
                    w1, w3 = W(L2F, "w1s")[:, m * P:(m + 1) * P], W(L2F, "w3s")[:, m * P:(m + 1) * P]
                    x3 = xT[g][:, :]
                nc.tensor.matmul(bank(i % 2), w1, xT[g][:, :], start=True, stop=True)
                nc.tensor.matmul(bank(2 + i % 2), w3, x3, start=True, stop=True).then_inc(e_gu.sem, 1)

            def down(i):
                g, n = EC[i]
                pe.wait_ge(e_hid.sem, i + 1)
                w = W(L2F, "w2")[:, n * P:(n + 1) * P] if n < 32 else W(L2F, "w2s")[:, (n - 32) * P:(n - 31) * P]
                nc.tensor.matmul(bank(6 + g), w, e_h[i % 2], start=(n == 0), stop=(n == 35)).then_inc(e_down.sem, 1)

            turn_weights(0)
            spread(0, 0)
            for i, (g, n) in enumerate(EC):
                gate_up(i)
                if i >= 1:
                    down(i - 1)
                if n < 32 and n % 4 == 1 and n // 4 + 1 < 8:
                    spread(g, n // 4 + 1)
                if i == 8:
                    pe_l2f_route(pe, 1)
                if i == 30:
                    turn_weights(1)
                if i == 34:
                    spread(1, 0)
                if i == 39:
                    pe_turn_result(pe, L2F, 0, e_copied, e_sT)
            down(len(EC) - 1)
            pe_turn_result(pe, L2F, 1, e_copied, e_sT)
            nc.tensor.drain().then_inc(layer_done.sem, 1)

        def act_l2f_exps(act, g):
            act.wait_ge(e_sub.sem, e_sub[g])
            nc.scalar.activation(e_lg[g], e_lg[g], ACT.Exp).then_inc(e_exp.sem, 1)

        def act_l2f(act):
            def weights(g):
                act.wait_ge(e_turn.sem, e_turn[g])
                nc.scalar.activation(e_wT3[g], bank(5)[0:24, 0:T // 2].bitcast(BF16), ACT.Copy).then_inc(e_wc.sem, 1)

            def result(g):
                act.wait_ge(e_down.sem, e_down[g, 35])
                nc.scalar.activation(e_sT[g], bank(6 + g), ACT.Copy).then_inc(e_copied.sem, 1)

            weights(0)
            for i, (g, n) in enumerate(EC):
                if i == 9:
                    act_copy_state(act, L2X, 1, xT[1][:, :])
                if i == 14:
                    act_l2f_exps(act, 1)
                if i == 32:
                    weights(1)
                act.wait_ge(e_gu.sem, e_gu[g, n])
                if i >= 2:
                    act.wait_ge(e_hid.sem, i - 1)
                nc.scalar.activation(e_sg[i % 2], bank(i % 2), ACT.Silu).then_inc(e_silu.sem, 1)
                if i == 37:
                    result(0)
            result(1)

        def dve_l2f_less_max(dve, g):
            dve.wait_ge(e_route.sem, e_route[g])
            lgp = ps[:, 6 - g, 0:32].rearrange("p (b e) -> p b e", b=NB)
            nc.vector.tensor_reduce(e_m[g], lgp, AX.X, ALU.max)
            nc.vector.drain()
            nc.vector.tensor_tensor(e_lg[g], lgp, bcast(e_m[g], 8), ALU.subtract).then_inc(e_sub.sem, 1)

        def dve_l2f_weights(dve, g):
            dve.wait_ge(e_exp.sem, e_exp[g])
            nc.vector.tensor_reduce(e_m[g], e_lg[g], AX.X, ALU.add)
            nc.vector.drain()
            nc.vector.reciprocal(e_m[g], e_m[g])
            nc.vector.drain()
            nc.vector.tensor_tensor(e_lg[g], e_lg[g], bcast(e_m[g], 8), ALU.mult)
            nc.vector.drain()
            top_two(e_lg[g], e_top[g], e_idx[g], e_idf[g], e_sel[g])
            nc.vector.tensor_tensor(e_sel[g][:, 0, :, :], e_sel[g][:, 0, :, :], e_sel[g][:, 1, :, :], ALU.add)
            nc.vector.drain()
            nc.vector.scalar_tensor_tensor(out=e_lg[g], in0=e_lg[g], scalar=0.5, in1=e_sel[g][:, 0, :, :],
                                           op0=ALU.mult, op1=ALU.mult)
            nc.vector.drain()
            split3(e_lg[g], e_w3[g]).then_inc(e_split.sem, 1)

        def dve_l2f(dve):
            def weighted(g, e):
                dve.wait_ge(e_sp.sem, e_sp[g, e])
                if (g, e) >= (0, 2):
                    k = EX.index((g, e)) - 2
                    g2, e2 = EX[k]
                    dve.wait_ge(e_gu.sem, e_gu[g2, 4 * e2 + 3])
                nc.vector.tensor_tensor(e_xw[e % 2], bank(4), xT[g][:, :], ALU.mult).then_inc(e_xs.sem, 1)

            weighted(0, 0)
            dve_normalise(dve, L2X, 1, x_tok[1])
            for i, (g, n) in enumerate(EC):
                if i == 12:
                    dve_l2f_less_max(dve, 1)
                if i == 18:
                    dve_l2f_weights(dve, 1)
                dve.wait_ge(e_silu.sem, e_silu[g, n])
                if i >= 2:
                    dve.wait_ge(e_down.sem, i - 1)
                if n < 32:
                    j = nc.vector.tensor_tensor(e_h[i % 2], bank(2 + i % 2), e_sg[i % 2], ALU.mult)
                else:
                    j = nc.vector.scalar_tensor_tensor(out=e_h[i % 2], in0=bank(2 + i % 2), scalar=0.0625,
                                                       in1=e_sg[i % 2], op0=ALU.mult, op1=ALU.mult)
                j.then_inc(e_hid.sem, 1)
                if n < 32 and n % 4 == 1 and n // 4 + 1 < 8:
                    weighted(g, n // 4 + 1)
                if i == 34:
                    weighted(1, 0)
                if i == 40:
                    dve_sum(dve, L2F, 0)
                if i == 41:
                    dve_normalise(dve, L2F, 0, x_tok[0])
            dve_norm(dve, L2F, 1)

        def pool_l2f(pool):
            for g in G:
                pool_rstd(pool, L2F, g)

        R = CB[L3A]
        RB = 32
        r_q = signal("r_queries_spread", range(8))
        r_mm = signal("r_position_terms", range(RB))
        r_ea = signal("r_terms_low", range(RB // 2))
        r_ed = signal("r_terms_high", range(RB // 2))
        r_k = signal("r_keys", list(G))
        r_v = signal("r_values", list(G))

        def pe_l3a(pe):
            pe.wait_ge(w_loaded[L3A].sem, 16)
            for g in G:
                pe_turn_state(pe, L2F, g)
                pe.wait_ge(xT_ready.sem, xT_ready[L2F, g])
                nc.tensor.matmul(bank(6 + g), W(L3A, "Wq"), xT[g][:, :], start=True, stop=True).then_inc(c_qp.sem, 1)
                nc.tensor.matmul(bank(4 + g), W(L3A, "Wk"), xT[g][:, :], start=True, stop=True).then_inc(r_k.sem, 1)
            for g in G:
                pe.wait_ge(c_qc.sem, c_qc[L3A, g])
                for b in range(NB):
                    mm = nc.tensor.matmul(ps[:, 6 + g, b * P:(b + 1) * P], xT[g][:, b * P:(b + 1) * P], W(L3A, "Wv"),
                                          start=True, stop=True)
                mm.then_inc(r_v.sem, 1)
            for n in range(RB):
                if n % 4 == 0:
                    pe.wait_ge(r_q.sem, r_q[n // 4])
                if n >= 4:
                    s, e = (r_ea, 2 * ((n - 4) // 4) + n % 4) if n % 4 < 2 else (r_ed, 2 * ((n - 4) // 4) + n % 4 - 2)
                    pe.wait_ge(s.sem, s[e])
                for t in range(4 * n, 4 * n + 4):
                    mm = nc.tensor.matmul(ps[:, n % 4, (t % 4) * P:(t % 4 + 1) * P],
                                          W(L3A, "rel")[:, 255 - t:255 - t + P],
                                          R["Q"][(n // 4) % 2][:, t % 16, :, :].rearrange("p b h -> p (b h)"),
                                          start=True, stop=True)
                mm.then_inc(r_mm.sem, 1)

            def scores(u):
                j, half = divmod(u, 2)
                g, b = divmod(j, NB)
                if u == 0:
                    pe.wait_ge(r_ea.sem, RB // 2)
                    pe.wait_ge(r_ed.sem, RB // 2)
                    pe.wait_ge(c_kc.sem, c_kc[L3A, 1])
                if u >= 2:
                    pe.wait_ge(c_sub.sem, c_sub[L3A, u - 2])
                for i in range(2):
                    out = bank(2 * (u % 2) + i)
                    for r in range(4):
                        nc.tensor.matmul(out[:, r * P:(r + 1) * P], R["S"][g][:, 16 * b + 8 * half + 4 * i + r, :],
                                         ident,
                                         is_transpose=True, start=(r == 0), stop=False, skip_group_check=True)
                    p = 32 * (2 * half + i)
                    mm = nc.tensor.matmul(out, R["q"][g][p:p + 32, b * P:(b + 1) * P], R["k"][g][p:p + 32, b, :, :],
                                          start=False, stop=True, tile_position=(p, 0), skip_group_check=True)
                mm.then_inc(c_sc.sem, 1)

            for i in range(16 + 3):
                if i < 16:
                    scores(i)
                if 0 <= i - 3:
                    pe_heads(pe, L3A, i - 3)
                if 0 <= i - 2 < 16:
                    pe_probs_turn(pe, L3A, i - 2)
                if i == 12:
                    pe_project_heads(pe, L3A, 0)
                if i == 16:
                    pe.wait_ge(c_sub.sem, c_sub[L3A, 15])
                    pe_context_part(pe, L3X, "k")
                if i == 17:
                    pe_context_queries(pe, L3X, 0)
                    pe_context_part(pe, L3X, "v")
            pe_project_heads(pe, L3A, 1)
            nc.tensor.drain().then_inc(layer_done.sem, 1)

        def r_bank(n, g):
            return ps[:, n % 4, :].rearrange("p (t g m) -> p g t m", g=NG, t=4)[:, g, :, :]

        def r_dst(n, g):
            return R["S"][g][:, :, 4 * n:4 * n + 4].rearrange("p m t -> p t m")

        def act_l3a(act):
            for g in G:
                act_copy_state(act, L2F, g, xT[g][:, :])
            act.wait_ge(c_mask.sem, c_mask[L3A])
            for g in G:
                act.wait_ge(r_k.sem, r_k[g])
                for r in range(4):
                    i = nc.scalar.activation(R["k"][g][:, :, r, :], bank(4 + g).rearrange("p (b k) -> p b k", b=NB),
                                             ACT.Identity, scale=R["rs"][:, r:r + 1], bias=R["bk"][:, r:r + 1])
                i.then_inc(c_kc.sem, 1)
            for g in G:
                act.wait_ge(r_v.sem, r_v[g])
                act.wait_ge(c_zero.sem, c_zero[L3A, g])
                act_values(g, P, R["v"], bank(6 + g)).then_inc(c_vc.sem, 1)
            for n in range(RB):
                if n % 4 < 2:
                    act.wait_ge(r_mm.sem, r_mm[n])
                    for g in G:
                        i = nc.scalar.activation(r_dst(n, g), r_bank(n, g), ACT.Copy)
                    i.then_inc(r_ea.sem, 1)
            for i in range(16 + 2):
                if i < 16:
                    act_exp(act, L3A, i, 1.0)
                if 0 <= i - 2:
                    act_turned(act, L3A, i - 2)
                if i == 11:
                    act_heads(act, L3A, 0)
                if i == 17:
                    act_context_part(act, L3X, "k")
                    act_copy_state(act, L3A, 0, xT[0][:, :])
            act_heads(act, L3A, 1)
            act_context_part(act, L3X, "v")

        def dve_l3a(dve):
            dve.wait_ge(w_loaded[L3A].sem, 16)
            rs8 = float(1.0 / np.sqrt(np.float32(8.0)))
            nc.vector.tensor_scalar(R["rs"], C("res4"), rs8, None, ALU.mult)
            nc.vector.drain()
            nc.vector.tensor_scalar(R["bk"], R["rs"], W(L3A, "bk"), None, ALU.mult).then_inc(c_mask.sem, 1)
            for g in G:
                dve.wait_ge(c_qp.sem, c_qp[L3A, g])
                nc.vector.tensor_scalar(R["q"][g], bank(6 + g), W(L3A, "bq"), None, ALU.add).then_inc(c_qc.sem, 1)
            nc.vector.drain()

            def spread(c):
                if c >= 2:
                    dve.wait_ge(r_mm.sem, r_mm[4 * (c - 2) + 3])
                q = R["q2"].rearrange("p (b t) -> p t b", b=NG * NB)[:, 16 * c:16 * c + 16, :]
                msk = C("head8").rearrange("p (t b h) -> p t b h", t=1, b=1).to_broadcast([P, 16, NG * NB, 16])
                nc.vector.tensor_tensor(R["Q"][c % 2], q.rearrange("p t (b o) -> p t b o", o=1)
                                        .to_broadcast([P, 16, NG * NB, 16]), msk, ALU.mult).then_inc(r_q.sem, 1)

            spread(0)
            spread(1)
            for c in range(8):
                for n in (4 * c + 2, 4 * c + 3):
                    dve.wait_ge(r_mm.sem, r_mm[n])
                    for g in G:
                        i = nc.vector.tensor_copy(r_dst(n, g), r_bank(n, g))
                    i.then_inc(r_ed.sem, 1)
                if c + 2 < 8:
                    spread(c + 2)
            for i in range(16 + 2):
                if i < 16:
                    dve_less_max(dve, L3A, i)
                if i == 14:
                    dve_normalise(dve, L3A, 0, x_tok[0])
                if 0 <= i - 1 < 16:
                    dve_sums(dve, L3A, i - 1)
                if 0 <= i - 2:
                    dve_turned(dve, L3A, i - 2)
                if i == 12:
                    dve_context_columns(dve, L3X)
                if i == 13:
                    dve_sum(dve, L3A, 0)
            dve_context_queries(dve, L3X, 0)
            dve_sum(dve, L3A, 1)

        def pool_l3a(pool):
            pool.wait_ge(layer_done.sem, layer_done[L2F])
            for g in G:
                nc.gpsimd.memset(R["v"][g], 0.0).then_inc(c_zero.sem, 1)
            for g in G:
                pool_add_bias(pool, L3A, L2F, g, W(L3A, "bo"))
            for u in U:
                pool_probs(pool, L3A, u)
                if u == 10:
                    pool_context_zero(pool, L3X)
                if u == 12:
                    pool_rstd(pool, L3A, 0)
            pool_rstd(pool, L3A, 1)

        ST = [(0, 0), (1, 0), (0, 1), (1, 1)]
        c = Carve(1)
        i_lg = [c.take(NB * 8).rearrange("p (b e) -> p b e", b=NB) for g in G]
        i_top = [c.take(NB * 8).rearrange("p (b e) -> p b e", b=NB) for g in G]
        i_idx = [c.take(NB * 8).bitcast(U32).rearrange("p (b e) -> p b e", b=NB) for g in G]
        i_idf = [c.take(NB * 8).rearrange("p (b e) -> p b e", b=NB) for g in G]
        i_one = [c.take(NB * 16).rearrange("p (s b e) -> p s b e", s=2, b=NB) for g in G]
        i_m = [c.take(NB) for g in G]
        i_s3 = [[c.take(NB * 12).bitcast(BF16).rearrange("p (b s e) -> p b s e", b=NB, s=3) for _ in range(3)]
                for g in G]
        i_sT = [[c.take(T // 2, 24).bitcast(BF16) for _ in range(3)] for g in G]
        i_mix = c.take(2)
        i_hb = c.take(1)
        i_iwb = c.take(1)
        i_b2 = c.take(3 * 384 // 2, 24).bitcast(BF16).rearrange("p (s d) -> p s d", s=3)
        i_b2f = c.take(384, 24)
        i_b2x = c.take(384 // 2, 24).bitcast(BF16)
        i_rh = [c.take(T, 32) for g in G]
        i_sh = [c.take(T, 65) for g in G]
        i_hh = [c.take(T, 32) for g in G]
        i_mb = [[c.take(T // 2).bitcast(BF16) for _ in range(8)] for g in G]
        i_th = [c.take(T) for g in G]
        c = Carve(0, w_even)
        i_h = [[c.take(T) for _ in range(4)] for g in G]
        i_hm = [[c.take(T) for _ in range(8)] for g in G]
        i_w = [[c.take(T) for _ in range(2)] for g in [0]] + [None]
        c = Carve(0)
        i_w[1] = [c.take(T) for _ in range(2)]
        i_ta = [c.take(T) for _ in range(2)]
        i_tg = [c.take(T) for _ in range(2)]
        i_sp = [c.take(T) for _ in range(2)]
        i_Y = [c.take(T) for _ in range(2)]
        i_U = [c.take(T) for _ in range(2)]
        i_X = [c.take(T) for g in G]
        i_V = [c.take(T) for g in G]
        i_d = [c.take(T) for g in G]
        i_res = [i_hm[g][0] for g in G]
        c = Carve(0, w_odd, cols[L3F]["_width"])
        i_v = [c.take(T) for g in G]

        def hidden_items(s):
            return [("hidden", s, p) for p in range(6)]
        ITEMS = ([("router", 0), ("router", 1)] + hidden_items(0) + hidden_items(1) + [("halt", 0), ("halt", 1)]
                 + [i for g in G for i in [("turned", g, k) for k in range(3)] + [("spread", g, k) for k in range(10)]]
                 + hidden_items(2) + [("halt", 2)] + hidden_items(3) + [("halt", 3)]
                 + [("refine", 0, k) for k in range(3)] + [("refine", 1, k) for k in range(3)])
        i_logit = signal("i_logits", list(G))
        i_staged = signal("i_products_staged", ITEMS)
        i_taken = signal("i_staged_taken", ITEMS)
        GATES = [(q, m) for q in range(12) for m in ((1, 2, 0) if q >= 6 else (1, 2))]
        i_ctl = signal("i_gate_products", GATES)
        i_act = signal("i_gate_functions", GATES)
        i_read = signal("i_gate_banks_read", range(12))
        i_term = signal("i_terms", range(12))
        i_sum = signal("i_terms_added", [(s, j) for s in range(4) for j in (1, 2)])
        i_less = signal("i_logits_less_max", list(G))
        i_exp = signal("i_exp", list(G))
        i_sel = signal("i_selected", list(G))
        i_new = signal("i_new_state", range(4))
        i_msk = signal("i_hidden_masked", [(s, k, p) for s in range(4) for k in range(2) for p in range(4)])

        def staged_bank(item):
            return 6 + (i_staged[item] - 1) % 2

        def pe_l3f(pe):
            pe.wait_ge(w_loaded[L3F].sem, 16)

            def free(item):
                if i_staged[item] > 2:
                    pe.wait_ge(i_taken.sem, i_staged[item] - 2)
                return bank(staged_bank(item))

            def hidden(s):
                g, it = ST[s]
                if it:
                    pe.wait_ge(i_new.sem, i_new[s - 2])
                for p in range(6):
                    o = free(("hidden", s, p))
                    if p < 4:
                        w = [W(L3F, "ew1")[:, n * T + p * P:n * T + (p + 1) * P] for n in range(2)]
                        n = P
                    elif p == 4:
                        w, n = [W(L3F, "sw1")[:, n * 64:(n + 1) * 64] for n in range(2)], 64
                    else:
                        w, n = [W(L3F, "hw1")], 32
                    o = o[0:n, :]
                    both = it == 1 and p < 5
                    mm = nc.tensor.matmul(o, w[0], xT[g][:, :], start=True, stop=not both)
                    if both:
                        mm = nc.tensor.matmul(o, w[1], i_v[g], start=False, stop=True)
                    mm.then_inc(i_staged.sem, 1)

            def halt(s):
                g, it = ST[s]
                pe.wait_ge(i_taken.sem, i_taken["hidden", s, 5])
                nc.tensor.matmul(free(("halt", s)), W(L3F, "hw2", 32), i_hh[g], start=True, stop=True)\
                    .then_inc(i_staged.sem, 1)

            def spread(g):
                pe.wait_ge(i_sel.sem, i_sel[g])
                for k in range(3):
                    o = free(("turned", g, k))[0:24, 0:T // 2].bitcast(BF16)
                    for b in range(NB):
                        mm = nc.tensor.transpose(o[:, b * P:(b + 1) * P],
                                                 i_s3[g][k][:, b, :, :].rearrange("p s e -> p (s e)"), ident_bf[:, :])
                    mm.then_inc(i_staged.sem, 1)
                pe.wait_ge(i_taken.sem, i_taken["turned", g, 2])
                for n in range(10):
                    o = free(("spread", g, n))
                    if n < 2:
                        mm = nc.tensor.matmul(o, expand8[:, n * P:(n + 1) * P], i_sT[g][2], start=True, stop=True)
                    else:
                        k, p = divmod(n - 2, 4)
                        mm = nc.tensor.matmul(o, expand[0:8, p * P:(p + 1) * P], i_sT[g][k][0:8, :],
                                              start=True, stop=True)
                    mm.then_inc(i_staged.sem, 1)

            def gates(s, j):
                g, it = ST[s]
                q = 3 * s + j
                if q >= 2:
                    pe.wait_ge(i_read.sem, i_read[q - 2])
                    pe.wait_ge(i_act.sem, i_act[q - 2, 0 if q >= 8 else 2])
                if j == 0:
                    pe.wait_ge(i_taken.sem, i_taken["hidden", s, 4])
                for m in (1, 2, 0) if it else (1, 2):
                    o = bank(3 * (q % 2) + m)
                    if j == 0:
                        mm = nc.tensor.matmul(o, W(L3F, "sw2", 65)[:, m * P:(m + 1) * P], i_sh[g],
                                              start=True, stop=True)
                        mm.then_inc(i_ctl.sem, 1)
                        continue
                    for p in range(4):
                        if m == 1:
                            pe.wait_ge(i_msk.sem, i_msk[s, j - 1, p])
                        nc.tensor.matmul(o, W(L3F, "ew2")[:, p * 384 + m * P:p * 384 + (m + 1) * P],
                                         i_hm[g][4 * (j - 1) + p], start=(p == 0), stop=False)
                    nc.tensor.matmul(o, i_b2x[:, m * P:(m + 1) * P], i_sT[g][j - 1], start=False, stop=True)\
                        .then_inc(i_ctl.sem, 1)

            def refine(g):
                pe.wait_ge(i_new.sem, i_new[2 + g])
                for k in range(2):
                    nc.tensor.matmul(free(("refine", g, k)), W(L3F, "fw1")[:, k * P:(k + 1) * P], xT[g][:, :],
                                     start=True, stop=True).then_inc(i_staged.sem, 1)
                pe.wait_ge(i_taken.sem, i_taken["refine", g, 1])
                o = free(("refine", g, 2))
                for k in range(2):
                    mm = nc.tensor.matmul(o, W(L3F, "fw2")[:, k * P:(k + 1) * P], i_h[g][k], start=(k == 0),
                                          stop=(k == 1))
                mm.then_inc(i_staged.sem, 1)
                pe.wait_ge(i_taken.sem, i_taken["refine", g, 2])
                for b in range(NB):
                    mm = nc.tensor.transpose(ps[:, 6 + g, b * P:(b + 1) * P], i_res[g][:, b * P:(b + 1) * P], ident)
                mm.then_inc(sub_ready.sem, 1)

            for g in G:
                if g == 1:
                    pe.wait_ge(i_taken.sem, i_taken["router", 0])
                pe_turn_state(pe, L3X, g)
                pe.wait_ge(xT_ready.sem, xT_ready[L3X, g])
                nc.tensor.matmul(bank(6 + g)[0:32, :], W(L3F, "rw1"), xT[g][:, :], start=True, stop=True)\
                    .then_inc(i_staged.sem, 1)
            for g in G:
                pe.wait_ge(i_taken.sem, i_taken["router", g])
                for b in range(NB):
                    mm = nc.tensor.matmul(ps[:, 3 * g, 8 * b:8 * b + 8], i_rh[g][:, b * P:(b + 1) * P],
                                          W(L3F, "rw2", 32), start=True, stop=True)
                mm.then_inc(i_logit.sem, 1)
            hidden(0)
            hidden(1)
            halt(0)
            halt(1)
            spread(0)
            gates(0, 0)
            spread(1)
            gates(0, 1)
            gates(0, 2)
            gates(1, 0)
            gates(1, 1)
            hidden(2)
            gates(1, 2)
            halt(2)
            gates(2, 0)
            gates(2, 1)
            hidden(3)
            gates(2, 2)
            halt(3)
            gates(3, 0)
            gates(3, 1)
            refine(0)
            gates(3, 2)
            pe.wait_ge(sub_read.sem, sub_read[L3F, 0])
            refine(1)
            nc.tensor.drain().then_inc(layer_done.sem, 1)

        def act_l3f(act):
            def take(item, out, rows=P, f=ACT.Copy, **kw):
                act.wait_ge(i_staged.sem, i_staged[item])
                nc.scalar.activation(out, bank(staged_bank(item))[0:rows, :], f, **kw).then_inc(i_taken.sem, 1)

            def hidden(s):
                g, it = ST[s]
                for p in range(4):
                    take(("hidden", s, p), i_h[g][p], f=ACT.Gelu, bias=W(L3F, "eb1")[:, p:p + 1])
                take(("hidden", s, 4), i_sh[g][0:64, :], 64, f=ACT.Gelu, bias=W(L3F, "sb1", 64))
                take(("hidden", s, 5), i_hh[g], 32, f=ACT.Gelu, bias=W(L3F, "hb1", 32))

            def halt(s):
                take(("halt", s), i_th[ST[s][0]], f=ACT.Tanh, scale=0.5, bias=i_hb)

            def gates(s, j):
                g, it = ST[s]
                q = 3 * s + j
                o = 3 * (q % 2)
                act.wait_ge(i_ctl.sem, i_ctl[q, 1])
                if q >= 2:
                    act.wait_ge(i_term.sem, i_term[q - 2])
                nc.scalar.activation(i_sp[q % 2], bank(o + 1), ACT.Abs)
                nc.scalar.drain()
                nc.scalar.activation(i_sp[q % 2], i_sp[q % 2], ACT.Exp, scale=-1.0)
                nc.scalar.drain()
                nc.scalar.activation(i_sp[q % 2], i_sp[q % 2], ACT.Ln, bias=1.0).then_inc(i_act.sem, 1)
                act.wait_ge(i_ctl.sem, i_ctl[q, 2])
                nc.scalar.activation(i_tg[q % 2], bank(o + 2), ACT.Tanh, scale=0.5).then_inc(i_act.sem, 1)
                if it:
                    act.wait_ge(i_ctl.sem, i_ctl[q, 0])
                    nc.scalar.activation(i_ta[q % 2], bank(o), ACT.Tanh, scale=0.5).then_inc(i_act.sem, 1)

            def refine(g):
                for k in range(2):
                    take(("refine", g, k), i_h[g][k], f=ACT.Gelu, bias=W(L3F, "fb1")[:, k:k + 1])
                take(("refine", g, 2), i_res[g], f=ACT.Identity, scale=W(L3F, "iw"), bias=i_iwb)

            act.wait_ge(w_loaded[L3F].sem, 16)
            nc.scalar.activation(i_mix[:, 0:1], W(L3F, "sw"), ACT.Tanh, scale=0.5)
            for g in G:
                act_copy_state(act, L3X, g, xT[g][:, :])
                take(("router", g), i_rh[g], 32, f=ACT.Gelu, bias=W(L3F, "rb1", 32))
            for g in G:
                act.wait_ge(i_less.sem, i_less[g])
                nc.scalar.activation(i_lg[g], i_lg[g], ACT.Exp).then_inc(i_exp.sem, 1)
            hidden(0)
            hidden(1)
            halt(0)
            halt(1)
            for g in G:
                for k in range(3):
                    act.wait_ge(i_staged.sem, i_staged["turned", g, k])
                    nc.scalar.activation(i_sT[g][k], bank(staged_bank(("turned", g, k)))[0:24, 0:T // 2].bitcast(BF16),
                                         ACT.Copy).then_inc(i_taken.sem, 1)
                for n in range(10):
                    take(("spread", g, n), i_w[g][n] if n < 2 else i_mb[g][n - 2])
            for j in range(3):
                gates(0, j)
            gates(1, 0)
            hidden(2)
            gates(1, 1)
            halt(2)
            gates(1, 2)
            gates(2, 0)
            hidden(3)
            gates(2, 1)
            halt(3)
            gates(2, 2)
            gates(3, 0)
            refine(0)
            gates(3, 1)
            gates(3, 2)
            refine(1)

        def dve_l3f(dve):
            dve.wait_ge(w_loaded[L3F].sem, 16)
            nc.vector.tensor_scalar(i_hb, W(L3F, "hb2"), 0.5, None, ALU.mult)
            nc.vector.tensor_tensor(i_iwb, W(L3F, "iw"), W(L3F, "fb2"), ALU.mult)
            for g in G:
                nc.vector.memset(i_sh[g][64:65, :], 1.0)
            def split_biases():
                nc.vector.tensor_copy(i_b2f, W(L3F, "eb2", 24))
                nc.vector.drain()
                split3(i_b2f.rearrange("p (o d) -> p o d", o=1), i_b2.rearrange("p (o s) d -> p o s d", o=1))
                nc.vector.drain()
                nc.vector.tensor_scalar(i_b2f, i_b2[:, 0, :], C("res4")[0:24, 0:1], None, ALU.mult)
                nc.vector.drain()
                nc.vector.scalar_tensor_tensor(out=i_b2f, in0=i_b2[:, 1, :], scalar=C("res4")[0:24, 1:2], in1=i_b2f,
                                               op0=ALU.mult, op1=ALU.add)
                nc.vector.drain()
                nc.vector.scalar_tensor_tensor(out=i_b2x, in0=i_b2[:, 2, :], scalar=C("res4")[0:24, 2:3], in1=i_b2f,
                                               op0=ALU.mult, op1=ALU.add)
                nc.vector.drain()

            def less_max(g):
                dve.wait_ge(i_logit.sem, i_logit[g])
                rb2 = W(L3F, "rb2").rearrange("p (o e) -> p o e", o=1).to_broadcast([P, NB, 8])
                nc.vector.tensor_tensor(i_lg[g], ps[:, 3 * g, 0:32].rearrange("p (b e) -> p b e", b=NB), rb2, ALU.add)
                nc.vector.drain()
                nc.vector.tensor_reduce(i_m[g], i_lg[g], AX.X, ALU.max)
                nc.vector.drain()
                nc.vector.tensor_tensor(i_lg[g], i_lg[g], bcast(i_m[g], 8), ALU.subtract).then_inc(i_less.sem, 1)

            def select(g):
                dve.wait_ge(i_exp.sem, i_exp[g])
                nc.vector.tensor_reduce(i_m[g], i_lg[g], AX.X, ALU.add)
                if g == 0:
                    nc.vector.tensor_scalar(i_mix[:, 1:2], i_mix[:, 0:1], -0.5, 0.5, ALU.mult, ALU.add)
                nc.vector.drain()
                nc.vector.reciprocal(i_m[g], i_m[g])
                if g == 0:
                    nc.vector.tensor_scalar(i_mix[:, 0:1], i_mix[:, 0:1], 0.5, 0.5, ALU.mult, ALU.add)
                nc.vector.drain()
                nc.vector.tensor_tensor(i_lg[g], i_lg[g], bcast(i_m[g], 8), ALU.mult)
                nc.vector.drain()
                top_two(i_lg[g], i_top[g], i_idx[g], i_idf[g], i_one[g])
                for k in range(2):
                    o = i_one[g][:, k, :, :].rearrange("p b (s e) -> p b s e", s=1).to_broadcast([P, NB, 3, 8])
                    nc.vector.tensor_copy(i_s3[g][k], o)
                nc.vector.tensor_reduce(i_m[g], i_top[g][:, :, 0:2], AX.X, ALU.add)
                nc.vector.drain()
                nc.vector.reciprocal(i_m[g], i_m[g])
                nc.vector.drain()
                nc.vector.tensor_scalar(i_m[g], i_m[g], i_mix[:, 1:2], None, ALU.mult)
                nc.vector.drain()
                nc.vector.tensor_tensor(i_top[g], i_top[g], bcast(i_m[g], 8), ALU.mult)
                nc.vector.drain()
                split3(i_top[g], i_s3[g][2]).then_inc(i_sel.sem, 1)

            def to_mean(g):
                nc.vector.tensor_scalar(i_d[g], xT[g][:, :], W(L3F, "mu"), -2.0, ALU.subtract, ALU.mult)

            def terms(s, j):
                g, it = ST[s]
                q = 3 * s + j
                sp, Y, U = i_sp[q % 2], (i_V[g] if j == 0 else i_Y[j - 1]), (i_X[g] if j == 0 else i_U[j - 1])
                dve.wait_ge(i_act.sem, i_act[q, 1])
                nc.vector.scalar_tensor_tensor(out=sp, in0=bank(3 * (q % 2) + 1), scalar=0.0, in1=sp,
                                               op0=ALU.max, op1=ALU.add).then_inc(i_read.sem, 1)
                nc.vector.drain()
                nc.vector.tensor_tensor(sp, sp, i_d[g], ALU.mult)
                dve.wait_ge(i_act.sem, i_act[q, 0 if it else 2])
                if it:
                    nc.vector.scalar_tensor_tensor(out=i_ta[q % 2], in0=i_ta[q % 2], scalar=1.0, in1=i_v[g],
                                                   op0=ALU.add, op1=ALU.mult)
                nc.vector.drain()
                if it:
                    nc.vector.tensor_tensor(sp, sp, i_ta[q % 2], ALU.add)
                    nc.vector.drain()
                if j and s:
                    dve.wait_ge(i_sum.sem, i_sum[s - 1, j])
                if j == 0:
                    nc.vector.tensor_scalar(Y, sp, i_mix[:, 0:1], None, ALU.mult)
                else:
                    nc.vector.tensor_tensor(Y, sp, i_w[g][j - 1], ALU.mult)
                nc.vector.drain()
                nc.vector.scalar_tensor_tensor(out=U, in0=i_tg[q % 2], scalar=1.0, in1=Y, op0=ALU.add, op1=ALU.mult)\
                    .then_inc(i_term.sem, 1)

            def update(s):
                g, it = ST[s]
                dve.wait_ge(i_sum.sem, i_sum[s, 2])
                dve.wait_ge(i_taken.sem, i_taken["halt", s])
                nc.vector.scalar_tensor_tensor(out=i_X[g], in0=i_th[g], scalar=1.0, in1=i_X[g], op0=ALU.add,
                                               op1=ALU.mult)
                if it == 0:
                    nc.vector.scalar_tensor_tensor(out=i_v[g], in0=i_th[g], scalar=1.0, in1=i_V[g], op0=ALU.add,
                                                   op1=ALU.mult)
                nc.vector.drain()
                if it == 0:
                    nc.vector.tensor_scalar(i_v[g], i_v[g], 0.25, None, ALU.mult)
                nc.vector.scalar_tensor_tensor(out=xT[g][:, :], in0=i_X[g], scalar=0.1 / 8, in1=xT[g][:, :],
                                               op0=ALU.mult, op1=ALU.add).then_inc(i_new.sem, 1)
                nc.vector.drain()
                if it == 0:
                    to_mean(g)
                    nc.vector.drain()

            for g in G:
                less_max(g)
            select(0)
            to_mean(0)
            split_biases()
            select(1)
            to_mean(1)
            for s in range(4):
                for j in range(3):
                    terms(s, j)
                update(s)
                if s == 3:
                    dve_norm(dve, L3F, 0, twice=True)
            dve_norm(dve, L3F, 1, twice=True)

        def pool_l3f(pool):
            def mask(s):
                g, it = ST[s]
                for k in range(2):
                    for p in range(4):
                        if s < 2:
                            pool.wait_ge(i_taken.sem, i_taken["spread", g, 2 + 4 * k + p])
                        elif k == 0:
                            pool.wait_ge(i_taken.sem, i_taken["hidden", s, p])
                        nc.gpsimd.tensor_tensor(i_hm[g][4 * k + p], i_h[g][p], i_mb[g][4 * k + p], ALU.mult)\
                            .then_inc(i_msk.sem, 1)

            def add(s, j):
                g, it = ST[s]
                pool.wait_ge(i_term.sem, i_term[3 * s + j])
                if it == 0:
                    nc.gpsimd.tensor_tensor(i_V[g], i_V[g], i_Y[j - 1], ALU.add)
                nc.gpsimd.tensor_tensor(i_X[g], i_X[g], i_U[j - 1], ALU.add)
                nc.gpsimd.drain().then_inc(i_sum.sem, 1)

            mask(0)
            mask(1)
            add(0, 1)
            add(0, 2)
            mask(2)
            add(1, 1)
            add(1, 2)
            mask(3)
            add(2, 1)
            add(2, 2)
            add(3, 1)
            add(3, 2)
            for g in G:
                pool_rstd(pool, L3F, g)


        pe_layers = [pe_l0a]
        act_layers = [act_l0a]
        dve_layers = [dve_l0a]
        pool_layers = [pool_l0a]
        for fs in ((pe_l0x, act_l0x, dve_l0x, pool_l0x), (pe_l0f, act_l0f, dve_l0f, pool_l0f),
                   (pe_l1a, act_l1a, dve_l1a, pool_l1a),
                   (pe_context(L1X), act_context(L1X), dve_context(L1X), pool_context(L1X)),
                   (pe_l1f, act_l1f, dve_l1f, pool_l1f), (pe_l2a, act_l2a, dve_l2a, pool_l2a),
                   (pe_context(L2X), act_context(L2X), dve_context(L2X), pool_context(L2X)),
                   (pe_l2f, act_l2f, dve_l2f, pool_l2f), (pe_l3a, act_l3a, dve_l3a, pool_l3a),
                   (pe_context(L3X), act_context(L3X), dve_context(L3X), pool_context(L3X)),
                   (pe_l3f, act_l3f, dve_l3f, pool_l3f)):
            for engine, f in zip((pe_layers, act_layers, dve_layers, pool_layers), fs):
                engine.append(f)

        with nc.Block() as block:
            @block.sync
            def _(sp):
                sp.dma_start(const[:, :], dram["const"]).then_inc(const_loaded, 16)
                sp.dma_start(arena[0][0:96, 0:32 * 64], dram["expand"]).then_inc(const_loaded, 16)
                sp.dma_start(arena[1][0:24, 0:8 * P], dram["expand8"]).then_inc(const_loaded, 16)
                for L in (L0A, L0X):
                    sp.dma_start(w_first[L][:, :], dram[f"w{L}"]).then_inc(w_first_loaded, 16)
                for g in G:
                    sp.dma_start(x_in[g][:, :, :], dram["x"][NB * g:NB * g + NB, :, :].rearrange("b t d -> t b d"))\
                        .then_inc(first_x_loaded, 16)
                sp.wait_ge(w_first_loaded, 32)
                sp.wait_ge(first_x_loaded, 16 * NG)

            @block.vector
            def _(dve):
                nc.vector.memset(minus_half[:, :], -0.5)
                dve.wait_ge(const_loaded, 48)
                nc.vector.tensor_copy(expand[:, :], arena[0][0:96, 0:32 * 64])
                nc.vector.tensor_copy(expand8[:, :], arena[1][0:24, 0:8 * P])
                nc.vector.tensor_copy(ident_bf[:, :], ident)
                nc.vector.drain()
        nc.all_engine_barrier()

        with nc.Fori(0, steps) as step:
            with nc.Block() as block:
                @block.sync
                def _(sp):
                    sp.dma_start(ctxT[:, :], dram["ctxT"][:, bass.ds(NG * NB * KC * step, NG * NB * KC)])\
                        .then_inc(ctx_loaded.sem, 16)
                    sp.dma_start(mask_i[:, :, :],
                                 dram["mask_b"][bass.ds(NG * NB * step, NG * NB), :, :].rearrange("b t k -> t b k"))\
                        .then_inc(ctx_loaded.sem, 16)
                    for g in G:
                        sp.wait_ge(sub_read.sem, sub_read[L0A, g])
                        sp.dma_start(x_in[g][:, :, :],
                                     dram["x"][bass.ds(NG * NB * step + NG * NB + NB * g, NB), :, :]
                                     .rearrange("b t d -> t b d")).then_inc(x_loaded.sem, 16)
                    for L in range(2, 12):
                        if L >= 4:
                            sp.wait_ge(layer_done.sem, layer_done[L - 2])
                            if (L - 2, 1) in res_ready.value:
                                sp.wait_ge(res_ready.sem, res_ready[L - 2, 1])
                        t = w_even if L % 2 == 0 else w_odd
                        sp.dma_start(t[:, 0:cols[L]["_width"]], dram[f"w{L}"]).then_inc(w_loaded[L].sem, 16)
                    for g in G:
                        sp.wait_ge(x_ready.sem, x_ready[L3F, g])
                        sp.dma_start(out[bass.ds(NG * NB * step + NB * g, NB), :, :].rearrange("b t d -> t b d"),
                                     x_tok[g][:, :, :]).then_inc(stored.sem, 16)
                    sp.wait_ge(x_loaded.sem, 16 * NG)
                    sp.wait_ge(stored.sem, 16 * NG)

                @block.tensor
                def _(pe):
                    for layer in pe_layers:
                        layer(pe)

                @block.scalar
                def _(act):
                    for layer in act_layers:
                        layer(act)

                @block.vector
                def _(dve):
                    for layer in dve_layers:
                        layer(dve)

                @block.gpsimd
                def _(pool):
                    for layer in pool_layers:
                        layer(pool)
            nc.multi_engine_barrier([ENG.PE, ENG.DVE, ENG.Activation, ENG.Pool, ENG.SP],
                                    sems_to_clear=range(sems[0].num, sems[-1].num + 1))


def arrange(inp):
    f = {k: np.asarray(v) for k, v in inp.items()}
    packs = {}

    def T_(n):
        return f[n].T

    def col(a):
        return a.reshape(-1, 1)

    def rows(a, n=P):
        return np.broadcast_to(a.reshape(1, -1), (n, a.size))

    def heads(n):
        return f[n].transpose(1, 0, 2).reshape(P, -1)

    def spread(n):
        w = f[n].T.reshape(8, 16, P).transpose(1, 0, 2).reshape(16, 8 * P)
        return np.concatenate([w] * 8, axis=0)

    eye = np.eye(P, dtype=np.float32)
    p = np.arange(P)
    packs["const"] = [
        ("ident", eye),
        ("res4", (((p // 8) % 4)[:, None] == np.arange(4)[None, :]).astype(np.float32)),
        ("causal", (p[:, None] <= p[None, :]).astype(np.float32)),
        ("block16", (p[:, None] // 16 == p[None, :] // 16).astype(np.float32)),
        ("block8", (p[:, None] // 8 == p[None, :] // 8).astype(np.float32)),
        ("head16", (p[:, None] // 16 == np.arange(8)[None, :]).astype(np.float32)),
        ("head8", (p[:, None] // 8 == np.arange(16)[None, :]).astype(np.float32)),
        ("early", np.where(np.arange(16)[None, :] <= p[:, None], 0.0, -1e30).astype(np.float32)),
        ("iota8", np.broadcast_to(np.arange(8, dtype=np.float32)[None, :], (P, 8))),
    ]
    packs[0] = [("Wqkv", np.concatenate([T_("L0_attn_Wq"), T_("L0_attn_Wk"), T_("L0_attn_Wv")], 1)),
                ("Wo", T_("L0_attn_Wo"))]
    packs[1] = [
        ("qkv0", np.concatenate([heads("L0_xattn_Wq1"), heads("L0_xattn_Wk1"), heads("L0_xattn_Wv1")], 1)),
        ("qkv1", np.concatenate([heads("L0_xattn_Wq2"), heads("L0_xattn_Wk2"), heads("L0_xattn_Wv2")], 1)),
        ("Wo0", spread("L0_xattn_Wo1")), ("Wo1", spread("L0_xattn_Wo2")),
        ("E1", f["L0_xattn_E1"]), ("D1", T_("L0_xattn_D1")), ("E2", f["L0_xattn_E2"]), ("D2", T_("L0_xattn_D2")),
        *[(f"{v}{k}", rows(f[f"L0_xattn_{v}{k}"])) for k in (1, 2, 3) for v in "gb"],
        *[(f"{v}{k}c", col(f[f"L0_xattn_{v}{k}"])) for k in (1, 2) for v in "gb"],
    ]
    def experts(n):
        return f[n].transpose(1, 0, 2).reshape(P, -1)
    packs[2] = [
        ("Wr", f["L0_ffn_Wr"]), ("br", rows(f["L0_ffn_br"])),
        ("Wg", experts("L0_ffn_Wg")), ("Wu", experts("L0_ffn_Wu")),
        ("Wd", f["L0_ffn_Wd"].reshape(16, P, P).transpose(1, 0, 2).reshape(P, -1)),
        ("Wgs", f["L0_ffn_Wg_s"]), ("Wus", f["L0_ffn_Wu_s"]), ("Wds", f["L0_ffn_Wd_s"]),
        ("bg", f["L0_ffn_bg"].reshape(16, P).T), ("bu", f["L0_ffn_bu"].reshape(16, P).T),
        ("bgs", col(f["L0_ffn_bg_s"])), ("bus", col(f["L0_ffn_bu_s"])), ("bds", col(f["L0_ffn_bd_s"])),
        ("bd", np.concatenate([f["L0_ffn_bd"]] * 3, 0)),
    ]
    packs[3] = [("Wq", experts("L1_attn_w_q")), ("Wk", experts("L1_attn_w_k")), ("Wv", experts("L1_attn_w_v")),
                ("Wo", f["L1_attn_w_o"].reshape(8, P, P).transpose(1, 0, 2).reshape(P, -1))]
    packs[4] = [(w, T_(f"L1_xattn_{w}")) for w in ("Wq", "Wk", "Wv", "Wo")] + \
               [(b, col(f[f"L1_xattn_{b}"])) for b in ("bq", "bk", "bv")] + [("bo", rows(f["L1_xattn_bo"]))]
    def chunks(n):
        w = f[n].T
        return w.reshape(-1, P, w.shape[1]).transpose(1, 0, 2).reshape(P, -1)
    def scale(n):
        return f[n].reshape(-1, P).T
    packs[5] = [("w1", chunks("L1_ffn_w1_w")), ("w2", chunks("L1_ffn_w2_w")), ("h1", chunks("L1_ffn_h1_w")),
                ("h2", chunks("L1_ffn_h2_w")), ("w3", chunks("L1_ffn_w3_w")),
                *[(f"{n}s", scale(f"L1_ffn_{n}_s")) for n in ("w1", "w2", "h1", "h2", "w3")]]
    packs[6] = [("Wq", f["L2_attn_Wq"]), ("Wkv", np.concatenate([f["L2_attn_Wk"], f["L2_attn_Wv"]], 1)),
                ("Wo", f["L2_attn_Wp"]), ("bq", col(f["L2_attn_bq"])),
                ("bkv", np.concatenate([rows(f["L2_attn_bk"]), rows(f["L2_attn_bv"])], 1)),
                ("bo", rows(f["L2_attn_bp"]))]
    packs[7] = [(w, f[f"L2_xattn_{w}"]) for w in ("Wq", "Wk", "Wv", "Wo")] + \
               [(b, col(f[f"L2_xattn_{b}"])) for b in ("bq", "bk", "bv")] + \
               [("bo", rows(f["L2_xattn_bo"])), ("mask", f["mask_SxS2_fk1"])]
    def down(n):
        w = f[n]
        return w.reshape(-1, P, P).transpose(1, 0, 2).reshape(P, -1)
    packs[8] = [("gate", T_("L2_ffn_gate_W")), ("w1", experts("L2_ffn_w1_e")), ("w3", experts("L2_ffn_w3_e")),
                ("w2", down("L2_ffn_w2_e")), ("w1s", experts("L2_ffn_w1_s")), ("w3s", experts("L2_ffn_w3_s")),
                ("w2s", down("L2_ffn_w2_s"))]
    packs[9] = [(w, T_(f"L3_attn_{w}")) for w in ("Wq", "Wk", "Wv", "Wo")] + \
               [(b, col(f[f"L3_attn_{b}"])) for b in ("bq", "bk", "bv")] + \
               [("bo", rows(f["L3_attn_bo"])), ("rel", np.concatenate([f["L3_attn_rel_emb"].T] * 16, 0))]
    packs[10] = [(w, T_(f"L3_xattn_{w}")) for w in ("Wq", "Wk", "Wv", "Wo")]
    def halves(a):
        return a.reshape(2, P, -1).transpose(1, 0, 2).reshape(P, -1)
    ew1 = f["L3_ffn_expert_w1"].transpose(1, 0, 2).reshape(2 * P, 512)
    packs[11] = [
        ("iw", col(f["L3_ffn_integration_weight"])), ("mu", col(f["L3_ffn_mu"])),
        ("rw1", f["L3_ffn_router_w1"]), ("rb1", col(f["L3_ffn_router_b1"])),
        ("rw2", f["L3_ffn_router_w2"]), ("rb2", rows(f["L3_ffn_router_b2"])),
        ("hw1", f["L3_ffn_halt_w1"]), ("hb1", col(f["L3_ffn_halt_b1"])),
        ("hw2", np.broadcast_to(f["L3_ffn_halt_w2"], (32, P))), ("hb2", rows(f["L3_ffn_halt_b2"])),
        ("ew1", halves(ew1)), ("eb1", f["L3_ffn_expert_b1"].reshape(4, P).T),
        ("ew2", f["L3_ffn_expert_w2"].reshape(4, P, 384).transpose(1, 0, 2).reshape(P, -1)),
        ("eb2", np.concatenate([f["L3_ffn_expert_b2"]] * 3, 0)),
        ("sw1", halves(f["L3_ffn_shared_w1"])), ("sb1", col(f["L3_ffn_shared_b1"])),
        ("sw2", np.concatenate([f["L3_ffn_shared_w2"], f["L3_ffn_shared_b2"].reshape(1, -1)], 0)),
        ("sw", np.broadcast_to(f["L3_ffn_shared_weight"].reshape(1, 1), (P, 1))),
        ("fw1", f["L3_ffn_refine_w1"]), ("fb1", f["L3_ffn_refine_b1"].reshape(2, P).T),
        ("fw2", halves(f["L3_ffn_refine_w2"])), ("fb2", col(f["L3_ffn_refine_b2"])),
    ]
    arrays, cols = {}, {}
    for key, items in packs.items():
        at, where, parts = 0, {}, []
        for name, a in items:
            r, c = a.shape
            where[name] = (at, r, c)
            parts.append(a if r == P else np.concatenate([a, np.zeros((P - r, c), np.float32)], 0))
            at += c
        where["_width"] = at
        cols[key] = where
        arrays["const" if key == "const" else f"w{key}"] = np.ascontiguousarray(np.concatenate(parts, 1))
    arrays["x"] = np.concatenate([f["x"], np.zeros((NG * NB, P, P), np.float32)], 0)
    arrays["ctxT"] = np.ascontiguousarray(f["ctx_1024"].transpose(2, 0, 1).reshape(P, -1))
    arrays["mask_b"] = f["mask_BxSxS2_ik0"]
    e = np.arange(96) % 32
    arrays["expand"] = (e[:, None] == (np.arange(2048) // 64)[None, :]).astype(np.float32)
    arrays["expand8"] = ((np.arange(24) % 8)[:, None] == (np.arange(1024) // P)[None, :]).astype(np.float32)
    return arrays, cols


def kernel(**inputs):
    import concourse.bacc as bacc
    from concourse.bass_utils import run_bass_kernel_spmd

    arrays, cols = arrange(inputs)
    n = inputs["x"].shape[0]
    nc = bacc.Bacc("TRN2", target_bir_lowering=False, num_devices=1)
    dram = {k: nc.dram_tensor("in_" + k, a.shape, mybir.dt.from_np(a.dtype), kind="ExternalInput").ap()
            for k, a in arrays.items()}
    out = nc.dram_tensor("result", (n, P, P), F32, kind="ExternalOutput").ap()
    build(nc, dram, cols, out, n // (NG * NB))
    r = run_bass_kernel_spmd(nc, [{"in_" + k: a for k, a in arrays.items()}], core_ids=[0])
    return r.results[0]["result"]
```
